# Optimizing a Trainium2 kernel written in Bass

```python
import numpy as np
import jax
import jax.numpy as jnp

def _softmax(x, axis=-1):
    return jax.nn.softmax(x, axis=axis)

def _gelu(x):
    return jax.nn.gelu(x, approximate=True)

def _silu(x):
    return jax.nn.silu(x)

def _sigmoid(x):
    return jax.nn.sigmoid(x)

def _layernorm(x, axis=-1, eps=1e-05):
    m = jnp.mean(x, axis=axis, keepdims=True)
    v = jnp.var(x, axis=axis, keepdims=True)
    return (x - m) / jnp.sqrt(v + eps)

def _scatter_add(tgt, idx, src, axis=0):
    return tgt.at[idx].add(src)

def _segment_sum(src, seg, n):
    return jax.ops.segment_sum(src, seg, n)
kernel_name = 'mk_xattn_ffn_d2_seqx_r4_690077'

def setup_inputs(seed: int=0):
    np.random.seed(seed)
    _w = jnp.asarray

    def _rec_inputs():
        import jax
        import jax.numpy as jnp
        _rk = jax.random.key(seed)
        x = 7.22e-05 + 1 * jax.random.normal(jax.random.fold_in(_rk, 1), (4, 512, 256), jnp.float32)
        _lenS = 512 - jax.random.randint(jax.random.fold_in(_rk, 7), (4,), 0, max(1, 512 // 4) + 1, jnp.int32)
        _lenS2 = 512 - jax.random.randint(jax.random.fold_in(_rk, 8), (4,), 0, max(1, 512 // 4) + 1, jnp.int32)
        _ctx_1024P = jax.random.normal(jax.random.fold_in(_rk, 11), (4, 16, 256), jnp.float32)
        _ctx_1024c = jax.random.dirichlet(jax.random.fold_in(_rk, 511), 0.3 * jnp.ones((16,), jnp.float32), (4, 512))
        _ctx_1024t = jnp.einsum('bsk,bkd->bsd', _ctx_1024c, _ctx_1024P)
        _ctx_1024t = _ctx_1024t * jax.lax.rsqrt(jnp.mean(jnp.square(_ctx_1024t)) + 1e-12) * 0.953939
        ctx_1024 = 4.13588e-05 + 0.999923 * (_ctx_1024t + 0.3 * jax.random.normal(jax.random.fold_in(_rk, 611), (4, 512, 256), jnp.float32))
        return (x, ctx_1024)
    x, ctx_1024 = _rec_inputs()

    def _L0_xattn_setup():
        import jax, jax.numpy as jnp
        import numpy as np
        NUM_HEADS = 8
        D_MODEL = 256
        DIM = D_MODEL // NUM_HEADS
        HEAD_DIM = DIM // NUM_HEADS
        B, S = (4, 512)

        def _split_heads(x):
            b, s, _ = x.shape
            return x.reshape(b, s, NUM_HEADS, HEAD_DIM).transpose(0, 2, 1, 3)
        key = jax.random.key(seed)
        ks = jax.random.split(key, 11)
        sd_in = 1.0 / np.sqrt(D_MODEL)
        sd_o = 1.0 / np.sqrt(DIM)
        return {'queries': jax.random.normal(ks[0], (B, S, D_MODEL), jnp.float32), 'keys': jax.random.normal(ks[1], (B, S, D_MODEL), jnp.float32), 'values': jax.random.normal(ks[2], (B, S, D_MODEL), jnp.float32), 'Wq': jax.random.normal(ks[3], (D_MODEL, DIM), jnp.float32) * sd_in, 'bq': jnp.zeros((DIM,), jnp.float32), 'Wk': jax.random.normal(ks[4], (D_MODEL, DIM), jnp.float32) * sd_in, 'bk': jnp.zeros((DIM,), jnp.float32), 'Wv': jax.random.normal(ks[5], (D_MODEL, DIM), jnp.float32) * sd_in, 'bv': jnp.zeros((DIM,), jnp.float32), 'Wo': jax.random.normal(ks[6], (DIM, D_MODEL), jnp.float32) * sd_o, 'bo': jnp.zeros((D_MODEL,), jnp.float32)}
    _L0_xattn_all = _L0_xattn_setup()
    _L0_xattn_in = {k: v for k, v in _L0_xattn_all.items() if k in ('Wq', 'bq', 'Wk', 'bk', 'Wv', 'bv', 'Wo', 'bo')}
    del _L0_xattn_all

    def _L0_ffn_setup():
        import math
        import jax, jax.numpy as jnp
        import numpy as np
        D_MODEL = 256
        D_FF = 1024
        E = 8
        K = 2
        CF = 1.25
        CLAMP = 10000.0
        key = jax.random.key(seed)
        k0, k1, k2, k3 = jax.random.split(key, 4)
        B, S = (4, 512)
        x = jax.random.normal(k0, (B, S, D_MODEL), dtype=jnp.float32)
        ln_gamma = jnp.ones((D_MODEL,), jnp.float32)
        ln_beta = jnp.zeros((D_MODEL,), jnp.float32)
        rb = 0.02 * math.sqrt(3.0)
        Wr = jax.random.uniform(k1, (E, D_MODEL), jnp.float32, -rb, rb)
        b12 = math.sqrt(6.0 / (D_MODEL + 2 * D_FF))
        W12 = jax.random.uniform(k2, (E, 2 * D_FF, D_MODEL), jnp.float32, -b12, b12)
        b3 = math.sqrt(6.0 / (D_FF + D_MODEL))
        W3 = jax.random.uniform(k3, (E, D_MODEL, D_FF), jnp.float32, -b3, b3)
        return {'x': x, 'ln_gamma': ln_gamma, 'ln_beta': ln_beta, 'Wr': Wr, 'W12': W12, 'W3': W3}
    _L0_ffn_all = _L0_ffn_setup()
    _L0_ffn_in = {k: v for k, v in _L0_ffn_all.items() if k in ('ln_gamma', 'ln_beta', 'Wr', 'W12', 'W3')}
    del _L0_ffn_all

    def _L1_xattn_setup():
        import jax, jax.numpy as jnp
        import numpy as np
        MODEL_DIM = 256
        NUM_HEADS = 16
        HEAD_DIM = MODEL_DIM // NUM_HEADS
        SCALE = HEAD_DIM ** (-0.5)
        key = jax.random.key(seed)
        ks = jax.random.split(key, 8)
        B, LQ, LC = (2, 512, 512)
        std = MODEL_DIM ** (-0.5)
        return {'query': jax.random.normal(ks[0], (B, LQ, MODEL_DIM), jnp.float32), 'context': jax.random.normal(ks[1], (B, LC, MODEL_DIM), jnp.float32), 'Wq': jax.random.normal(ks[2], (MODEL_DIM, MODEL_DIM), jnp.float32) * std, 'bq': jnp.zeros((MODEL_DIM,), jnp.float32), 'Wkv': jax.random.normal(ks[3], (MODEL_DIM, 2 * MODEL_DIM), jnp.float32) * std, 'bkv': jnp.zeros((2 * MODEL_DIM,), jnp.float32), 'Wout': jax.random.normal(ks[4], (MODEL_DIM, MODEL_DIM), jnp.float32) * std, 'bout': jnp.zeros((MODEL_DIM,), jnp.float32)}
    _L1_xattn_all = _L1_xattn_setup()
    _L1_xattn_in = {k: v for k, v in _L1_xattn_all.items() if k in ('Wq', 'bq', 'Wkv', 'bkv', 'Wout', 'bout')}
    del _L1_xattn_all

    def _L1_ffn_setup():
        import jax, jax.numpy as jnp
        import numpy as np
        S, B, D = (256, 2, 256)
        E, TOPK = (15, 3)
        F = 256
        FS = 512

        def _uinit(k, shape, out_dim):
            std = out_dim ** (-0.5)
            return jax.random.uniform(k, shape, jnp.float32, -std, std)
        key = jax.random.key(seed)
        ks = jax.random.split(key, 10)
        return {'x': jax.random.normal(ks[0], (S, B, D), jnp.float32), 'gate_w': jax.random.normal(ks[1], (E, D), jnp.float32) * D ** (-0.5), 'fc1_w': _uinit(ks[2], (E, 2 * F, D), 2 * F), 'fc1_b': _uinit(ks[3], (E, 2 * F), 2 * F), 'geglu_mult': jnp.ones((E, F), jnp.float32), 'fc2_w': _uinit(ks[4], (E, D, F), D), 'fc2_b': _uinit(ks[5], (E, D), D), 's_fc1_w': _uinit(ks[6], (2 * FS, D), 2 * FS), 's_fc1_b': _uinit(ks[7], (2 * FS,), 2 * FS), 's_geglu_mult': jnp.ones((FS,), jnp.float32), 's_fc2_w': _uinit(ks[8], (D, FS), D), 's_fc2_b': _uinit(ks[9], (D,), D)}
    _L1_ffn_all = _L1_ffn_setup()
    _L1_ffn_in = {k: v for k, v in _L1_ffn_all.items() if k in ('gate_w', 'fc1_w', 'fc1_b', 'geglu_mult', 'fc2_w', 'fc2_b', 's_fc1_w', 's_fc1_b', 's_geglu_mult', 's_fc2_w', 's_fc2_b')}
    del _L1_ffn_all
    return {'x': x, 'ctx_1024': ctx_1024, 'L0_xattn_Wq': _L0_xattn_in['Wq'], 'L0_xattn_bq': _L0_xattn_in['bq'], 'L0_xattn_Wk': _L0_xattn_in['Wk'], 'L0_xattn_bk': _L0_xattn_in['bk'], 'L0_xattn_Wv': _L0_xattn_in['Wv'], 'L0_xattn_bv': _L0_xattn_in['bv'], 'L0_xattn_Wo': _L0_xattn_in['Wo'], 'L0_xattn_bo': _L0_xattn_in['bo'], 'L0_ffn_ln_gamma': _L0_ffn_in['ln_gamma'], 'L0_ffn_ln_beta': _L0_ffn_in['ln_beta'], 'L0_ffn_Wr': _L0_ffn_in['Wr'], 'L0_ffn_W12': _L0_ffn_in['W12'], 'L0_ffn_W3': _L0_ffn_in['W3'], 'L1_xattn_Wq': _L1_xattn_in['Wq'], 'L1_xattn_bq': _L1_xattn_in['bq'], 'L1_xattn_Wkv': _L1_xattn_in['Wkv'], 'L1_xattn_bkv': _L1_xattn_in['bkv'], 'L1_xattn_Wout': _L1_xattn_in['Wout'], 'L1_xattn_bout': _L1_xattn_in['bout'], 'L1_ffn_gate_w': _L1_ffn_in['gate_w'], 'L1_ffn_fc1_w': _L1_ffn_in['fc1_w'], 'L1_ffn_fc1_b': _L1_ffn_in['fc1_b'], 'L1_ffn_geglu_mult': _L1_ffn_in['geglu_mult'], 'L1_ffn_fc2_w': _L1_ffn_in['fc2_w'], 'L1_ffn_fc2_b': _L1_ffn_in['fc2_b'], 'L1_ffn_s_fc1_w': _L1_ffn_in['s_fc1_w'], 'L1_ffn_s_fc1_b': _L1_ffn_in['s_fc1_b'], 'L1_ffn_s_geglu_mult': _L1_ffn_in['s_geglu_mult'], 'L1_ffn_s_fc2_w': _L1_ffn_in['s_fc2_w'], 'L1_ffn_s_fc2_b': _L1_ffn_in['s_fc2_b']}

def reference(x, ctx_1024, L0_xattn_Wq, L0_xattn_bq, L0_xattn_Wk, L0_xattn_bk, L0_xattn_Wv, L0_xattn_bv, L0_xattn_Wo, L0_xattn_bo, L0_ffn_ln_gamma, L0_ffn_ln_beta, L0_ffn_Wr, L0_ffn_W12, L0_ffn_W3, L1_xattn_Wq, L1_xattn_bq, L1_xattn_Wkv, L1_xattn_bkv, L1_xattn_Wout, L1_xattn_bout, L1_ffn_gate_w, L1_ffn_fc1_w, L1_ffn_fc1_b, L1_ffn_geglu_mult, L1_ffn_fc2_w, L1_ffn_fc2_b, L1_ffn_s_fc1_w, L1_ffn_s_fc1_b, L1_ffn_s_geglu_mult, L1_ffn_s_fc2_w, L1_ffn_s_fc2_b):
    import jax
    import jax.numpy as jnp

    def _L0_xattn_ref(queries, keys, values, Wq, bq, Wk, bk, Wv, bv, Wo, bo):
        import jax, jax.numpy as jnp
        import numpy as np
        NUM_HEADS = 8
        D_MODEL = 256
        DIM = D_MODEL // NUM_HEADS
        HEAD_DIM = DIM // NUM_HEADS
        B, S = (4, 512)

        def _split_heads(x):
            b, s, _ = x.shape
            return x.reshape(b, s, NUM_HEADS, HEAD_DIM).transpose(0, 2, 1, 3)
        q = _split_heads(queries @ Wq + bq)
        k = _split_heads(keys @ Wk + bk)
        v = _split_heads(values @ Wv + bv)
        scale = 1.0 / np.sqrt(D_MODEL / NUM_HEADS).astype(np.float32)
        scores = jnp.einsum('bhqd,bhkd->bhqk', q, k) * scale
        attn = jax.nn.softmax(scores, axis=-1)
        o = jnp.einsum('bhqk,bhkd->bhqd', attn, v)
        b, h, s, hd = o.shape
        o = o.transpose(0, 2, 1, 3).reshape(b, s, h * hd)
        return o @ Wo + bo

    def _L0_ffn_ref(x, ln_gamma, ln_beta, Wr, W12, W3):
        import math
        import jax, jax.numpy as jnp
        import numpy as np
        D_MODEL = 256
        D_FF = 1024
        E = 8
        K = 2
        CF = 1.25
        CLAMP = 10000.0
        B, S, D = x.shape
        T = B * S
        xf = x.reshape(T, D)
        mu = xf.mean(-1, keepdims=True)
        var = ((xf - mu) ** 2).mean(-1, keepdims=True)
        xn = (xf - mu) / jnp.sqrt(var + 1e-05) * ln_gamma + ln_beta
        logits = jnp.clip(xn @ Wr.T, -CLAMP, CLAMP)
        m = logits.max(-1, keepdims=True)
        ex = jnp.exp(logits - m)
        probs = ex / (ex.sum(-1, keepdims=True) + 1e-12)
        top_p, top_i = jax.lax.top_k(probs, K)
        Sslots = T * K
        experts = top_i.reshape(-1)
        weights = top_p.reshape(-1)
        tokens = jnp.repeat(jnp.arange(T, dtype=jnp.int32), K)
        order = jnp.argsort(experts, stable=True)
        e_s = experts[order]
        w_s = weights[order]
        t_s = tokens[order]
        counts = jnp.bincount(e_s, length=E)
        offsets = jnp.concatenate([jnp.zeros((1,), counts.dtype), jnp.cumsum(counts)])
        rank = jnp.arange(Sslots, dtype=counts.dtype) - offsets[e_s]
        cap = max(1, math.ceil(math.ceil(T * K * CF) / E))
        kept = rank < cap
        pos = jnp.where(kept, rank, cap)
        buf = jnp.zeros((E, cap, D), x.dtype).at[e_s, pos].set(xn[t_s], mode='drop')
        gu = jnp.einsum('ecd,efd->ecf', buf, W12)
        g, u = (gu[..., :D_FF], gu[..., D_FF:])
        h = jax.nn.silu(g) * u
        y = jnp.einsum('ecf,edf->ecd', h, W3)
        y_slot = y[e_s, jnp.minimum(pos, cap - 1)] * (w_s * kept.astype(x.dtype))[:, None]
        out = jnp.zeros((T, D), x.dtype).at[t_s].add(y_slot)
        return out.reshape(B, S, D)

    def _L1_xattn_ref(query, context, Wq, bq, Wkv, bkv, Wout, bout):
        import jax, jax.numpy as jnp
        import numpy as np
        MODEL_DIM = 256
        NUM_HEADS = 16
        HEAD_DIM = MODEL_DIM // NUM_HEADS
        SCALE = HEAD_DIM ** (-0.5)
        B, LQ, _ = query.shape
        LC = context.shape[1]
        H, D = (NUM_HEADS, HEAD_DIM)
        q = query @ Wq + bq
        kv = context @ Wkv + bkv
        kv = kv.reshape(B, LC, H, D, 2)
        k = jnp.transpose(kv[..., 0], (0, 2, 1, 3))
        v = jnp.transpose(kv[..., 1], (0, 2, 1, 3))
        q = jnp.transpose(q.reshape(B, LQ, H, D), (0, 2, 1, 3))
        scores = jnp.einsum('bhid,bhjd->bhij', q, k) * SCALE
        attn = jax.nn.softmax(scores, axis=-1)
        out = jnp.einsum('bhij,bhjd->bhid', attn, v)
        out = jnp.transpose(out, (0, 2, 1, 3)).reshape(B, LQ, H * D)
        return out @ Wout + bout

    def _L1_ffn_ref(x, gate_w, fc1_w, fc1_b, geglu_mult, fc2_w, fc2_b, s_fc1_w, s_fc1_b, s_geglu_mult, s_fc2_w, s_fc2_b):
        import jax, jax.numpy as jnp
        import numpy as np
        S, B, D = (256, 2, 256)
        E, TOPK = (15, 3)
        F = 256
        FS = 512

        def _uinit(k, shape, out_dim):
            std = out_dim ** (-0.5)
            return jax.random.uniform(k, shape, jnp.float32, -std, std)
        s, b, d = x.shape
        xt = x.reshape(-1, d)
        T = xt.shape[0]
        logits = xt @ gate_w.T
        scores = jax.nn.softmax(logits, axis=-1)
        topk_w, topk_idx = jax.lax.top_k(scores, TOPK)
        topk_w = topk_w / (jnp.sum(topk_w, axis=-1, keepdims=True) + 1e-20)
        comb = jnp.zeros((T, E), xt.dtype).at[jnp.arange(T)[:, None], topk_idx].add(topk_w)
        h = jnp.einsum('td,efd->etf', xt, fc1_w) + fc1_b[:, None, :]
        xh, g = (h[..., :F], h[..., F:])
        a = jax.nn.gelu(g, approximate=False) * xh * geglu_mult[:, None, :]
        yexp = jnp.einsum('etf,edf->etd', a, fc2_w) + fc2_b[:, None, :]
        y = jnp.einsum('etd,te->td', yexp, comb)
        hs = xt @ s_fc1_w.T + s_fc1_b
        xs, gs = (hs[..., :FS], hs[..., FS:])
        as_ = jax.nn.gelu(gs, approximate=False) * xs * s_geglu_mult
        ys = as_ @ s_fc2_w.T + s_fc2_b
        return (y + ys).reshape(s, b, d)
    x = x + _L0_xattn_ref(_layernorm(x, axis=-1), ctx_1024, ctx_1024, L0_xattn_Wq, L0_xattn_bq, L0_xattn_Wk, L0_xattn_bk, L0_xattn_Wv, L0_xattn_bv, L0_xattn_Wo, L0_xattn_bo)
    x = x + _L0_ffn_ref(_layernorm(x, axis=-1), L0_ffn_ln_gamma, L0_ffn_ln_beta, L0_ffn_Wr, L0_ffn_W12, L0_ffn_W3)
    x = x + _L1_xattn_ref(_layernorm(x, axis=-1), ctx_1024, L1_xattn_Wq, L1_xattn_bq, L1_xattn_Wkv, L1_xattn_bkv, L1_xattn_Wout, L1_xattn_bout)
    x = x + _L1_ffn_ref(_layernorm(x, axis=-1), L1_ffn_gate_w, L1_ffn_fc1_w, L1_ffn_fc1_b, L1_ffn_geglu_mult, L1_ffn_fc2_w, L1_ffn_fc2_b, L1_ffn_s_fc1_w, L1_ffn_s_fc1_b, L1_ffn_s_geglu_mult, L1_ffn_s_fc2_w, L1_ffn_s_fc2_b)
    return x

_drawn_inputs = setup_inputs


def setup_inputs(seed=0):
    import zlib

    import numpy as np

    out = dict(_drawn_inputs(seed))
    spreads = {'L0_xattn_bq': (0.0, 0.8),
     'L0_xattn_bk': (0.0, 0.8),
     'L0_xattn_bv': (0.0, 0.1),
     'L0_xattn_bo': (0.0, 0.1),
     'L0_ffn_ln_gamma': (1.0, 0.6),
     'L0_ffn_ln_beta': (0.0, 0.8),
     'L1_xattn_bq': (0.0, 0.458),
     'L1_xattn_bkv': (0.0, 0.1),
     'L1_xattn_bout': (0.0, 0.1),
     'L1_ffn_geglu_mult': (1.0, 0.6),
     'L1_ffn_s_geglu_mult': (1.0, 0.6)}
    factors = {'L1_ffn_fc1_b': 8.0, 'L1_ffn_fc2_b': 3.205, 'L1_ffn_s_fc1_b': 8.0}
    for name, (base, spread) in spreads.items():
        noise = np.random.default_rng([zlib.crc32(name.encode()), seed]).standard_normal(out[name].shape)
        drawn = base * np.exp(spread * noise) if base else spread * noise
        out[name] = jnp.asarray(drawn.astype(out[name].dtype))
    for name, factor in factors.items():
        out[name] = (out[name] * factor).astype(out[name].dtype)
    return out
```

```python
from contextlib import ExitStack

import concourse.bass as bass
from concourse import mybir

F32 = mybir.dt.float32
BF16 = mybir.dt.bfloat16
I32 = mybir.dt.int32
U32 = mybir.dt.uint32
ALU = mybir.AluOpType
ACT = mybir.ActivationFunctionType
AX = mybir.AxisListType

P = 128
BATCH, SEQ, D = 4, 512, 256
TOK = BATCH * SEQ
NT = TOK // P
TPB = SEQ // P
KD = D // P
EPS = 1e-5
HP = 16
GH = 4
VW = 32
Q_TERMS = (0, 0, 0, 1, 1, 2)
K_TERMS = (0, 1, 2, 0, 1, 0)
ROWS = HP * len(Q_TERMS)
SHIFT = 2
SLOTS = 4

E0, K0, FF0, CAP0 = 8, 2, 1024, 640
E1, K1, FF1, FFS = 15, 3, 256, 512
TILES1 = (TOK * K1 + E1 * (P - 1)) // P
FAR = 1 << 20


def wait(eng, sem, value):
    if not isinstance(value, int) or value > 0:
        eng.wait_ge(sem, value)


class Link:

    def __init__(self, eng, sem):
        self.eng, self.sem, self.count = eng, sem, 0

    def __call__(self, ins):
        self.count += 1
        ins.then_inc(self.sem, 1)
        self.eng.wait_ge(self.sem, self.count)


def scope(nc, ctx):
    def sb(name, shape, dt=F32):
        return ctx.enter_context(nc.sbuf_tensor(name, shape, dt))

    def ps(name, shape):
        return ctx.enter_context(nc.psum_tensor(name, shape, F32))

    def sem(name):
        return ctx.enter_context(nc.semaphore(name))

    return sb, ps, sem


def deviation(act, env, mv, rstd, var_ready, dev_done, n):
    act.wait_ge(var_ready, n + 1)
    act.activation(rstd[:, :], mv[:, :, 1], ACT.Sqrt, bias=env.eps[:, :]).then_inc(dev_done, 1)


def layernorm(dve, link, src, dst, stats, mv, rstd, var_ready, dev_done, n, done=None):
    for t in range(NT):
        ins = dve.bn_stats(stats[:, t, :], src[:, t, :])
    link(ins)
    for t in range(NT):
        ins = dve.bn_aggr(mv[:, t, :], stats[:, t, :])
    ins.then_inc(var_ready, 1)
    dve.wait_ge(dev_done, n + 1)
    link(dve.reciprocal(rstd[:, :], rstd[:, :]))
    for t in range(NT):
        ins = dve.tensor_scalar(dst[:, t, :], src[:, t, :], mv[:, t, 0:1], rstd[:, t:t + 1],
                                ALU.subtract, ALU.mult)
        if done is not None:
            ins.then_inc(done, 1)
    if done is None:
        link(ins)


def setup(nc, env, ins):
    with ExitStack() as ctx:
        sb, ps, sem = scope(nc, ctx)
        zeros = sb("zeros", [P, 2048])
        loaded, zeroed, filled = sem("su_loaded"), sem("su_zeroed"), sem("su_filled")
        const0 = sem("su_const0")
        block = ctx.enter_context(nc.Block())

        @block.sync
        def _(sp):
            sp.dma_start(env.X[:, :, :], ins["x"].rearrange("(t p) d -> p t d", p=P)).then_inc(loaded, 16)
            sp.wait_ge(zeroed, 1)
            n = 0
            for dram, rows in ((env.xs0, E0 * CAP0), (env.xs1, TILES1 * P)):
                for r in range(0, rows, 1024):
                    k = min(1024, rows - r)
                    sp.dma_start(dram[r:r + k, :].rearrange("(p a) d -> p (a d)", p=P),
                                 zeros[:, 0:k * D // P]).then_inc(filled, 16)
                    n += 1
            sp.wait_ge(loaded, 16)
            sp.wait_ge(filled, 16 * n)

        @block.gpsimd
        def _(pool):
            pool.memset(zeros[:, :], 0.0).then_inc(zeroed, 1)
            for m in (env.ident, env.swap):
                pool.memset(m[:, :], 0.0)
            pool.memset(env.ones[:, :], 1.0)
            pool.memset(env.eps[:, :], EPS)
            pool.memset(env.before[:, :], 1.0)
            pool.memset(env.earlier[:, :, :], 1.0).then_inc(const0, 1)
            pool.wait_ge(const0, 1)
            pool.affine_select(out=env.ident[:, :], in_=env.ident[:, :], compare_op=ALU.not_equal, fill=1.0,
                               base=0, pattern=[[-1, P]], channel_multiplier=1)
            sw = env.swap[:, :].rearrange("p (j i) -> p j i", i=VW)
            pool.affine_select(out=sw, in_=sw, compare_op=ALU.not_equal, fill=1.0,
                               base=-HP, pattern=[[-VW, GH], [0, VW]], channel_multiplier=1)
            pool.affine_select(out=env.before[:, :], in_=env.before[:, :], compare_op=ALU.is_gt, fill=0.0,
                               base=0, pattern=[[1, P]], channel_multiplier=-1)
            pool.affine_select(out=env.earlier[:, :, :], in_=env.earlier[:, :, :], compare_op=ALU.is_gt,
                               fill=0.0, base=0, pattern=[[1, E1], [-1, E1]], channel_multiplier=0)
            pool.iota(env.iota[:, :], [[1, TILES1]], base=0, channel_multiplier=0,
                      allow_small_or_imprecise_dtypes=True)


def project(nc, env, ins, lay):
    L, hd, halves, gpb = lay.name, lay.hd, lay.halves, lay.gpb
    heads, width = lay.heads, lay.heads * HP
    with ExitStack() as ctx:
        sb, ps, sem = scope(nc, ctx)
        ctxT = sb(f"ctxT{L}", [P, KD, TOK])
        XN = sb(f"XN{L}", [P, NT, D])
        XNT = sb(f"XNT{L}", [P, KD, TOK])
        W = {w: sb(f"w{w}{L}", [P, KD, width]) for w in "qkv"}
        bias = {w: sb(f"b{w}{L}", [P, halves]) for w in "qk"}
        bv = sb(f"bv{L}", [1, width])
        parts = sb(f"parts{L}", [P, 2, 3, SEQ], BF16)
        rest = sb(f"rest{L}", [P, 2, SEQ])
        stats, mv, rstd = sb(f"st{L}", [P, NT, 6]), sb(f"mv{L}", [P, NT, 2]), sb(f"rs{L}", [P, NT])
        tp = ps(f"tp{L}", [P, 2, SEQ])
        pv = ps(f"pv{L}", [P, 2, SEQ])
        pq = ps(f"pq{L}", [P, 2, SEQ])
        w_zero, w_loaded, ctx_loaded = sem(f"w_zero{L}"), sem(f"w_loaded{L}"), sem(f"ctx_loaded{L}")
        chain, xn_done = sem(f"chain{L}"), sem(f"xn_done{L}")
        tp_ready, xnt_done = sem(f"tp_ready{L}"), sem(f"xnt_done{L}")
        v_ready, v_done = sem(f"v_ready{L}"), sem(f"v_done{L}")
        qk_ready, p1_done, r1_done, p2_done, p3_done = (
            sem(f"{n}{L}") for n in ("qk_ready", "p1_done", "r1_done", "p2_done", "p3_done"))
        stored = [sem(f"stored{i}{L}") for i in range(2)]
        var_ready, dev_done = sem(f"var_ready{L}"), sem(f"dev_done{L}")
        block = ctx.enter_context(nc.Block())

        units = [(w, half, b) for w in "kq" for half in range(halves) for b in range(BATCH)]
        n_loads = 8 if hd == HP else 2 * KD * 3 // 2 + 3

        @block.sync
        def _(sp):
            sp.dma_start(ctxT[:, :, :], ins["ctxT"].rearrange("(k p) t -> p k t", p=P)).then_inc(ctx_loaded, 16)
            sp.wait_ge(w_zero, 1)
            for w in "qkv":
                src = ins[f"W{w}{L}"].rearrange("(k p) (h d) -> k p h d", p=P, d=hd)
                for k in range(KD):
                    dst = W[w][:, k, :].rearrange("p (h d) -> p h d", d=HP)[:, :, 0:hd]
                    sp.dma_start(dst, src[k]).then_inc(w_loaded, 16)
            for w in "qk":
                src = ins[f"b{w}{L}"]
                if hd == HP:
                    with nc.allow_non_contiguous_dma(reason="a small bias"):
                        sp.dma_start(bias[w][:, :], src.rearrange("(f p) -> p f", p=P)).then_inc(w_loaded, 16)
                else:
                    for h in range(heads):
                        with nc.allow_non_contiguous_dma(reason="a small bias"):
                            sp.dma_start(bias[w][HP * h:HP * h + hd, 0:1],
                                         src[hd * h:hd * h + hd].unsqueeze(1)).then_inc(w_loaded, 16)
            sp.dma_start(bv[0:1, :].rearrange("o (h d) -> o h d", d=HP)[:, :, 0:hd],
                         ins[f"bv{L}"].rearrange("(o h d) -> o h d", o=1, d=hd)).then_inc(w_loaded, 16)
            for i, (w, half, b) in enumerate(units):
                sp.wait_ge(p3_done, i + 1)
                first = b * gpb + half * (P // (GH * HP))
                dst = env.scr[w][:, first:first + 2, :, :].rearrange("s g r t -> (g r) s t")
                sp.dma_start(dst, parts[:, i % 2, :, :]).then_inc(stored[i % 2], 16)
            for i in range(2):
                sp.wait_ge(stored[i], 16 * len(units) // 2)

        weights = 16 * (3 * KD + 1 + (2 if hd == HP else 2 * heads))

        @block.gpsimd
        def _(pool):
            if hd != HP:
                for w in "qkv":
                    pool.memset(W[w][:, :, :], 0.0)
                for w in "qk":
                    pool.memset(bias[w][:, :], 0.0)
            pool.memset(bv[:, :], 0.0).then_inc(w_zero, 1)

        @block.vector
        def _(dve):
            link = Link(dve, chain)
            link(dve.memset(env.VA[:, 0:lay.groups, :, :], 1.0))
            layernorm(dve, link, env.X, XN, stats, mv, rstd, var_ready, dev_done, 0, xn_done)
            for i, (w, half, b) in enumerate(units):
                dve.wait_ge(p1_done, i + 1)
                if i >= 2:
                    dve.wait_ge(p2_done, i - 1)
                dve.scalar_tensor_tensor(rest[:, i % 2, :], pq[:, i % 2, :], bias[w][:, half:half + 1],
                                         parts[:, i % 2, 0, :], ALU.add, ALU.subtract).then_inc(r1_done, 1)
                dve.wait_ge(p2_done, i + 1)
                dve.tensor_tensor(parts[:, i % 2, 2, :], rest[:, i % 2, :], parts[:, i % 2, 1, :],
                                  ALU.subtract).then_inc(p3_done, 1)

        @block.scalar
        def _(act):
            deviation(act, env, mv, rstd, var_ready, dev_done, 0)
            act.wait_ge(chain, 1)
            for t in range(NT):
                act.wait_ge(v_ready, t + 1)
                b, kt = divmod(t, TPB)
                dst = env.VA[:, b * gpb:(b + 1) * gpb, kt, :].rearrange("p g (h c) -> p g h c", c=VW)
                src = pv[:, t % 2, 0:width].rearrange("p (g h c) -> p g h c", h=GH, c=HP)
                for g in range(gpb):
                    ins_ = act.copy(dst[:, g, :, 0:HP], src[:, g, :, :])
                ins_.then_inc(v_done, 1)

            def split(i):
                w, half, b = units[i]
                act.wait_ge(qk_ready, i + 1)
                if i >= 2:
                    act.wait_ge(stored[i % 2], 16 * (i // 2))
                act.activation(parts[:, i % 2, 0, :], pq[:, i % 2, :], ACT.Identity,
                               bias=bias[w][:, half:half + 1]).then_inc(p1_done, 1)
                act.wait_ge(r1_done, i + 1)
                act.copy(parts[:, i % 2, 1, :], rest[:, i % 2, :]).then_inc(p2_done, 1)

            for i in range(halves * BATCH):
                split(i)
            for n in range(TPB * KD):
                t4, k = divmod(n, KD)
                act.wait_ge(tp_ready, n + 1)
                act.copy(XNT[:, k, t4 * SEQ:(t4 + 1) * SEQ], tp[:, n % 2, :]).then_inc(xnt_done, 1)
            for i in range(halves * BATCH, len(units)):
                split(i)

        @block.tensor
        def _(pe):
            pe.wait_ge(ctx_loaded, 16)
            pe.wait_ge(w_loaded, weights)
            for t in range(NT):
                if t >= 2:
                    pe.wait_ge(v_done, t - 1)
                for k in range(KD):
                    pe.matmul(pv[:, t % 2, 0:width], ctxT[:, k, t * P:(t + 1) * P], W["v"][:, k, :],
                              start=(k == 0), stop=False)
                pe.matmul(pv[:, t % 2, 0:width], env.ones[0:1, :], bv[:, :],
                          start=False, stop=True).then_inc(v_ready, 1)

            def unit(i):
                w, half, b = units[i]
                src = ctxT if w == "k" else XNT
                if i >= 2:
                    pe.wait_ge(r1_done, i - 1)
                for k in range(KD):
                    m = pe.matmul(pq[:, i % 2, :], W[w][:, k, half * P:(half + 1) * P],
                                  src[:, k, b * SEQ:(b + 1) * SEQ], start=(k == 0), stop=(k == KD - 1))
                m.then_inc(qk_ready, 1)

            for i in range(halves * BATCH):
                unit(i)
            for n in range(TPB * KD):
                t4, k = divmod(n, KD)
                pe.wait_ge(xn_done, (t4 + 1) * TPB)
                if n >= 2:
                    pe.wait_ge(xnt_done, n - 1)
                for j in range(TPB):
                    m = pe.transpose(tp[:, n % 2, j * P:(j + 1) * P], XN[:, t4 * TPB + j, k * P:(k + 1) * P],
                                     env.ident[:, :])
                m.then_inc(tp_ready, 1)
            for i in range(halves * BATCH, len(units)):
                b = units[i][2]
                pe.wait_ge(xnt_done, KD * (b + 1))
                unit(i)


def attend(nc, env, lay):
    L, NG = lay.name, lay.groups
    with ExitStack() as ctx:
        sb, ps, sem = scope(nc, ctx)
        QS = sb(f"QS{L}", [P, SLOTS, GH, SEQ], BF16)
        KS = sb(f"KS{L}", [P, SLOTS, GH, SEQ], BF16)
        PT = sb(f"PT{L}", [P, 2, GH, TPB, SEQ])
        VG = sb(f"VG{L}", [P, 2, TPB, P])
        M = sb(f"M{L}", [P, 2, GH * TPB])
        NM = sb(f"NM{L}", [GH * TPB, 2, SHIFT, P], BF16)
        OSB = sb(f"OSB{L}", [P, 2, SEQ])
        RI = sb(f"RI{L}", [P, SEQ])
        S1 = ps(f"S1{L}", [P, 2, SEQ])
        S2 = ps(f"S2{L}", [P, 2, 2, SEQ])
        PV = ps(f"PV{L}", [P, SEQ])
        MISC = ps(f"MISC{L}", [P, SEQ])
        qk_loaded = [sem(f"qk_loaded{i}{L}") for i in range(SLOTS)]
        nm_loaded = [sem(f"nm_loaded{i}{L}") for i in range(SLOTS)]
        (shift_ones, s1_ready, max_done, mt_ready, nm1_done, nm_done, s2_ready, exp_done, vg_ready, pv_ready,
         osb_done, sw_ready, rinv_done, on_done) = (sem(n + L) for n in (
             "shift_ones", "s1_ready", "max_done", "mt_ready", "nm1_done", "nm_done", "s2_ready", "exp_done",
             "vg_ready", "pv_ready", "osb_done", "sw_ready", "rinv_done", "on_done"))
        loads = 16 * (len(Q_TERMS) + len(K_TERMS))
        block = ctx.enter_context(nc.Block())

        def steps(eng, step):
            for c in range(SLOTS + 1):
                step(0, c)
            if NG > 2 * SLOTS:
                with eng.Fori(1, NG // SLOTS - 1) as r:
                    for c in range(1, 1 + SLOTS):
                        step(r, c)
            for c in range(1, SLOTS):
                step(NG // SLOTS - 1, c)

        def last(r, c, ahead):
            return isinstance(r, int) and SLOTS * r + c + ahead >= NG

        @block.sync
        def _(sp):
            def load(r, c):
                n, slot = r * SLOTS + c, c % SLOTS
                for stack, terms, w in ((QS, Q_TERMS, "q"), (KS, K_TERMS, "k")):
                    for i, part in enumerate(terms):
                        sp.dma_start(stack[HP * i:HP * (i + 1), slot, :, :],
                                     env.scr[w][part, n, :, :].rearrange("(h d) t -> d h t", d=HP)
                                     ).then_inc(qk_loaded[slot], 16)

            def shift(r, c):
                n, slot = r * SLOTS + c, c % SLOTS
                sp.wait_ge(nm_done, n + 1)
                for i in range(SHIFT):
                    sp.dma_start(QS[ROWS + i:ROWS + i + 1, slot, :, :].rearrange("o h (q t) -> o (h q) t", t=P),
                                 NM[:, c % 2, i, :]).then_inc(nm_loaded[slot], 16)

            for c in range(SLOTS - 1):
                load(0, c)
            shift(0, 0)

            def step(r, c):
                if not last(r, c, 3):
                    wait(sp, s2_ready, 8 * (r * SLOTS + c))
                    load(r, c + 3)
                if not last(r, c, 1):
                    shift(r, c + 1)

            steps(sp, step)

        @block.gpsimd
        def _(pool):
            pool.memset(KS[ROWS:ROWS + 32, :, :, :], 1.0).then_inc(shift_ones, 1)
            pool.wait_ge(shift_ones, 1)

            def step(r, c):
                n = r * SLOTS + c
                wait(pool, pv_ready, n - 1)
                pool.tensor_copy(VG[:, c % 2, :, :], env.VA[:, n, :, :]).then_inc(vg_ready, 1)

            steps(pool, step)

        @block.tensor
        def _(pe):
            def maxima(r, c, h):
                n, slot = r * SLOTS + c, c % SLOTS
                if h == 0:
                    pe.wait_ge(qk_loaded[slot], loads * (r + c // SLOTS + 1))
                for q in range(TPB):
                    i = n * GH * TPB + h * TPB + q
                    wait(pe, max_done, i - 1)
                    pe.matmul(S1[:, q % 2, :], QS[0:ROWS, slot, h, q * P:(q + 1) * P], KS[0:ROWS, slot, h, :],
                              start=True, stop=True).then_inc(s1_ready, 1)

            def turn(r, c):
                n = r * SLOTS + c
                pe.wait_ge(max_done, GH * TPB * (n + 1))
                wait(pe, rinv_done, n - 2)
                pe.transpose(MISC[0:GH * TPB, 0:P], M[:, c % 2, :], env.ident[:, :]).then_inc(mt_ready, 1)

            def scores(r, c, h):
                n, slot = r * SLOTS + c, c % SLOTS
                if h == 0:
                    pe.wait_ge(nm_loaded[slot], 16 * SHIFT * (r + c // SLOTS + 1))
                for u in range(2):
                    i = n * 2 * GH + h * 2 + u
                    wait(pe, exp_done, i - 1)
                    for j in range(2):
                        kt = 2 * u + j
                        m = pe.matmul(S2[:, u, j, :], KS[0:ROWS + SHIFT, slot, h, kt * P:(kt + 1) * P],
                                      QS[0:ROWS + SHIFT, slot, h, :], start=True, stop=True)
                    m.then_inc(s2_ready, 1)

            def values(r, c):
                n = r * SLOTS + c
                pe.wait_ge(exp_done, 2 * GH * (n + 1))
                pe.wait_ge(vg_ready, n + 1)
                wait(pe, osb_done, n)
                for kt in range(TPB):
                    for h in range(GH):
                        m = pe.matmul(PV[VW * h:VW * (h + 1), :], VG[:, c % 2, kt, VW * h:VW * (h + 1)],
                                      PT[:, c % 2, h, kt, :], start=(kt == 0), stop=(kt == TPB - 1))
                m.then_inc(pv_ready, 1)

            def sums(r, c, turned):
                n = r * SLOTS + c
                pe.wait_ge(osb_done, n + 1)
                pe.wait_ge(nm_done, turned)
                wait(pe, rinv_done, n)
                pe.matmul(MISC[:, :], env.swap[:, :], OSB[:, c % 2, :], start=True, stop=True).then_inc(sw_ready, 1)

            pe.wait_ge(shift_ones, 1)
            for c in range(2):
                for h in range(GH):
                    maxima(0, c, h)
            turn(0, 0)

            def step(r, c):
                n = r * SLOTS + c
                first = isinstance(r, int) and n == 0
                for h in range(GH):
                    scores(r, c, h)
                    if not last(r, c, 2):
                        maxima(r, c + 2, h)
                    if h == 0 and not last(r, c, 1):
                        turn(r, c + 1)
                    if h == 1 and not first:
                        values(r, c - 1)
                    if h == 3 and not first:
                        sums(r, c - 1, NG if last(r, c, 2) else n + 2)

            steps(pe, step)
            values((NG - 1) // SLOTS, (NG - 1) % SLOTS)
            sums((NG - 1) // SLOTS, (NG - 1) % SLOTS, NG)

        @block.scalar
        def _(act):
            def negate(r, c):
                n = r * SLOTS + c
                act.wait_ge(mt_ready, n + 1)
                if not (isinstance(r, int) and n < 2):
                    act.wait_ge(nm_loaded[(c - 2) % SLOTS], 16 * SHIFT * (r + (c - 2) // SLOTS + 1))
                act.activation(NM[:, c % 2, 0, :], MISC[0:GH * TPB, 0:P], ACT.Copy, scale=-1.0).then_inc(nm1_done, 1)

            def keep(r, c):
                n = r * SLOTS + c
                act.wait_ge(pv_ready, n + 1)
                wait(act, on_done, n)
                act.copy(OSB[:, c % 2, :], PV[:, :]).then_inc(osb_done, 1)

            negate(0, 0)

            def step(r, c):
                n = r * SLOTS + c
                wait(act, pv_ready, n - 1)
                for h in range(GH):
                    for u in range(2):
                        act.wait_ge(s2_ready, n * 2 * GH + h * 2 + u + 1)
                        act.activation(PT[:, c % 2, h, 2 * u:2 * u + 2, :], S2[:, u, :, :], ACT.Exp,
                                       scale=lay.scale).then_inc(exp_done, 1)
                    if h == 0 and not last(r, c, 1):
                        negate(r, c + 1)
                    if h == 2 and not (isinstance(r, int) and n == 0):
                        keep(r, c - 1)

            steps(act, step)
            keep((NG - 1) // SLOTS, (NG - 1) % SLOTS)

        @block.vector
        def _(dve):
            def maxima(r, c, h):
                n = r * SLOTS + c
                if h == 0:
                    wait(dve, mt_ready, n - 1)
                for q in range(TPB):
                    i = n * GH * TPB + h * TPB + q
                    dve.wait_ge(s1_ready, i + 1)
                    dve.tensor_reduce(M[:, c % 2, h * TPB + q:h * TPB + q + 1], S1[:, q % 2, :], AX.X,
                                      ALU.max).then_inc(max_done, 1)

            def negate(r, c):
                dve.wait_ge(nm1_done, r * SLOTS + c + 1)
                dve.scalar_tensor_tensor(NM[:, c % 2, 1, :], MISC[0:GH * TPB, 0:P], -1.0, NM[:, c % 2, 0, :],
                                         ALU.mult, ALU.subtract).then_inc(nm_done, 1)

            def normalize(r, c):
                n = r * SLOTS + c
                dve.wait_ge(sw_ready, n + 1)
                wait(dve, on_done, n)
                dve.reciprocal(RI[:, :], MISC[:, :]).then_inc(rinv_done, 1)
                dve.wait_ge(rinv_done, n + 1)
                dve.tensor_tensor(env.ON[:, n, :], OSB[:, c % 2, :], RI[:, :], ALU.mult).then_inc(on_done, 1)

            for c in range(2):
                for h in range(GH):
                    maxima(0, c, h)
            negate(0, 0)

            def step(r, c):
                first = isinstance(r, int) and r * SLOTS + c == 0
                for h in range(GH):
                    if not last(r, c, 2):
                        maxima(r, c + 2, h)
                    if h == 1 and not last(r, c, 1):
                        negate(r, c + 1)
                if not first:
                    normalize(r, c - 1)

            steps(dve, step)
            normalize((NG - 1) // SLOTS, (NG - 1) % SLOTS)


def pick(dve, link, env, w, E, K, logits, cut):
    wide = [P, NT, E]
    if cut:
        link(dve.tensor_scalar(w.lg[:, :, :], logits, -1e4, 1e4, ALU.max, ALU.min))
    else:
        link(dve.tensor_copy(w.lg[:, :, :], logits))
    link(dve.tensor_reduce(w.red[:, :], w.lg[:, :, :], AX.X, ALU.max))
    link(dve.tensor_tensor(w.lg[:, :, :], w.lg[:, :, :], w.red[:, :].unsqueeze(2).to_broadcast(wide), ALU.subtract))


def softmax_top(dve, link, env, w, E, K, floor):
    wide = [P, NT, E]
    link(dve.tensor_reduce(w.red[:, :], w.ex[:, :, :], AX.X, ALU.add))
    if floor:
        link(dve.tensor_scalar(w.red[:, :], w.red[:, :], floor, None, ALU.add))
    link(dve.reciprocal(w.red2[:, :], w.red[:, :]))
    link(dve.tensor_tensor(w.pr[:, :, :], w.ex[:, :, :], w.red2[:, :].unsqueeze(2).to_broadcast(wide), ALU.mult))
    for t in range(NT):
        ins = dve.max(w.top[:, t, :], w.pr[:, t, :])
    link(ins)
    for t in range(NT):
        ins = dve.max_index(w.idx[:, t, :], w.top[:, t, :], w.pr[:, t, :])
    link(ins)
    link(dve.tensor_copy(w.idf[:, :, :], w.idx[:, :, 0:K].rearrange("p t k -> p k t")))
    for k in range(K):
        ins = dve.tensor_tensor(w.hot[:, k, :, :], env.iota[:, 0:E].unsqueeze(1).to_broadcast(wide),
                                w.idf[:, k, :].unsqueeze(2).to_broadcast(wide), ALU.is_equal)
    link(ins)
    link(dve.tensor_tensor(w.all[:, :, :], w.hot[:, 0, :, :], w.hot[:, 1, :, :], ALU.add))
    for k in range(2, K):
        link(dve.tensor_tensor(w.all[:, :, :], w.all[:, :, :], w.hot[:, k, :, :], ALU.add))
    link(dve.memset(w.run[:, 0, :], 0.0))
    for t in range(NT):
        link(dve.tensor_tensor(w.run[:, t + 1, :], w.run[:, t, :], w.all[:, t, :], ALU.add))


class Work:
    pass


def routing_buffers(sb, L, E, K):
    w = Work()
    w.lg, w.ex, w.pr, w.all, w.tmp = (sb(f"{n}{L}", [P, NT, E]) for n in ("lg", "ex", "pr", "all", "tmp"))
    w.red, w.red2 = sb(f"red{L}", [P, NT]), sb(f"red2{L}", [P, NT])
    w.top, w.idx = sb(f"top{L}", [P, NT, 8]), sb(f"idx{L}", [P, NT, 8], U32)
    w.idf, w.hot = sb(f"idf{L}", [P, K, NT]), sb(f"hot{L}", [P, K, NT, E])
    w.run = sb(f"run{L}", [P, NT + 1, E])
    w.rank, w.over = sb(f"rank{L}", [P, K, NT]), sb(f"over{L}", [P, K, NT])
    w.slot = sb(f"pos{L}", [P, K, NT])
    return w


def out_projection(pe, env, lay, WO, po, wo_loaded, wo_ready, x_done):
    pe.wait_ge(wo_loaded, 16 * (lay.gpb * GH + 1))
    for t in range(NT):
        b, q = divmod(t, TPB)
        if t >= 2:
            pe.wait_ge(x_done, t - 1)
        for g in range(lay.gpb):
            m = pe.matmul(po[:, t % 2, 0:D], env.ON[:, b * lay.gpb + g, q * P:(q + 1) * P], WO[:, g, :],
                          start=(g == 0), stop=(g == lay.gpb - 1))
        m.then_inc(wo_ready, 1)


def load_out_weights(sp, ins, lay, WO, wo_zero, wo_loaded):
    sp.wait_ge(wo_zero, 1)
    for g in range(lay.gpb):
        for h in range(GH):
            r = (g * GH + h) * lay.hd
            sp.dma_start(WO[VW * h:VW * h + lay.hd, g, :], ins[f"Wo{lay.name}"][r:r + lay.hd, :]).then_inc(wo_loaded, 16)
    sp.dma_start(WO[HP:HP + 1, 0, :], ins[f"bo{lay.name}"].unsqueeze(0)).then_inc(wo_loaded, 16)


def route0(nc, env, ins, lay):
    with ExitStack() as ctx:
        sb, ps, sem = scope(nc, ctx)
        WO = sb("WO0", [P, lay.gpb, D])
        Hn, XF, XFT = sb("H0", [P, NT, D]), sb("XF0", [P, NT, D]), sb("XFT0", [P, KD, TOK])
        gamma, beta, Wr = sb("gamma", [P, D]), sb("beta", [P, D]), sb("Wr", [P, KD, E0])
        stats, mv, rstd = sb("st0r", [P, NT, 6]), sb("mv0r", [P, NT, 2]), sb("rs0r", [P, NT])
        w = routing_buffers(sb, "0", E0, K0)
        var_ready, dev_done = sem("var_ready0r"), sem("dev_done0r")
        into = sb("into0", [P, K0, NT], U32)
        po, tp = ps("po0", [P, 2, SEQ]), ps("tp0r", [P, 2, SEQ])
        lgp, rk = ps("lgp0", [P, NT, E0]), ps("rk0", [P, NT, E0])
        wo_zero, wo_loaded, wo_ready, x_done, chain, xf_done, r_loaded = (sem(n + "0r") for n in (
            "wo_zero", "wo_loaded", "wo_ready", "x_done", "chain", "xf_done", "r_loaded"))
        tp_ready, xft_done, lg_ready, lg_sub, ex_done, run_done, rk_ready, slots_done, scattered = (
            sem(n + "0r") for n in ("tp_ready", "xft_done", "lg_ready", "lg_sub", "ex_done", "run_done", "rk_ready",
                                    "slots_done", "scattered"))
        block = ctx.enter_context(nc.Block())

        @block.sync
        def _(sp):
            sp.dma_start(gamma[:, :], ins["gamma"].partition_broadcast(P)).then_inc(r_loaded, 16)
            sp.dma_start(beta[:, :], ins["beta"].partition_broadcast(P)).then_inc(r_loaded, 16)
            with nc.allow_non_contiguous_dma(reason="a small matrix"):
                sp.dma_start(Wr[:, :, :], ins["WrT"].rearrange("(k p) e -> p k e", p=P)).then_inc(r_loaded, 16)
            load_out_weights(sp, ins, lay, WO, wo_zero, wo_loaded)

        @block.gpsimd
        def _(pool):
            pool.memset(WO[:, :, :], 0.0).then_inc(wo_zero, 1)
            pool.wait_ge(slots_done, 1)
            for t in range(NT):
                for k in range(K0):
                    pool.indirect_dma_start(
                        out=env.xs0[:, :], out_offset=bass.IndirectOffsetOnAxis(ap=into[:, k, t:t + 1], axis=0),
                        in_=XF[:, t, :], in_offset=None, bounds_check=E0 * CAP0 - 1, oob_is_err=False,
                    ).then_inc(scattered, 16)
            pool.wait_ge(scattered, 16 * NT * K0)

        @block.tensor
        def _(pe):
            out_projection(pe, env, lay, WO, po, wo_loaded, wo_ready, x_done)
            for n in range(TPB * KD):
                t4, k = divmod(n, KD)
                pe.wait_ge(xf_done, 1)
                if n >= 2:
                    pe.wait_ge(xft_done, n - 1)
                for j in range(TPB):
                    m = pe.transpose(tp[:, n % 2, j * P:(j + 1) * P], XF[:, t4 * TPB + j, k * P:(k + 1) * P],
                                     env.ident[:, :])
                m.then_inc(tp_ready, 1)
            pe.wait_ge(xft_done, TPB * KD)
            pe.wait_ge(r_loaded, 48)
            for t in range(NT):
                for k in range(KD):
                    m = pe.matmul(lgp[:, t, :], XFT[:, k, t * P:(t + 1) * P], Wr[:, k, :],
                                  start=(k == 0), stop=(k == KD - 1))
            m.then_inc(lg_ready, 1)
            pe.wait_ge(run_done, 1)
            pe.matmul(rk[:, :, :], env.before[:, :], w.all[:, :, :], start=True, stop=False)
            pe.matmul(rk[:, :, :], env.ones[:, :], w.run[:, 0:NT, :], start=False, stop=True).then_inc(rk_ready, 1)

        @block.scalar
        def _(act):
            for n in range(2):
                deviation(act, env, mv, rstd, var_ready, dev_done, n)
            for n in range(TPB * KD):
                t4, k = divmod(n, KD)
                act.wait_ge(tp_ready, n + 1)
                act.copy(XFT[:, k, t4 * SEQ:(t4 + 1) * SEQ], tp[:, n % 2, :]).then_inc(xft_done, 1)
            act.wait_ge(lg_sub, 1)
            act.activation(w.ex[:, :, :], w.lg[:, :, :], ACT.Exp).then_inc(ex_done, 1)

        @block.vector
        def _(dve):
            link = Link(dve, chain)
            for t in range(NT):
                dve.wait_ge(wo_ready, t + 1)
                dve.tensor_tensor(env.X[:, t, :], po[:, t % 2, 0:D], env.X[:, t, :], ALU.add).then_inc(x_done, 1)
            dve.wait_ge(x_done, NT)
            layernorm(dve, link, env.X, Hn, stats, mv, rstd, var_ready, dev_done, 0)
            layernorm(dve, link, Hn, XF, stats, mv, rstd, var_ready, dev_done, 1)
            dve.wait_ge(r_loaded, 48)
            wide = [P, NT, D]
            link(dve.tensor_tensor(XF[:, :, :], XF[:, :, :], gamma[:, :].unsqueeze(1).to_broadcast(wide), ALU.mult))
            dve.tensor_tensor(XF[:, :, :], XF[:, :, :], beta[:, :].unsqueeze(1).to_broadcast(wide),
                              ALU.add).then_inc(xf_done, 1)
            dve.wait_ge(lg_ready, 1)
            pick(dve, link, env, w, E0, K0, lgp[:, :, :], True)
            dve.nop().then_inc(lg_sub, 1)
            dve.wait_ge(ex_done, 1)
            softmax_top(dve, link, env, w, E0, K0, 1e-12)
            dve.nop().then_inc(run_done, 1)
            dve.wait_ge(rk_ready, 1)
            for k in range(K0):
                link(dve.tensor_tensor(w.tmp[:, :, :], rk[:, :, :], w.hot[:, k, :, :], ALU.mult))
                link(dve.tensor_reduce(w.rank[:, k, :], w.tmp[:, :, :], AX.X, ALU.add))
            link(dve.tensor_scalar(w.over[:, :, :], w.rank[:, :, :], float(CAP0), None, ALU.is_ge))
            link(dve.scalar_tensor_tensor(w.slot[:, :, :], w.idf[:, :, :], float(CAP0), w.rank[:, :, :],
                                          ALU.mult, ALU.add))
            link(dve.scalar_tensor_tensor(into[:, :, :], w.over[:, :, :], float(FAR), w.slot[:, :, :],
                                          ALU.mult, ALU.add))
            link(dve.tensor_scalar(w.rank[:, :, :], w.rank[:, :, :], float(CAP0 - 1), None, ALU.min))
            link(dve.scalar_tensor_tensor(env.slot0[:, :, :], w.idf[:, :, :], float(CAP0), w.rank[:, :, :],
                                          ALU.mult, ALU.add))
            link(dve.tensor_scalar(w.over[:, :, :], w.over[:, :, :], -1.0, 1.0, ALU.mult, ALU.add))
            link(dve.tensor_tensor(env.wt0[:, :, :], w.top[:, :, 0:K0].rearrange("p t k -> p k t"), w.over[:, :, :],
                                   ALU.mult))
            dve.nop().then_inc(slots_done, 1)


def experts0(nc, env, ins):
    NTE = CAP0 // P
    FB = FF0 // P
    HALF = CAP0 // 2
    with ExitStack() as ctx:
        sb, ps, sem = scope(nc, ctx)
        W12, W3 = sb("W12", [P, 2, KD, 2 * FF0]), sb("W3", [P, 2, FB, D])
        XS, XST = sb("XSm0", [P, 2, NTE, D]), sb("XSTm0", [P, KD, CAP0])
        SG, HT, YS = sb("SGm0", [P, 2, HALF]), sb("HTm0", [P, FB, CAP0]), sb("YSm0", [P, 2, NTE, D])
        G, U = ps("Gm0", [P, 2, SEQ]), ps("Um0", [P, 2, SEQ])
        TP, Y = ps("TPm0", [P, 2, SEQ]), ps("Ym0", [P, 2, SEQ])
        w_loaded = [sem(f"w_loaded{i}m0") for i in range(2)]
        y_stored = [sem(f"y_stored{i}m0") for i in range(2)]
        tp_ready, xst_done, gu_ready, sg_done, h_done, y_ready, y_done = (
            sem(n + "m0") for n in ("tp_ready", "xst_done", "gu_ready", "sg_done", "h_done", "y_ready", "y_done"))
        block = ctx.enter_context(nc.Block())
        CH = 2 * FB

        def pairs(eng, expert):
            for s in range(2):
                expert(0, s)
            with eng.Fori(1, E0 // 2 - 1) as r:
                for s in range(2):
                    expert(r, s)
            for s in range(2):
                expert(E0 // 2 - 1, s)

        @block.sync
        def _(sp):
            def load(r, s):
                e = 2 * r + s
                sp.dma_start(XS[:, s, :, :], env.xs0[:, :].rearrange("(e n p) d -> e p n d", p=P, n=NTE)[e]
                             ).then_inc(w_loaded[s], 16)
                sp.dma_start(W12[:, s, :, :], ins["W12T"][e].rearrange("(k p) f -> p k f", p=P)
                             ).then_inc(w_loaded[s], 16)
                sp.dma_start(W3[:, s, :, :], ins["W3T"][e].rearrange("(j p) d -> p j d", p=P)
                             ).then_inc(w_loaded[s], 16)

            for s in range(2):
                load(0, s)

            def expert(r, s):
                e = 2 * r + s
                sp.wait_ge(y_done, NTE * (e + 1))
                sp.dma_start(env.ys0[:, :].rearrange("(e n p) d -> e p n d", p=P, n=NTE)[e], YS[:, s, :, :]
                             ).then_inc(y_stored[s], 16)
                if not (isinstance(r, int) and r == E0 // 2 - 1):
                    load(r + 1, s)

            pairs(sp, expert)
            for s in range(2):
                sp.wait_ge(y_stored[s], 16 * E0 // 2)

        @block.tensor
        def _(pe):
            def turn(r, s):
                e = 2 * r + s
                pe.wait_ge(w_loaded[s], 48 * (r + 1))
                for i in range(NTE):
                    wait(pe, xst_done, e * NTE + i - 1)
                    for k in range(KD):
                        m = pe.transpose(TP[:, (s * NTE + i) % 2, k * P:(k + 1) * P],
                                         XS[:, s, i, k * P:(k + 1) * P], env.ident[:, :])
                    m.then_inc(tp_ready, 1)

            turn(0, 0)

            def expert(r, s):
                e = 2 * r + s
                pe.wait_ge(xst_done, NTE * (e + 1))
                for c in range(CH):
                    j, half = divmod(c, 2)
                    wait(pe, h_done, e * CH + c - 1)
                    for bank, f in ((G, j * P), (U, FF0 + j * P)):
                        for k in range(KD):
                            m = pe.matmul(bank[:, half, 0:HALF], W12[:, s, k, f:f + P],
                                          XST[:, k, half * HALF:(half + 1) * HALF],
                                          start=(k == 0), stop=(k == KD - 1))
                    m.then_inc(gu_ready, 1)
                if not (isinstance(r, int) and e == E0 - 1):
                    turn(r + s, 1 - s)
                pe.wait_ge(h_done, CH * (e + 1))
                for i in range(NTE):
                    wait(pe, y_done, e * NTE + i - 1)
                    for j in range(FB):
                        m = pe.matmul(Y[:, (s * NTE + i) % 2, 0:D], HT[:, j, i * P:(i + 1) * P], W3[:, s, j, :],
                                      start=(j == 0), stop=(j == FB - 1))
                    m.then_inc(y_ready, 1)

            pairs(pe, expert)

        @block.scalar
        def _(act):
            def turn(r, s):
                for i in range(NTE):
                    act.wait_ge(tp_ready, (2 * r + s) * NTE + i + 1)
                    act.copy(XST[:, :, i * P:(i + 1) * P],
                             TP[:, (s * NTE + i) % 2, 0:D].rearrange("p (k c) -> p k c", k=KD)).then_inc(xst_done, 1)

            turn(0, 0)

            def expert(r, s):
                e = 2 * r + s
                for c in range(CH):
                    act.wait_ge(gu_ready, e * CH + c + 1)
                    wait(act, h_done, e * CH + c - 1)
                    act.activation(SG[:, c % 2, :], G[:, c % 2, 0:HALF], ACT.Silu).then_inc(sg_done, 1)
                if not (isinstance(r, int) and e == E0 - 1):
                    turn(r + s, 1 - s)

            pairs(act, expert)

        @block.vector
        def _(dve):
            def expert(r, s):
                e = 2 * r + s
                for c in range(CH):
                    j, half = divmod(c, 2)
                    dve.wait_ge(sg_done, e * CH + c + 1)
                    dve.tensor_tensor(HT[:, j, half * HALF:(half + 1) * HALF], U[:, half, 0:HALF], SG[:, half, :],
                                      ALU.mult).then_inc(h_done, 1)
                for i in range(NTE):
                    dve.wait_ge(y_ready, e * NTE + i + 1)
                    if i == 0 and not (isinstance(r, int) and r == 0):
                        dve.wait_ge(y_stored[s], 16 * r)
                    dve.tensor_copy(YS[:, s, i, :], Y[:, (s * NTE + i) % 2, 0:D]).then_inc(y_done, 1)

            pairs(dve, expert)


def combine(nc, env, L, K, ys, slot, wt, out=None):
    DEEP = 8
    with ExitStack() as ctx:
        sb, ps, sem = scope(nc, ctx)
        YG = sb(f"YG{L}", [P, DEEP, D])
        gathered = [sem(f"gathered{i}c{L}") for i in range(DEEP)]
        added, sent = sem(f"added{L}"), sem(f"sent{L}")
        block = ctx.enter_context(nc.Block())

        @block.gpsimd
        def _(pool):
            for n in range(NT * K):
                t, k = divmod(n, K)
                if n >= DEEP:
                    pool.wait_ge(added, n - DEEP + 1)
                pool.indirect_dma_start(
                    out=YG[:, n % DEEP, :], out_offset=None, in_=ys[:, :],
                    in_offset=bass.IndirectOffsetOnAxis(ap=slot[:, k, t:t + 1], axis=0),
                ).then_inc(gathered[n % DEEP], 16)

        @block.vector
        def _(dve):
            for n in range(NT * K):
                t, k = divmod(n, K)
                dve.wait_ge(gathered[n % DEEP], 16 * (n // DEEP + 1))
                if k:
                    dve.wait_ge(added, n)
                dve.scalar_tensor_tensor(env.X[:, t, :], YG[:, n % DEEP, :], wt[:, k, t:t + 1], env.X[:, t, :],
                                         ALU.mult, ALU.add).then_inc(added, 1)

        if out is not None:
            @block.sync
            def _(sp):
                for t in range(0, NT, 4):
                    sp.wait_ge(added, K * (t + 4))
                    sp.dma_start(out.rearrange("(t p) d -> p t d", p=P)[:, t:t + 4, :], env.X[:, t:t + 4, :]
                                 ).then_inc(sent, 16)
                sp.wait_ge(sent, 16 * (NT // 4))


def route1(nc, env, ins, lay):
    JS = FFS // P
    with ExitStack() as ctx:
        sb, ps, sem = scope(nc, ctx)
        WO = sb("WO1", [P, lay.gpb, D])
        XF, XFT = sb("XF1", [P, NT, D]), sb("XFT1", [P, KD, TOK])
        gate, s1, s2 = sb("gate", [P, KD, E1]), sb("s1", [P, KD, 2 * FFS]), sb("s2", [P, JS, D])
        s1b, smul = sb("s1b", [P, 2 * JS]), sb("smul", [P, JS])
        s2b, f2b = sb("s2b", [1, D]), sb("f2b", [E1, D])
        stats, mv, rstd = sb("st1r", [P, NT, 6]), sb("mv1r", [P, NT, 2]), sb("rs1r", [P, NT])
        w = routing_buffers(sb, "1", E1, K1)
        var_ready, dev_done = sem("var_ready1r"), sem("dev_done1r")
        comb, combT = sb("comb", [P, NT, E1]), sb("combT", [E1, TOK])
        fill, ntile, base, ends = sb("fill", [P, E1]), sb("ntile", [P, E1]), sb("base", [P, E1]), sb("ends", [P, E1])
        sq, many, upto = sb("sq", [P, E1, E1]), sb("many", [P, E1, NT]), sb("upto", [1, TILES1, E1])
        tile_e = sb("tile_e", [1, TILES1])
        GE, AT = sb("GE1", [P, 2, SEQ]), sb("AT1", [P, 2, JS, SEQ])
        pw, pg = ps("pw1", [P, 2, SEQ]), ps("pg1", [P, 4, SEQ])
        lgp, rk = ps("lgp1", [P, NT, E1]), ps("rk1", [P, NT + 1, E1])
        wo_zero, wo_loaded, wo_ready, x_done, chain, xf_done, r_loaded, chain_p = (sem(n + "1r") for n in (
            "wo_zero", "wo_loaded", "wo_ready", "x_done", "chain", "xf_done", "r_loaded", "chain_p"))
        tp_ready, xft_done, lg_ready, lg_sub, ex_done, run_done, rk_ready, slots_done, scattered = (
            sem(n + "1r") for n in ("tp_ready", "xft_done", "lg_ready", "lg_sub", "ex_done", "run_done", "rk_ready",
                                    "slots_done", "scattered"))
        gs_ready, ge_done, at_done, ct_ready, ct_done, ys_ready, shared_done, folded = (sem(n + "1r") for n in (
            "gs_ready", "ge_done", "at_done", "ct_ready", "ct_done", "ys_ready", "shared_done", "folded"))
        block = ctx.enter_context(nc.Block())
        n_small = 8

        @block.sync
        def _(sp):
            with nc.allow_non_contiguous_dma(reason="small matrices and vectors"):
                sp.dma_start(gate[:, :, :], ins["gateT"].rearrange("(k p) e -> p k e", p=P)).then_inc(r_loaded, 16)
                sp.dma_start(s1b[:, :], ins["s_fc1_b"].rearrange("(j p) -> p j", p=P)).then_inc(r_loaded, 16)
                sp.dma_start(smul[:, :], ins["s_mult"].rearrange("(j p) -> p j", p=P)).then_inc(r_loaded, 16)
                sp.dma_start(env.mult[:, :, :], ins["mult"].rearrange("e (k p) -> p e k", p=P)).then_inc(r_loaded, 16)
            sp.dma_start(s2b[:, :], ins["s_fc2_b"].unsqueeze(0)).then_inc(r_loaded, 16)
            sp.dma_start(f2b[:, :], ins["fc2_b"]).then_inc(r_loaded, 16)
            load_out_weights(sp, ins, lay, WO, wo_zero, wo_loaded)
            sp.dma_start(s1[:, :, :], ins["s_fc1T"].rearrange("(k p) f -> p k f", p=P)).then_inc(r_loaded, 16)
            sp.dma_start(s2[:, :, :], ins["s_fc2T"].rearrange("(j p) d -> p j d", p=P)).then_inc(r_loaded, 16)

        @block.gpsimd
        def _(pool):
            pool.memset(WO[:, :, :], 0.0).then_inc(wo_zero, 1)
            pool.wait_ge(r_loaded, 16 * n_small)
            for j in range(JS):
                pool.tensor_scalar(s2[:, j, :], s2[:, j, :], smul[:, j:j + 1], None, ALU.mult).then_inc(folded, 1)
            pool.wait_ge(slots_done, 1)
            for t in range(NT):
                for k in range(K1):
                    pool.indirect_dma_start(
                        out=env.xs1[:, :], out_offset=bass.IndirectOffsetOnAxis(ap=env.slot1[:, k, t:t + 1], axis=0),
                        in_=XF[:, t, :], in_offset=None).then_inc(scattered, 16)
            pool.wait_ge(scattered, 16 * NT * K1)

        @block.tensor
        def _(pe):
            out_projection(pe, env, lay, WO, pw, wo_loaded, wo_ready, x_done)
            for n in range(TPB * KD):
                t4, k = divmod(n, KD)
                pe.wait_ge(xf_done, (t4 + 1) * TPB)
                if n >= 2:
                    pe.wait_ge(xft_done, n - 1)
                for j in range(TPB):
                    m = pe.transpose(pg[:, n % 2, j * P:(j + 1) * P], XF[:, t4 * TPB + j, k * P:(k + 1) * P],
                                     env.ident[:, :])
                m.then_inc(tp_ready, 1)
            pe.wait_ge(xft_done, TPB * KD)
            pe.wait_ge(r_loaded, 16 * n_small)
            for t in range(NT):
                for k in range(KD):
                    m = pe.matmul(lgp[:, t, :], XFT[:, k, t * P:(t + 1) * P], gate[:, k, :],
                                  start=(k == 0), stop=(k == KD - 1))
            m.then_inc(lg_ready, 1)

            def shared_in(c):
                for j in range(JS):
                    i = c * JS + j
                    if i >= 2:
                        pe.wait_ge(at_done, i - 1)
                    for half in range(2):
                        for k in range(KD):
                            m = pe.matmul(pg[:, 2 * (i % 2) + half, :], s1[:, k, half * FFS + j * P:half * FFS + (j + 1) * P],
                                          XFT[:, k, c * SEQ:(c + 1) * SEQ], start=(k == 0), stop=(k == KD - 1))
                    m.then_inc(gs_ready, 1)

            def shared_out(c):
                pe.wait_ge(at_done, JS * (c + 1))
                pe.wait_ge(folded, JS)
                for q in range(TPB):
                    t = c * TPB + q
                    if t >= 2:
                        pe.wait_ge(shared_done, t - 1)
                    for j in range(JS):
                        pe.matmul(pw[:, t % 2, 0:D], AT[:, c % 2, j, q * P:(q + 1) * P], s2[:, j, :],
                                  start=(j == 0), stop=False)
                    pe.matmul(pw[:, t % 2, 0:D], env.ones[0:1, :], s2b[:, :], start=False, stop=False)
                    pe.matmul(pw[:, t % 2, 0:D], combT[:, t * P:(t + 1) * P], f2b[:, :],
                              start=False, stop=True).then_inc(ys_ready, 1)

            shared_in(0)
            pe.wait_ge(run_done, 1)
            pe.matmul(rk[:, 0:NT, :], env.before[:, :], w.all[:, :, :], start=True, stop=False)
            pe.matmul(rk[:, 0:NT, :], env.ones[:, :], w.run[:, 0:NT, :], start=False, stop=True)
            pe.matmul(rk[:, NT, :], env.ones[:, :], w.run[:, NT, :], start=True, stop=True).then_inc(rk_ready, 1)
            shared_in(1)
            for t4 in range(TPB):
                if t4 >= 2:
                    pe.wait_ge(ct_done, t4 - 1)
                if t4 == 0:
                    pe.wait_ge(slots_done, 1)
                for j in range(TPB):
                    m = pe.transpose(pw[0:E1, t4 % 2, j * P:(j + 1) * P], comb[:, t4 * TPB + j, :], env.ident[:, :])
                m.then_inc(ct_ready, 1)
            pe.wait_ge(ct_done, TPB)
            for c in range(BATCH):
                shared_out(c)
                if c + 2 < BATCH:
                    shared_in(c + 2)

        @block.scalar
        def _(act):
            deviation(act, env, mv, rstd, var_ready, dev_done, 0)
            for n in range(TPB * KD):
                t4, k = divmod(n, KD)
                act.wait_ge(tp_ready, n + 1)
                act.copy(XFT[:, k, t4 * SEQ:(t4 + 1) * SEQ], pg[:, n % 2, :]).then_inc(xft_done, 1)
            act.wait_ge(lg_sub, 1)
            act.activation(w.ex[:, :, :], w.lg[:, :, :], ACT.Exp).then_inc(ex_done, 1)
            act.wait_ge(r_loaded, 16 * n_small)

            def gelu(c):
                for j in range(JS):
                    i = c * JS + j
                    act.wait_ge(gs_ready, i + 1)
                    if i >= 2:
                        act.wait_ge(at_done, i - 1)
                    act.activation(GE[:, i % 2, :], pg[:, 2 * (i % 2) + 1, :], ACT.Gelu,
                                   bias=s1b[:, JS + j:JS + j + 1]).then_inc(ge_done, 1)

            gelu(0)
            gelu(1)
            for t4 in range(TPB):
                act.wait_ge(ct_ready, t4 + 1)
                act.copy(combT[:, t4 * SEQ:(t4 + 1) * SEQ], pw[0:E1, t4 % 2, :]).then_inc(ct_done, 1)
            gelu(2)
            gelu(3)

        @block.vector
        def _(dve):
            link = Link(dve, chain)
            for t in range(NT):
                dve.wait_ge(wo_ready, t + 1)
                dve.tensor_tensor(env.X[:, t, :], pw[:, t % 2, 0:D], env.X[:, t, :], ALU.add).then_inc(x_done, 1)
            dve.wait_ge(x_done, NT)
            layernorm(dve, link, env.X, XF, stats, mv, rstd, var_ready, dev_done, 0, xf_done)
            dve.wait_ge(lg_ready, 1)
            pick(dve, link, env, w, E1, K1, lgp[:, :, :], False)
            dve.nop().then_inc(lg_sub, 1)
            dve.wait_ge(ex_done, 1)
            softmax_top(dve, link, env, w, E1, K1, 0.0)
            dve.nop().then_inc(run_done, 1)

            def shared(c):
                for j in range(JS):
                    i = c * JS + j
                    dve.wait_ge(ge_done, i + 1)
                    if c >= 2:
                        dve.wait_ge(ys_ready, TPB * (c - 1))
                    dve.scalar_tensor_tensor(AT[:, c % 2, j, :], pg[:, 2 * (i % 2), :], s1b[:, j:j + 1],
                                             GE[:, i % 2, :], ALU.add, ALU.mult).then_inc(at_done, 1)

            shared(0)
            dve.wait_ge(rk_ready, 1)
            link(dve.tensor_copy(fill[:, :], rk[:, NT, :]))
            link(dve.tensor_scalar(w.red[:, :], env.iota[:, 0:NT], float(P), None, ALU.mult))
            link(dve.tensor_tensor(many[:, :, :], fill[:, :].unsqueeze(2).to_broadcast([P, E1, NT]),
                                   w.red[:, :].unsqueeze(1).to_broadcast([P, E1, NT]), ALU.is_gt))
            link(dve.tensor_reduce(ntile[:, :], many[:, :, :], AX.X, ALU.add))
            link(dve.tensor_tensor(sq[:, :, :], ntile[:, :].unsqueeze(1).to_broadcast([P, E1, E1]),
                                   env.earlier[:, :, :], ALU.mult))
            link(dve.tensor_reduce(base[:, :], sq[:, :, :], AX.X, ALU.add))
            link(dve.tensor_tensor(ends[:, :], base[:, :], ntile[:, :], ALU.add))
            link(dve.tensor_tensor(upto[:, :, :], env.iota[0:1, :].unsqueeze(2).to_broadcast([1, TILES1, E1]),
                                   ends[0:1, :].unsqueeze(1).to_broadcast([1, TILES1, E1]), ALU.is_ge))
            link(dve.tensor_reduce(tile_e[:, :], upto[:, :, :], AX.X, ALU.add))
            link(dve.tensor_scalar(env.expert[:, :], tile_e[:, :], float(E1 - 1), None, ALU.min))
            link(dve.scalar_tensor_tensor(
                w.lg[:, :, :], base[:, :].unsqueeze(1).to_broadcast([P, NT, E1]), float(P), rk[:, 0:NT, :],
                ALU.mult, ALU.add))
            for k in range(K1):
                link(dve.tensor_tensor(w.tmp[:, :, :], w.lg[:, :, :], w.hot[:, k, :, :], ALU.mult))
                link(dve.tensor_reduce(w.slot[:, k, :], w.tmp[:, :, :], AX.X, ALU.add))
            link(dve.tensor_copy(env.slot1[:, :, :], w.slot[:, :, :]))
            link(dve.tensor_reduce(w.red[:, :], w.top[:, :, 0:K1], AX.X, ALU.add))
            link(dve.tensor_scalar(w.red[:, :], w.red[:, :], 1e-20, None, ALU.add))
            link(dve.reciprocal(w.red2[:, :], w.red[:, :]))
            for k in range(K1):
                link(dve.tensor_tensor(env.wt1[:, k, :], w.top[:, :, k], w.red2[:, :], ALU.mult))
                wide = env.wt1[:, k, :].unsqueeze(2).to_broadcast([P, NT, E1])
                if k == 0:
                    link(dve.tensor_tensor(comb[:, :, :], w.hot[:, k, :, :], wide, ALU.mult))
                else:
                    link(dve.tensor_tensor(w.tmp[:, :, :], w.hot[:, k, :, :], wide, ALU.mult))
                    link(dve.tensor_tensor(comb[:, :, :], comb[:, :, :], w.tmp[:, :, :], ALU.add))
            dve.nop().then_inc(slots_done, 1)
            shared(1)
            for c in range(BATCH):
                for q in range(TPB):
                    t = c * TPB + q
                    dve.wait_ge(ys_ready, t + 1)
                    dve.tensor_tensor(env.X[:, t, :], pw[:, t % 2, 0:D], env.X[:, t, :], ALU.add).then_inc(shared_done, 1)
                if c + 2 < BATCH:
                    shared(c + 2)


def experts1(nc, env, ins):
    KF = FF1 // P
    with ExitStack() as ctx:
        sb, ps, sem = scope(nc, ctx)
        W1, W2 = sb("W1e", [P, KD, E1, 2 * FF1]), sb("W2e", [P, KF, E1, D])
        B1 = sb("B1e", [P, E1, 2 * FF1])
        DEEP = 4
        XS, XST = sb("XS1", [P, DEEP, D]), sb("XST1", [P, 2, KD, P])
        HB, GE, A = sb("HB1", [P, 2, 2 * FF1]), sb("GE1e", [P, 2, FF1]), sb("A1", [P, 2, FF1])
        AT, YS = sb("AT1e", [P, 2, KF, P]), sb("YS1", [P, DEEP, D])
        TP, H = ps("TP1", [P, 2, SEQ]), ps("H1", [P, 2, SEQ])
        TA, Y = ps("TA1", [P, 2, SEQ]), ps("Y1", [P, 2, SEQ])
        xs_loaded = [sem(f"xs_loaded{i}e1") for i in range(DEEP)]
        y_stored = [sem(f"y_stored{i}e1") for i in range(DEEP)]
        (w_loaded, folded, xt_ready, xst_done, h_ready, hb_done, ge_done, a_done, at_ready, at_done, y_ready,
         y_done) = (sem(n + "e1") for n in (
             "w_loaded", "folded", "xt_ready", "xst_done", "h_ready", "hb_done", "ge_done", "a_done", "at_ready",
             "at_done", "y_ready", "y_done"))
        block = ctx.enter_context(nc.Block())
        n_weights = 1 + KD + KF
        HEAD = 4
        LOOPS = (TILES1 - HEAD) // DEEP

        def steps(eng, step):
            for c in range(HEAD):
                step(0, c)
            with eng.Fori(1, 1 + LOOPS) as r:
                for c in range(DEEP):
                    step(r, c)
            for j in range(HEAD + DEEP * LOOPS, TILES1):
                step(j // DEEP, j % DEEP)

        xs_tiles = env.xs1[:, :].rearrange("(j p) d -> j p d", p=P)
        ys_tiles = env.ys1[:, :].rearrange("(j p) d -> j p d", p=P)

        @block.sync
        def _(sp):
            sp.dma_start(B1[:, :, :], ins["fc1_b"].partition_broadcast(P)).then_inc(w_loaded, 16)
            for k in range(KD):
                sp.dma_start(W1[:, k, :, :], ins["fc1T"].rearrange("e (k p) f -> k p e f", p=P)[k]).then_inc(w_loaded, 16)
            for k in range(KF):
                sp.dma_start(W2[:, k, :, :], ins["fc2T"].rearrange("e (k p) d -> k p e d", p=P)[k]).then_inc(w_loaded, 16)

            def step(r, c):
                j = r * DEEP + c
                if not (isinstance(r, int) and j < DEEP):
                    sp.wait_ge(xt_ready, j - DEEP + 1)
                sp.dma_start(XS[:, c, :], xs_tiles[j]).then_inc(xs_loaded[c], 16)

            steps(sp, step)

        @block.gpsimd
        def _(pool):
            pool.wait_ge(w_loaded, 16 * n_weights)
            for k in range(KF):
                for e in range(E1):
                    ins_ = pool.tensor_scalar(W2[:, k, e, :], W2[:, k, e, :], env.mult[:, e, k:k + 1], None, ALU.mult)
            ins_.then_inc(folded, 1)

            def step(r, c):
                j = r * DEEP + c
                pool.wait_ge(y_done, j + 1)
                pool.dma_start(ys_tiles[j], YS[:, c, :]).then_inc(y_stored[c], 16)

            steps(pool, step)
            for c in range(DEEP):
                pool.wait_ge(y_stored[c], 16 * ((TILES1 - c + DEEP - 1) // DEEP))

        @block.tensor
        def _(pe):
            def turn(r, c):
                j = r * DEEP + c
                pe.wait_ge(xs_loaded[c % DEEP], 16 * (r + c // DEEP + 1))
                wait(pe, xst_done, j - 1)
                for k in range(KD):
                    m = pe.transpose(TP[:, c % 2, k * P:(k + 1) * P], XS[:, c % DEEP, k * P:(k + 1) * P], env.ident[:, :])
                m.then_inc(xt_ready, 1)

            def first(r, c):
                j = r * DEEP + c
                e = pe.value_load(env.expert[0:1, bass.ds(j, 1)], min_val=0, max_val=E1 - 1)
                pe.wait_ge(xst_done, j + 1)
                wait(pe, hb_done, j - 1)
                for k in range(KD):
                    m = pe.matmul(H[:, c % 2, :], XST[:, c % 2, k, :], W1[:, k, bass.ds(e, 1), :],
                                  start=(k == 0), stop=(k == KD - 1))
                m.then_inc(h_ready, 1)

            def turn_back(r, c):
                j = r * DEEP + c
                pe.wait_ge(a_done, j + 1)
                wait(pe, at_done, j - 1)
                for k in range(KF):
                    m = pe.transpose(TA[:, c % 2, k * P:(k + 1) * P], A[:, c % 2, k * P:(k + 1) * P], env.ident[:, :])
                m.then_inc(at_ready, 1)

            def second(r, c):
                j = r * DEEP + c
                e = pe.value_load(env.expert[0:1, bass.ds(j, 1)], min_val=0, max_val=E1 - 1)
                pe.wait_ge(at_done, j + 1)
                wait(pe, y_done, j - 1)
                for k in range(KF):
                    m = pe.matmul(Y[:, c % 2, 0:D], AT[:, c % 2, k, :], W2[:, k, bass.ds(e, 1), :],
                                  start=(k == 0), stop=(k == KF - 1))
                m.then_inc(y_ready, 1)

            turn(0, 0)
            pe.wait_ge(w_loaded, 16 * n_weights)
            pe.wait_ge(folded, 1)

            def step(r, c):
                j = r * DEEP + c
                static = isinstance(r, int)
                if not (static and j + 1 >= TILES1):
                    turn(r, c + 1)
                first(r, c)
                if not (static and j < 1):
                    turn_back(r, c - 1)
                if not (static and j < 2):
                    second(r, c - 2)

            steps(pe, step)
            r, c = divmod(TILES1 - 1, DEEP)
            turn_back(r, c)
            second(r, c - 1)
            second(r, c)

        @block.scalar
        def _(act):
            def turn(r, c):
                j = r * DEEP + c
                act.wait_ge(xt_ready, j + 1)
                wait(act, h_ready, j - 1)
                act.copy(XST[:, c % 2, :, :], TP[:, c % 2, 0:D].rearrange("p (k t) -> p k t", k=KD)).then_inc(xst_done, 1)

            def turn_back(r, c):
                j = r * DEEP + c
                act.wait_ge(at_ready, j + 1)
                wait(act, y_ready, j - 1)
                act.copy(AT[:, c % 2, :, :], TA[:, c % 2, 0:FF1].rearrange("p (k t) -> p k t", k=KF)).then_inc(at_done, 1)

            turn(0, 0)

            def step(r, c):
                j = r * DEEP + c
                static = isinstance(r, int)
                if not (static and j + 1 >= TILES1):
                    turn(r, c + 1)
                act.wait_ge(hb_done, j + 1)
                wait(act, a_done, j - 1)
                act.activation(GE[:, c % 2, :], HB[:, c % 2, FF1:2 * FF1], ACT.Gelu).then_inc(ge_done, 1)
                if not (static and j < 1):
                    turn_back(r, c - 1)

            steps(act, step)
            turn_back(*divmod(TILES1 - 1, DEEP))

        @block.vector
        def _(dve):
            dve.wait_ge(w_loaded, 16 * n_weights)

            def bias(r, c):
                j = r * DEEP + c
                e = dve.value_load(env.expert[0:1, bass.ds(j, 1)], min_val=0, max_val=E1 - 1)
                dve.wait_ge(h_ready, j + 1)
                wait(dve, a_done, j - 1)
                dve.tensor_tensor(HB[:, c % 2, :], H[:, c % 2, :], B1[:, bass.ds(e, 1), :].squeeze(1), ALU.add).then_inc(hb_done, 1)

            def gated(r, c):
                j = r * DEEP + c
                dve.wait_ge(ge_done, j + 1)
                wait(dve, at_ready, j - 1)
                dve.tensor_tensor(A[:, c % 2, :], HB[:, c % 2, 0:FF1], GE[:, c % 2, :], ALU.mult).then_inc(a_done, 1)

            def keep(r, c):
                j = r * DEEP + c
                dve.wait_ge(y_ready, j + 1)
                if not (isinstance(r, int) and j < DEEP):
                    dve.wait_ge(y_stored[c % DEEP], 16 * (r + c // DEEP))
                dve.tensor_copy(YS[:, c % DEEP, :], Y[:, c % 2, 0:D]).then_inc(y_done, 1)

            def step(r, c):
                j = r * DEEP + c
                bias(r, c)
                gated(r, c)
                if not (isinstance(r, int) and j < 2):
                    keep(r, c - 2)

            steps(dve, step)
            for j in range(TILES1 - 2, TILES1):
                keep(*divmod(j, DEEP))


def recycle(nc):
    used = sorted(s if isinstance(s, int) else s.num for s in nc.released_uncleared_semaphores)
    with nc.Block() as block:
        @block.gpsimd
        def _(pool):
            first = 0
            for i in range(1, len(used) + 1):
                if i == len(used) or used[i] != used[i - 1] + 1:
                    pool.sem_clear(range(used[first], used[i - 1] + 1))
                    first = i


class Layer:
    def __init__(self, name, heads, hd, scale):
        self.name, self.heads, self.hd, self.scale = name, heads, hd, scale
        self.gpb = heads // GH
        self.groups = BATCH * self.gpb
        self.halves = heads * HP // P


def program(nc, ins, out):
    lay0 = Layer("0", 8, 4, (D / 8) ** -0.5)
    lay1 = Layer("1", 16, 16, 16 ** -0.5)
    env = Work()
    with ExitStack() as ctx:
        sb, ps, sem = scope(nc, ctx)
        env.X = sb("X", [P, NT, D])
        env.ident, env.swap, env.ones, env.before = (sb(n, [P, P]) for n in ("ident", "swap", "ones", "before"))
        env.earlier, env.iota = sb("earlier", [P, E1, E1]), sb("iota", [P, TILES1])
        env.slot0, env.wt0 = sb("slot0", [P, K0, NT], U32), sb("wt0", [P, K0, NT])
        env.slot1, env.wt1 = sb("slot1", [P, K1, NT], U32), sb("wt1", [P, K1, NT])
        env.eps = sb("eps", [P, 1])
        env.expert = sb("expert", [1, TILES1], I32)
        env.mult = sb("mult", [P, E1, FF1 // P])

        def dram(name, shape, dt=F32):
            return nc.dram_tensor(name, shape, dt, kind="Internal").ap()

        env.xs0, env.ys0 = dram("xs0", [E0 * CAP0, D]), dram("ys0", [E0 * CAP0, D])
        env.xs1, env.ys1 = dram("xs1", [TILES1 * P, D]), dram("ys1", [TILES1 * P, D])
        setup(nc, env, ins)
        for lay in (lay0, lay1):
            env.scr = {w: dram(f"scr{w}{lay.name}", [3, lay.groups, GH * HP, SEQ], BF16) for w in "qk"}
            with ExitStack() as att:
                asb, _, _ = scope(nc, att)
                env.ON = asb(f"ON{lay.name}", [P, lay.groups, SEQ])
                with ExitStack() as vals:
                    vsb, _, _ = scope(nc, vals)
                    env.VA = vsb(f"VA{lay.name}", [P, lay.groups, TPB, GH * VW])
                    project(nc, env, ins, lay)
                    attend(nc, env, lay)
                (route0 if lay is lay0 else route1)(nc, env, ins, lay)
            if lay is lay0:
                experts0(nc, env, ins)
                combine(nc, env, "0", K0, env.ys0, env.slot0, env.wt0)
                recycle(nc)
            else:
                experts1(nc, env, ins)
                combine(nc, env, "1", K1, env.ys1, env.slot1, env.wt1, out)


def kernel(**a):
    import numpy as np
    import concourse.bacc as bacc
    from concourse.bass_utils import run_bass_kernel_spmd

    a = {k: np.asarray(v) for k, v in a.items()}
    kv_w = a["L1_xattn_Wkv"].reshape(D, D, 2)
    kv_b = a["L1_xattn_bkv"].reshape(D, 2)
    arrays = {
        "x": a["x"].reshape(TOK, D), "ctxT": a["ctx_1024"].reshape(TOK, D).T,
        "Wq0": a["L0_xattn_Wq"], "bq0": a["L0_xattn_bq"], "Wk0": a["L0_xattn_Wk"], "bk0": a["L0_xattn_bk"],
        "Wv0": a["L0_xattn_Wv"], "bv0": a["L0_xattn_bv"], "Wo0": a["L0_xattn_Wo"], "bo0": a["L0_xattn_bo"],
        "gamma": a["L0_ffn_ln_gamma"], "beta": a["L0_ffn_ln_beta"], "WrT": a["L0_ffn_Wr"].T,
        "W12T": a["L0_ffn_W12"].transpose(0, 2, 1), "W3T": a["L0_ffn_W3"].transpose(0, 2, 1),
        "Wq1": a["L1_xattn_Wq"], "bq1": a["L1_xattn_bq"], "Wk1": kv_w[:, :, 0], "bk1": kv_b[:, 0],
        "Wv1": kv_w[:, :, 1], "bv1": kv_b[:, 1], "Wo1": a["L1_xattn_Wout"], "bo1": a["L1_xattn_bout"],
        "gateT": a["L1_ffn_gate_w"].T, "fc1T": a["L1_ffn_fc1_w"].transpose(0, 2, 1), "fc1_b": a["L1_ffn_fc1_b"],
        "mult": a["L1_ffn_geglu_mult"], "fc2T": a["L1_ffn_fc2_w"].transpose(0, 2, 1), "fc2_b": a["L1_ffn_fc2_b"],
        "s_fc1T": a["L1_ffn_s_fc1_w"].T, "s_fc1_b": a["L1_ffn_s_fc1_b"], "s_mult": a["L1_ffn_s_geglu_mult"],
        "s_fc2T": a["L1_ffn_s_fc2_w"].T, "s_fc2_b": a["L1_ffn_s_fc2_b"],
    }
    nc = bacc.Bacc("TRN2", target_bir_lowering=False, num_devices=1)
    ins, feeds = {}, {}
    for name, v in arrays.items():
        v = np.ascontiguousarray(v)
        feeds[f"in_{name}"] = v
        ins[name] = nc.dram_tensor(f"in_{name}", v.shape, mybir.dt.from_np(v.dtype), kind="ExternalInput").ap()
    out = nc.dram_tensor("out", (TOK, D), F32, kind="ExternalOutput").ap()
    program(nc, ins, out)
    r = run_bass_kernel_spmd(nc, [feeds], core_ids=[0])
    return np.asarray(r.results[0]["out"]).reshape(BATCH, SEQ, D)
```

```python
from contextlib import ExitStack

import concourse.bass as bass
from concourse import mybir

F32 = mybir.dt.float32
F32R = mybir.dt.float32r
BF16 = mybir.dt.bfloat16
I32 = mybir.dt.int32
U32 = mybir.dt.uint32
ALU = mybir.AluOpType
ACT = mybir.ActivationFunctionType
AX = mybir.AxisListType

P = 128
BATCH, SEQ, D = 4, 512, 256
TOK = BATCH * SEQ
NT = TOK // P
TPB = SEQ // P
KD = D // P
EPS = 1e-5
HP = 16
GH = 4
VW = 32
Q_TERMS = (0, 0, 0, 1, 1, 2)
K_TERMS = (0, 1, 2, 0, 1, 0)
ROWS = HP * len(Q_TERMS)
SHIFT = 2
SLOTS = 4

E0, K0, FF0, CAP0 = 8, 2, 1024, 640
E1, K1, FF1, FFS = 15, 3, 256, 512
TILES1 = (TOK * K1 + E1 * (P - 1)) // P
FAR = 1 << 20


def wait(eng, sem, value):
    if not isinstance(value, int) or value > 0:
        eng.wait_ge(sem, value)


class Link:

    def __init__(self, eng, sem):
        self.eng, self.sem, self.count = eng, sem, 0

    def __call__(self, ins):
        self.count += 1
        ins.then_inc(self.sem, 1)
        self.eng.wait_ge(self.sem, self.count)


def scope(nc, ctx):
    def sb(name, shape, dt=F32):
        return ctx.enter_context(nc.sbuf_tensor(name, shape, dt))

    def ps(name, shape):
        return ctx.enter_context(nc.psum_tensor(name, shape, F32))

    def sem(name):
        return ctx.enter_context(nc.semaphore(name))

    return sb, ps, sem


class Norm:

    def __init__(self, sb, sem, name):
        self.stats, self.mv, self.dev = sb(f"st{name}", [P, NT, 6]), sb(f"mv{name}", [P, NT, 2]), sb(f"dev{name}", [P, NT])
        self.var_ready, self.dev_done, self.done = sem(f"var_ready{name}"), sem(f"dev_done{name}"), sem(f"done{name}")


def norm_stats(dve, link, ln, src, b):
    for t in range(b * TPB, (b + 1) * TPB):
        ins = dve.bn_stats(ln.stats[:, t, :], src[:, t, :])
    link(ins)
    for t in range(b * TPB, (b + 1) * TPB):
        ins = dve.bn_aggr(ln.mv[:, t, :], ln.stats[:, t, :])
    ins.then_inc(ln.var_ready, 1)


def norm_root(act, env, ln, b):
    act.wait_ge(ln.var_ready, b + 1)
    ts = slice(b * TPB, (b + 1) * TPB)
    act.activation(ln.dev[:, ts], ln.mv[:, ts, 1], ACT.Sqrt, bias=env.eps[:, :]).then_inc(ln.dev_done, 1)


def norm_apply(dve, link, ln, src, dst, b):
    dve.wait_ge(ln.dev_done, b + 1)
    ts = slice(b * TPB, (b + 1) * TPB)
    link(dve.reciprocal(ln.dev[:, ts], ln.dev[:, ts]))
    for t in range(b * TPB, (b + 1) * TPB):
        dve.tensor_scalar(dst[:, t, :], src[:, t, :], ln.mv[:, t, 0:1], ln.dev[:, t:t + 1],
                          ALU.subtract, ALU.mult).then_inc(ln.done, 1)


def setup(nc, env, ins):
    with ExitStack() as ctx:
        sb, ps, sem = scope(nc, ctx)
        const0 = sem("su_const0")
        block = ctx.enter_context(nc.Block())

        @block.sync
        def _(sp):
            sp.dma_start(env.X[:, :, :], ins["x"].rearrange("(t p) d -> p t d", p=P)).then_inc(env.x_loaded, 16)

        @block.gpsimd
        def _(pool):
            pool.memset(env.zeros[:, :], 0.0)
            for m in (env.ident, env.sums):
                pool.memset(m[:, :], 0.0)
            pool.memset(env.ones[:, :], 1.0)
            pool.memset(env.eps[:, :], EPS)
            pool.memset(env.before[:, :], 1.0)
            pool.memset(env.earlier[:, :, :], 1.0).then_inc(const0, 1)
            pool.wait_ge(const0, 1)
            pool.affine_select(out=env.ident[:, :], in_=env.ident[:, :], compare_op=ALU.not_equal, fill=1.0,
                               base=0, pattern=[[-1, P]], channel_multiplier=1)
            pool.affine_select(out=env.sums[:, :], in_=env.sums[:, :], compare_op=ALU.not_equal, fill=1.0,
                               base=-HP, pattern=[[-VW, GH]], channel_multiplier=1)
            pool.affine_select(out=env.before[:, :], in_=env.before[:, :], compare_op=ALU.is_gt, fill=0.0,
                               base=0, pattern=[[1, P]], channel_multiplier=-1)
            pool.affine_select(out=env.earlier[:, :, :], in_=env.earlier[:, :, :], compare_op=ALU.is_gt,
                               fill=0.0, base=0, pattern=[[1, E1], [-1, E1]], channel_multiplier=0)
            pool.iota(env.iota[:, :], [[1, TILES1]], base=0, channel_multiplier=0,
                      allow_small_or_imprecise_dtypes=True)


def fill_slots(pool, env):
    for dram, rows in ((env.xs0, E0 * CAP0), (env.xs1, TILES1 * P)):
        for r in range(0, rows, ZROWS):
            k = min(ZROWS, rows - r)
            pool.dma_start(dram[r:r + k, :].rearrange("(p a) d -> p (a d)", p=P),
                           env.zeros[:, 0:k * D // P]).then_inc(env.filled, 16)


ZROWS = 1024
FILLS = 16 * (-(-E0 * CAP0 // ZROWS) - (-TILES1 * P // ZROWS))


def project(nc, env, ins, lay, experts=None):
    L, hd, halves, gpb = lay.name, lay.hd, lay.halves, lay.gpb
    heads, width = lay.heads, lay.heads * HP
    with ExitStack() as ctx:
        sb, ps, sem = scope(nc, ctx)
        ctxT = sb(f"ctxT{L}", [P, KD, TOK])
        XN = sb(f"XN{L}", [P, NT, D])
        XNT = sb(f"XNT{L}", [P, KD, TOK])
        W = {w: sb(f"w{w}{L}", [P, KD, width]) for w in "qkv"}
        bias = {w: sb(f"b{w}{L}", [P, halves]) for w in "qk"}
        bv = sb(f"bv{L}", [1, width])
        parts = sb(f"parts{L}", [P, 2, 3, SEQ], BF16)
        rest = sb(f"rest{L}", [P, 2, SEQ])
        ln = Norm(sb, sem, f"p{L}")
        YG = sb(f"YG{L}p", [P, GDEEP, D])
        tp = ps(f"tp{L}", [P, 2, SEQ])
        pv = ps(f"pv{L}", [P, 2, SEQ])
        pq = ps(f"pq{L}", [P, 2, SEQ])
        w_zero, w_loaded, ctx_loaded = sem(f"w_zero{L}"), sem(f"w_loaded{L}"), sem(f"ctx_loaded{L}")
        chain, va_ones, added = sem(f"chain{L}"), sem(f"va_ones{L}"), sem(f"added{L}p")
        gathered = [sem(f"gathered{i}p{L}") for i in range(GDEEP if experts else 0)]
        tp_ready, xnt_done = sem(f"tp_ready{L}"), sem(f"xnt_done{L}")
        v_ready, v_done = sem(f"v_ready{L}"), sem(f"v_done{L}")
        qk_ready, p1_done, r1_done, p2_done, p3_done = (
            sem(f"{n}{L}") for n in ("qk_ready", "p1_done", "r1_done", "p2_done", "p3_done"))
        stored = [sem(f"stored{i}{L}") for i in range(2)]
        block = ctx.enter_context(nc.Block())

        units = [(w, half, b) for w in "kq" for b in range(BATCH) for half in range(halves)]
        n_k = halves * BATCH

        @block.sync
        def _(sp):
            sp.dma_start(ctxT[:, :, :], ins["ctxT"].rearrange("(k p) t -> p k t", p=P)).then_inc(ctx_loaded, 16)
            sp.wait_ge(w_zero, 1)
            for w in "qkv":
                src = ins[f"W{w}{L}"].rearrange("(k p) (h d) -> k p h d", p=P, d=hd)
                for k in range(KD):
                    dst = W[w][:, k, :].rearrange("p (h d) -> p h d", d=HP)[:, :, 0:hd]
                    sp.dma_start(dst, src[k]).then_inc(w_loaded, 16)
            for w in "qk":
                src = ins[f"b{w}{L}"]
                if hd == HP:
                    with nc.allow_non_contiguous_dma(reason="a small bias"):
                        sp.dma_start(bias[w][:, :], src.rearrange("(f p) -> p f", p=P)).then_inc(w_loaded, 16)
                else:
                    for h in range(heads):
                        with nc.allow_non_contiguous_dma(reason="a small bias"):
                            sp.dma_start(bias[w][HP * h:HP * h + hd, 0:1],
                                         src[hd * h:hd * h + hd].unsqueeze(1)).then_inc(w_loaded, 16)
            sp.dma_start(bv[0:1, :].rearrange("o (h d) -> o h d", d=HP)[:, :, 0:hd],
                         ins[f"bv{L}"].rearrange("(o h d) -> o h d", o=1, d=hd)).then_inc(w_loaded, 16)
            for i, (w, half, b) in enumerate(units):
                sp.wait_ge(p3_done, i + 1)
                first = b * gpb + half * (P // (GH * HP))
                dst = env.scr[w][:, first:first + 2, :, :].rearrange("s g r t -> (g r) s t")
                sp.dma_start(dst, parts[:, i % 2, :, :]).then_inc(stored[i % 2], 16)
            for i in range(2):
                sp.wait_ge(stored[i], 16 * len(units) // 2)

        weights = 16 * (3 * KD + 1 + (2 if hd == HP else 2 * heads))

        @block.gpsimd
        def _(pool):
            if hd != HP:
                for w in "qkv":
                    pool.memset(W[w][:, :, :], 0.0)
                for w in "qk":
                    pool.memset(bias[w][:, :], 0.0)
            pool.memset(bv[:, :], 0.0).then_inc(w_zero, 1)
            if experts:
                for n in range(NT * experts.K):
                    gather(pool, experts, YG, gathered, added, n)
            else:
                pool.wait_ge(ctx_loaded, 16)
                fill_slots(pool, env)

        @block.vector
        def _(dve):
            link = Link(dve, chain)
            dve.memset(env.VA[:, 0:lay.groups, :, :], 1.0).then_inc(va_ones, 1)

            def split(i):
                w, half, b = units[i]
                dve.wait_ge(p1_done, i + 1)
                if i >= 2:
                    dve.wait_ge(p2_done, i - 1)
                dve.scalar_tensor_tensor(rest[:, i % 2, :], pq[:, i % 2, :], bias[w][:, half:half + 1],
                                         parts[:, i % 2, 0, :], ALU.add, ALU.subtract).then_inc(r1_done, 1)
                dve.wait_ge(p2_done, i + 1)
                dve.tensor_tensor(parts[:, i % 2, 2, :], rest[:, i % 2, :], parts[:, i % 2, 1, :],
                                  ALU.subtract).then_inc(p3_done, 1)

            for b in range(BATCH):
                if experts:
                    for n in range(b * TPB * experts.K, (b + 1) * TPB * experts.K):
                        add_gathered(dve, env, experts, YG, gathered, added, n)
                elif b == 0:
                    dve.wait_ge(env.x_loaded, 16)
                for half in range(halves):
                    split(b * halves + half)
                if experts:
                    dve.wait_ge(added, (b + 1) * TPB * experts.K)
                norm_stats(dve, link, ln, env.X, b)
                if b:
                    norm_apply(dve, link, ln, env.X, XN, b - 1)
            norm_apply(dve, link, ln, env.X, XN, BATCH - 1)
            for i in range(n_k, len(units)):
                split(i)

        @block.scalar
        def _(act):
            act.wait_ge(va_ones, 1)
            for t in range(NT):
                act.wait_ge(v_ready, t + 1)
                b, kt = divmod(t, TPB)
                dst = env.VA[:, b * gpb:(b + 1) * gpb, kt, :].rearrange("p g (h c) -> p g h c", c=VW)
                src = pv[:, t % 2, 0:width].rearrange("p (g h c) -> p g h c", h=GH, c=HP)
                for g in range(gpb):
                    ins_ = act.copy(dst[:, g, :, 0:HP], src[:, g, :, :])
                ins_.then_inc(v_done, 1)

            def split(i):
                w, half, b = units[i]
                act.wait_ge(qk_ready, i + 1)
                if i >= 2:
                    act.wait_ge(stored[i % 2], 16 * (i // 2))
                act.activation(parts[:, i % 2, 0, :], pq[:, i % 2, :], ACT.Identity,
                               bias=bias[w][:, half:half + 1]).then_inc(p1_done, 1)
                act.wait_ge(r1_done, i + 1)
                act.copy(parts[:, i % 2, 1, :], rest[:, i % 2, :]).then_inc(p2_done, 1)

            def turned(b):
                for k in range(KD):
                    act.wait_ge(tp_ready, b * KD + k + 1)
                    act.copy(XNT[:, k, b * SEQ:(b + 1) * SEQ], tp[:, k, :]).then_inc(xnt_done, 1)

            for b in range(BATCH):
                for half in range(halves):
                    split(b * halves + half)
                norm_root(act, env, ln, b)
            turned(0)
            for b in range(BATCH):
                if b + 1 < BATCH:
                    turned(b + 1)
                for half in range(halves):
                    split(n_k + b * halves + half)

        @block.tensor
        def _(pe):
            pe.wait_ge(ctx_loaded, 16)
            pe.wait_ge(w_loaded, weights)
            for t in range(NT):
                if t >= 2:
                    pe.wait_ge(v_done, t - 1)
                for k in range(KD):
                    pe.matmul(pv[:, t % 2, 0:width], ctxT[:, k, t * P:(t + 1) * P], W["v"][:, k, :],
                              start=(k == 0), stop=False)
                pe.matmul(pv[:, t % 2, 0:width], env.ones[0:1, :], bv[:, :],
                          start=False, stop=True).then_inc(v_ready, 1)

            def unit(i):
                w, half, b = units[i]
                src = ctxT if w == "k" else XNT
                if i >= 2:
                    pe.wait_ge(r1_done, i - 1)
                for k in range(KD):
                    m = pe.matmul(pq[:, i % 2, :], W[w][:, k, half * P:(half + 1) * P],
                                  src[:, k, b * SEQ:(b + 1) * SEQ], start=(k == 0), stop=(k == KD - 1))
                m.then_inc(qk_ready, 1)

            def turn(b):
                pe.wait_ge(ln.done, (b + 1) * TPB)
                for k in range(KD):
                    if b:
                        pe.wait_ge(xnt_done, (b - 1) * KD + k + 1)
                    for j in range(TPB):
                        m = pe.transpose(tp[:, k, j * P:(j + 1) * P], XN[:, b * TPB + j, k * P:(k + 1) * P],
                                         env.ident[:, :])
                    m.then_inc(tp_ready, 1)

            for i in range(n_k):
                unit(i)
            turn(0)
            for b in range(BATCH):
                if b + 1 < BATCH:
                    turn(b + 1)
                pe.wait_ge(xnt_done, KD * (b + 1))
                for half in range(halves):
                    unit(n_k + b * halves + half)


def attend(nc, env, lay):
    L, NG = lay.name, lay.groups
    with ExitStack() as ctx:
        sb, ps, sem = scope(nc, ctx)
        QS = sb(f"QS{L}", [P, SLOTS, GH, SEQ], BF16)
        KS = sb(f"KS{L}", [P, SLOTS, GH, SEQ], BF16)
        PT = sb(f"PT{L}", [P, 2, GH, TPB, SEQ])
        VG = sb(f"VG{L}", [P, 2, TPB, P])
        M = sb(f"M{L}", [P, 2, GH * TPB])
        NM = sb(f"NM{L}", [GH * TPB, 2, SHIFT, P], BF16)
        OSB = sb(f"OSB{L}", [P, 2, SEQ])
        RC, RX = sb(f"RC{L}", [P, 2, TPB, GH]), sb(f"RX{L}", [P, TPB, P])
        S1 = ps(f"S1{L}", [P, 2, SEQ])
        S2 = ps(f"S2{L}", [P, 2, 2, SEQ])
        PV = ps(f"PV{L}", [P, SEQ])
        MISC = ps(f"MISC{L}", [P, SEQ])
        qk_loaded = [sem(f"qk_loaded{i}{L}") for i in range(SLOTS)]
        nm_loaded = [sem(f"nm_loaded{i}{L}") for i in range(SLOTS)]
        (shift_ones, s1_ready, max_done, mt_ready, nm1_done, nm_done, s2_ready, exp_done, vg_ready, pv_ready,
         osb_done, cols_ready, rc_done, rx_done, spread_ready, on_done) = (sem(n + L) for n in (
             "shift_ones", "s1_ready", "max_done", "mt_ready", "nm1_done", "nm_done", "s2_ready", "exp_done",
             "vg_ready", "pv_ready", "osb_done", "cols_ready", "rc_done", "rx_done", "spread_ready", "on_done"))
        loads = 16 * (len(Q_TERMS) + len(K_TERMS))
        block = ctx.enter_context(nc.Block())

        def steps(eng, step):
            for c in range(SLOTS + 1):
                step(0, c)
            if NG > 2 * SLOTS:
                with eng.Fori(1, NG // SLOTS - 1) as r:
                    for c in range(1, 1 + SLOTS):
                        step(r, c)
            for c in range(1, SLOTS):
                step(NG // SLOTS - 1, c)

        def last(r, c, ahead):
            return isinstance(r, int) and SLOTS * r + c + ahead >= NG

        @block.sync
        def _(sp):
            def load(r, c):
                n, slot = r * SLOTS + c, c % SLOTS
                for stack, terms, w in ((QS, Q_TERMS, "q"), (KS, K_TERMS, "k")):
                    for i, part in enumerate(terms):
                        sp.dma_start(stack[HP * i:HP * (i + 1), slot, :, :],
                                     env.scr[w][part, n, :, :].rearrange("(h d) t -> d h t", d=HP)
                                     ).then_inc(qk_loaded[slot], 16)

            def shift(r, c):
                n, slot = r * SLOTS + c, c % SLOTS
                sp.wait_ge(nm_done, n + 1)
                for i in range(SHIFT):
                    sp.dma_start(QS[ROWS + i:ROWS + i + 1, slot, :, :].rearrange("o h (q t) -> o (h q) t", t=P),
                                 NM[:, c % 2, i, :]).then_inc(nm_loaded[slot], 16)

            for c in range(SLOTS - 1):
                load(0, c)
            shift(0, 0)

            def step(r, c):
                if not last(r, c, 3):
                    wait(sp, s2_ready, 8 * (r * SLOTS + c))
                    load(r, c + 3)
                if not last(r, c, 1):
                    shift(r, c + 1)

            steps(sp, step)

        @block.gpsimd
        def _(pool):
            pool.memset(KS[ROWS:ROWS + 32, :, :, :], 1.0).then_inc(shift_ones, 1)
            pool.wait_ge(shift_ones, 1)

            def step(r, c):
                n = r * SLOTS + c
                wait(pool, pv_ready, n - 1)
                pool.tensor_copy(VG[:, c % 2, :, :], env.VA[:, n, :, :]).then_inc(vg_ready, 1)

            steps(pool, step)

        @block.tensor
        def _(pe):
            def maxima(r, c, h, q):
                n, slot = r * SLOTS + c, c % SLOTS
                if h == 0 and q == 0:
                    pe.wait_ge(qk_loaded[slot], loads * (r + c // SLOTS + 1))
                i = n * GH * TPB + h * TPB + q
                wait(pe, max_done, i - 1)
                pe.matmul(S1[:, q % 2, :], QS[0:ROWS, slot, h, q * P:(q + 1) * P], KS[0:ROWS, slot, h, :],
                          start=True, stop=True).then_inc(s1_ready, 1)

            def turn(r, c):
                n = r * SLOTS + c
                pe.wait_ge(max_done, GH * TPB * (n + 1))
                wait(pe, on_done, n - 3)
                pe.transpose(MISC[0:GH * TPB, 0:P], M[:, c % 2, :], env.ident[:, :]).then_inc(mt_ready, 1)

            def scores(r, c, h, u):
                n, slot = r * SLOTS + c, c % SLOTS
                if h == 0 and u == 0:
                    pe.wait_ge(nm_loaded[slot], 16 * SHIFT * (r + c // SLOTS + 1))
                i = n * 2 * GH + h * 2 + u
                wait(pe, exp_done, i - 1)
                for j in range(2):
                    kt = 2 * u + j
                    m = pe.matmul(S2[:, u, j, :], KS[0:ROWS + SHIFT, slot, h, kt * P:(kt + 1) * P],
                                  QS[0:ROWS + SHIFT, slot, h, :], start=True, stop=True)
                m.then_inc(s2_ready, 1)

            def values(r, c, kt):
                n = r * SLOTS + c
                if kt == 0:
                    pe.wait_ge(exp_done, 2 * GH * (n + 1))
                    pe.wait_ge(vg_ready, n + 1)
                    wait(pe, osb_done, n)
                for h in range(GH):
                    m = pe.matmul(PV[VW * h:VW * (h + 1), :], VG[:, c % 2, kt, VW * h:VW * (h + 1)],
                                  PT[:, c % 2, h, kt, :], start=(kt == 0), stop=(kt == TPB - 1))
                if kt == TPB - 1:
                    m.then_inc(pv_ready, 1)

            def columns(r, c, turned):
                n = r * SLOTS + c
                pe.wait_ge(osb_done, n + 1)
                pe.wait_ge(nm_done, turned)
                wait(pe, on_done, n)
                for q in range(TPB):
                    m = pe.matmul(MISC[:, q * GH:(q + 1) * GH], OSB[:, c % 2, q * P:(q + 1) * P], env.sums[:, :],
                                  start=True, stop=True)
                m.then_inc(cols_ready, 1)

            def spread(r, c):
                n = r * SLOTS + c
                pe.wait_ge(rx_done, n + 1)
                for q in range(TPB):
                    m = pe.transpose(MISC[:, q * P:(q + 1) * P], RX[:, q, :], env.ident[:, :])
                m.then_inc(spread_ready, 1)

            pe.wait_ge(shift_ones, 1)
            for c in range(2):
                for h in range(GH):
                    for q in range(TPB):
                        maxima(0, c, h, q)
            turn(0, 0)

            def step(r, c):
                n = r * SLOTS + c
                least = n if isinstance(r, int) else 2
                for h in range(GH):
                    for u in range(2):
                        if not last(r, c, 2):
                            maxima(r, c + 2, h, 2 * u)
                        scores(r, c, h, u)
                        if not last(r, c, 2):
                            maxima(r, c + 2, h, 2 * u + 1)
                        if u == 0 and h >= 1 and least >= 1:
                            values(r, c - 1, h - 1)
                    if h == 1 and not last(r, c, 1):
                        turn(r, c + 1)
                    if h == 2 and least >= 2:
                        columns(r, c - 2, NG if last(r, c, 2) else n + 2)
                if least >= 1:
                    values(r, c - 1, TPB - 1)
                if least >= 2:
                    spread(r, c - 2)

            steps(pe, step)
            r, c = divmod(NG - 1, SLOTS)
            for kt in range(TPB):
                values(r, c, kt)
            for m in range(NG - 2, NG):
                columns(*divmod(m, SLOTS), NG)
                spread(*divmod(m, SLOTS))

        @block.scalar
        def _(act):
            def negate(r, c):
                n = r * SLOTS + c
                act.wait_ge(mt_ready, n + 1)
                if not (isinstance(r, int) and n < 2):
                    act.wait_ge(nm_loaded[(c - 2) % SLOTS], 16 * SHIFT * (r + (c - 2) // SLOTS + 1))
                act.activation(NM[:, c % 2, 0, :], MISC[0:GH * TPB, 0:P], ACT.Copy, scale=-1.0).then_inc(nm1_done, 1)

            def keep(r, c):
                n = r * SLOTS + c
                act.wait_ge(pv_ready, n + 1)
                wait(act, on_done, n - 1)
                act.copy(OSB[:, c % 2, :], PV[:, :]).then_inc(osb_done, 1)

            def widen(r, c):
                n = r * SLOTS + c
                act.wait_ge(rc_done, n + 1)
                wait(act, spread_ready, n)
                act.copy(RX[:, :, :].rearrange("p q (h i) -> p q h i", i=VW),
                         RC[:, c % 2, :, :].unsqueeze(3).to_broadcast([P, TPB, GH, VW])).then_inc(rx_done, 1)

            negate(0, 0)

            def step(r, c):
                n = r * SLOTS + c
                least = n if isinstance(r, int) else 2
                wait(act, pv_ready, n - 1)
                for h in range(GH):
                    for u in range(2):
                        act.wait_ge(s2_ready, n * 2 * GH + h * 2 + u + 1)
                        act.activation(PT[:, c % 2, h, 2 * u:2 * u + 2, :], S2[:, u, :, :], ACT.Exp,
                                       scale=lay.scale).then_inc(exp_done, 1)
                        if h == 3 and u == 0 and least >= 2:
                            widen(r, c - 2)
                    if h == 0 and least >= 2:
                        keep(r, c - 2)
                    if h == 1 and not last(r, c, 1):
                        negate(r, c + 1)

            steps(act, step)
            for m in range(NG - 2, NG):
                keep(*divmod(m, SLOTS))
                widen(*divmod(m, SLOTS))

        @block.vector
        def _(dve):
            def maxima(r, c, h):
                n = r * SLOTS + c
                if h == 0:
                    wait(dve, mt_ready, n - 1)
                for q in range(TPB):
                    i = n * GH * TPB + h * TPB + q
                    dve.wait_ge(s1_ready, i + 1)
                    dve.tensor_reduce(M[:, c % 2, h * TPB + q:h * TPB + q + 1], S1[:, q % 2, :], AX.X,
                                      ALU.max).then_inc(max_done, 1)

            def negate(r, c):
                dve.wait_ge(nm1_done, r * SLOTS + c + 1)
                dve.scalar_tensor_tensor(NM[:, c % 2, 1, :], MISC[0:GH * TPB, 0:P], -1.0, NM[:, c % 2, 0, :],
                                         ALU.mult, ALU.subtract).then_inc(nm_done, 1)

            def invert(r, c):
                n = r * SLOTS + c
                dve.wait_ge(cols_ready, n + 1)
                wait(dve, rx_done, n - 1)
                dve.reciprocal(RC[:, c % 2, :, :], MISC[:, 0:TPB * GH].rearrange("p (q h) -> p q h", h=GH)).then_inc(rc_done, 1)

            def normalize(r, c):
                n = r * SLOTS + c
                dve.wait_ge(spread_ready, n + 1)
                dve.tensor_tensor(env.ON[:, n, :], OSB[:, c % 2, :], MISC[:, :], ALU.mult).then_inc(on_done, 1)

            for c in range(2):
                for h in range(GH):
                    maxima(0, c, h)
            negate(0, 0)

            def step(r, c):
                least = r * SLOTS + c if isinstance(r, int) else 3
                for h in range(GH):
                    if not last(r, c, 2):
                        maxima(r, c + 2, h)
                    if h == 0 and least >= 3:
                        normalize(r, c - 3)
                    if h == 1 and not last(r, c, 1):
                        negate(r, c + 1)
                    if h == 2 and least >= 2:
                        invert(r, c - 2)

            steps(dve, step)
            normalize(*divmod(NG - 3, SLOTS))
            for m in range(NG - 2, NG):
                invert(*divmod(m, SLOTS))
                normalize(*divmod(m, SLOTS))


def pick(dve, link, env, w, E, K, logits, cut):
    wide = [P, NT, E]
    if cut:
        link(dve.tensor_scalar(w.lg[:, :, :], logits, -1e4, 1e4, ALU.max, ALU.min))
    else:
        link(dve.tensor_copy(w.lg[:, :, :], logits))
    link(dve.tensor_reduce(w.red[:, :], w.lg[:, :, :], AX.X, ALU.max))
    link(dve.tensor_tensor(w.lg[:, :, :], w.lg[:, :, :], w.red[:, :].unsqueeze(2).to_broadcast(wide), ALU.subtract))


def softmax_top(dve, link, env, w, E, K, floor):
    wide = [P, NT, E]
    link(dve.tensor_reduce(w.red[:, :], w.ex[:, :, :], AX.X, ALU.add))
    if floor:
        link(dve.tensor_scalar(w.red[:, :], w.red[:, :], floor, None, ALU.add))
    link(dve.reciprocal(w.red2[:, :], w.red[:, :]))
    link(dve.tensor_tensor(w.pr[:, :, :], w.ex[:, :, :], w.red2[:, :].unsqueeze(2).to_broadcast(wide), ALU.mult))
    for t in range(NT):
        ins = dve.max(w.top[:, t, :], w.pr[:, t, :])
    link(ins)
    for t in range(NT):
        ins = dve.max_index(w.idx[:, t, :], w.top[:, t, :], w.pr[:, t, :])
    link(ins)
    link(dve.tensor_copy(w.idf[:, :, :], w.idx[:, :, 0:K].rearrange("p t k -> p k t")))
    for k in range(K):
        ins = dve.tensor_tensor(w.hot[:, k, :, :], env.iota[:, 0:E].unsqueeze(1).to_broadcast(wide),
                                w.idf[:, k, :].unsqueeze(2).to_broadcast(wide), ALU.is_equal)
    link(ins)
    link(dve.tensor_tensor(w.all[:, :, :], w.hot[:, 0, :, :], w.hot[:, 1, :, :], ALU.add))
    for k in range(2, K):
        link(dve.tensor_tensor(w.all[:, :, :], w.all[:, :, :], w.hot[:, k, :, :], ALU.add))
    dve.memset(w.run[:, 0, :], 0.0)
    src, dst, d = w.all, w.tmp, 1
    while d < NT:
        if 2 * d >= NT:
            dst = w.run[:, 1:NT + 1, :]
        dve.tensor_copy(dst[:, 0:d, :], src[:, 0:d, :])
        link(dve.tensor_tensor(dst[:, d:NT, :], src[:, d:NT, :], src[:, 0:NT - d, :], ALU.add))
        src, dst, d = dst, w.pr if dst is w.tmp else w.tmp, 2 * d


class Work:
    pass


def routing_buffers(sb, L, E, K):
    w = Work()
    w.lg, w.ex, w.pr, w.all, w.tmp = (sb(f"{n}{L}", [P, NT, E]) for n in ("lg", "ex", "pr", "all", "tmp"))
    w.red, w.red2 = sb(f"red{L}", [P, NT]), sb(f"red2{L}", [P, NT])
    w.top, w.idx = sb(f"top{L}", [P, NT, 8]), sb(f"idx{L}", [P, NT, 8], U32)
    w.idf, w.hot = sb(f"idf{L}", [P, K, NT]), sb(f"hot{L}", [P, K, NT, E])
    w.run = sb(f"run{L}", [P, NT + 1, E])
    w.rank, w.over = sb(f"rank{L}", [P, K, NT]), sb(f"over{L}", [P, K, NT])
    w.slot = sb(f"pos{L}", [P, K, NT])
    return w


def out_projection(pe, env, lay, WO, po, wo_loaded, wo_ready, x_done):
    pe.wait_ge(wo_loaded, 16 * (lay.gpb * GH + 1))
    for t in range(NT):
        b, q = divmod(t, TPB)
        if t >= 2:
            pe.wait_ge(x_done, t - 1)
        for g in range(lay.gpb):
            m = pe.matmul(po[:, t % 2, 0:D], env.ON[:, b * lay.gpb + g, q * P:(q + 1) * P], WO[:, g, :],
                          start=(g == 0), stop=(g == lay.gpb - 1))
        m.then_inc(wo_ready, 1)


def load_out_weights(sp, ins, lay, WO, wo_zero, wo_loaded):
    sp.wait_ge(wo_zero, 1)
    for g in range(lay.gpb):
        for h in range(GH):
            r = (g * GH + h) * lay.hd
            sp.dma_start(WO[VW * h:VW * h + lay.hd, g, :], ins[f"Wo{lay.name}"][r:r + lay.hd, :]).then_inc(wo_loaded, 16)
    sp.dma_start(WO[HP:HP + 1, 0, :], ins[f"bo{lay.name}"].unsqueeze(0)).then_inc(wo_loaded, 16)


def route0(nc, env, ins, lay):
    with ExitStack() as ctx:
        sb, ps, sem = scope(nc, ctx)
        WO = sb("WO0", [P, lay.gpb, D])
        Hn, XF, XFT = sb("H0", [P, NT, D]), sb("XF0", [P, NT, D]), sb("XFT0", [P, KD, TOK])
        gamma, beta, Wr = sb("gamma", [P, D]), sb("beta", [P, D]), sb("Wr", [P, KD, E0])
        gammaT, betaT = sb("gammaT", [P, KD]), sb("betaT", [P, KD])
        ln1, ln2 = Norm(sb, sem, "r0"), Norm(sb, sem, "f0")
        w = routing_buffers(sb, "0", E0, K0)
        scaled = sem("scaled0r")
        into = sb("into0", [P, K0, NT], U32)
        po, tp = ps("po0", [P, 2, SEQ]), ps("tp0r", [P, 2, SEQ])
        lgp, rk = ps("lgp0", [P, NT, E0]), ps("rk0", [P, NT, E0])
        wo_zero, wo_loaded, wo_ready, x_done, chain, xf_done, r_loaded, t_loaded = (sem(n + "0r") for n in (
            "wo_zero", "wo_loaded", "wo_ready", "x_done", "chain", "xf_done", "r_loaded", "t_loaded"))
        tp_ready, xft_done, lg_ready, lg_sub, ex_done, run_done, rk_ready, slots_done, scattered = (
            sem(n + "0r") for n in ("tp_ready", "xft_done", "lg_ready", "lg_sub", "ex_done", "run_done", "rk_ready",
                                    "slots_done", "scattered"))
        block = ctx.enter_context(nc.Block())

        @block.sync
        def _(sp):
            sp.dma_start(gamma[:, :], ins["gamma"].partition_broadcast(P)).then_inc(r_loaded, 16)
            sp.dma_start(beta[:, :], ins["beta"].partition_broadcast(P)).then_inc(r_loaded, 16)
            with nc.allow_non_contiguous_dma(reason="a small matrix"):
                sp.dma_start(Wr[:, :, :], ins["WrT"].rearrange("(k p) e -> p k e", p=P)).then_inc(t_loaded, 16)
                sp.dma_start(gammaT[:, :], ins["gamma"].rearrange("(k p) -> p k", p=P)).then_inc(t_loaded, 16)
                sp.dma_start(betaT[:, :], ins["beta"].rearrange("(k p) -> p k", p=P)).then_inc(t_loaded, 16)
            load_out_weights(sp, ins, lay, WO, wo_zero, wo_loaded)
            load_weights(sp, ins, env.EW, 0, 0)

        @block.gpsimd
        def _(pool):
            pool.memset(WO[:, :, :], 0.0).then_inc(wo_zero, 1)
            pool.wait_ge(r_loaded, 32)
            for t in range(NT):
                pool.wait_ge(ln2.done, t + 1)
                pool.tensor_tensor(Hn[:, t, :], XF[:, t, :], gamma[:, :], ALU.mult).then_inc(scaled, 1)
                pool.wait_ge(scaled, t + 1)
                pool.tensor_tensor(Hn[:, t, :], Hn[:, t, :], beta[:, :], ALU.add).then_inc(xf_done, 1)
            load_weights_low(pool, env.EW, 0, 0)
            pool.wait_ge(env.filled, FILLS)
            pool.wait_ge(xf_done, NT)
            pool.wait_ge(slots_done, 1)
            for t in range(NT):
                for k in range(K0):
                    pool.indirect_dma_start(
                        out=env.xs0[:, :], out_offset=bass.IndirectOffsetOnAxis(ap=into[:, k, t:t + 1], axis=0),
                        in_=Hn[:, t, :], in_offset=None, bounds_check=E0 * CAP0 - 1, oob_is_err=False,
                    ).then_inc(scattered, 16)
            pool.wait_ge(scattered, 16 * NT * K0)

        @block.tensor
        def _(pe):
            out_projection(pe, env, lay, WO, po, wo_loaded, wo_ready, x_done)

            def router(b):
                pe.wait_ge(xft_done, (b + 1) * KD)
                for t in range(b * TPB, (b + 1) * TPB):
                    for k in range(KD):
                        m = pe.matmul(lgp[:, t, :], XFT[:, k, t * P:(t + 1) * P], Wr[:, k, :],
                                      start=(k == 0), stop=(k == KD - 1))
                return m

            pe.wait_ge(t_loaded, 48)
            for b in range(BATCH):
                pe.wait_ge(ln2.done, (b + 1) * TPB)
                for n in range(b * KD, (b + 1) * KD):
                    if n >= 2:
                        pe.wait_ge(xft_done, n - 1)
                    for j in range(TPB):
                        m = pe.transpose(tp[:, n % 2, j * P:(j + 1) * P],
                                         XF[:, b * TPB + j, (n - b * KD) * P:(n - b * KD + 1) * P], env.ident[:, :])
                    m.then_inc(tp_ready, 1)
                if b:
                    router(b - 1)
            router(BATCH - 1).then_inc(lg_ready, 1)
            pe.wait_ge(run_done, 1)
            pe.matmul(rk[:, :, :], env.before[:, :], w.all[:, :, :], start=True, stop=False)
            pe.matmul(rk[:, :, :], env.ones[:, :], w.run[:, 0:NT, :], start=False, stop=True).then_inc(rk_ready, 1)

        @block.scalar
        def _(act):
            for b in range(BATCH + 1):
                if b < BATCH:
                    norm_root(act, env, ln1, b)
                if b:
                    norm_root(act, env, ln2, b - 1)
            act.wait_ge(t_loaded, 48)
            for n in range(BATCH * KD):
                t4, k = divmod(n, KD)
                act.wait_ge(tp_ready, n + 1)
                act.activation(XFT[:, k, t4 * SEQ:(t4 + 1) * SEQ], tp[:, n % 2, :], ACT.Identity,
                               bias=betaT[:, k:k + 1], scale=gammaT[:, k:k + 1]).then_inc(xft_done, 1)
            load_weights_high(act, env.EW, 0, 0, range(STAGES))
            act.wait_ge(lg_sub, 1)
            act.activation(w.ex[:, :, :], w.lg[:, :, :], ACT.Exp).then_inc(ex_done, 1)
            load_weights_high(act, env.EW, 0, 0, range(STAGES, PIECES))

        @block.vector
        def _(dve):
            link = Link(dve, chain)
            for b in range(BATCH + 2):
                if b < BATCH:
                    for t in range(b * TPB, (b + 1) * TPB):
                        dve.wait_ge(wo_ready, t + 1)
                        dve.tensor_tensor(env.X[:, t, :], po[:, t % 2, 0:D], env.X[:, t, :], ALU.add).then_inc(x_done, 1)
                    dve.wait_ge(x_done, (b + 1) * TPB)
                    norm_stats(dve, link, ln1, env.X, b)
                if 1 <= b <= BATCH:
                    norm_apply(dve, link, ln1, env.X, Hn, b - 1)
                    dve.wait_ge(ln1.done, b * TPB)
                    norm_stats(dve, link, ln2, Hn, b - 1)
                if b >= 2:
                    norm_apply(dve, link, ln2, Hn, XF, b - 2)
            dve.wait_ge(lg_ready, 1)
            pick(dve, link, env, w, E0, K0, lgp[:, :, :], True)
            dve.nop().then_inc(lg_sub, 1)
            dve.wait_ge(ex_done, 1)
            softmax_top(dve, link, env, w, E0, K0, 1e-12)
            dve.nop().then_inc(run_done, 1)
            dve.wait_ge(rk_ready, 1)
            for k in range(K0):
                link(dve.tensor_tensor(w.tmp[:, :, :], rk[:, :, :], w.hot[:, k, :, :], ALU.mult))
                link(dve.tensor_reduce(w.rank[:, k, :], w.tmp[:, :, :], AX.X, ALU.add))
            link(dve.tensor_scalar(w.over[:, :, :], w.rank[:, :, :], float(CAP0), None, ALU.is_ge))
            link(dve.scalar_tensor_tensor(w.slot[:, :, :], w.idf[:, :, :], float(CAP0), w.rank[:, :, :],
                                          ALU.mult, ALU.add))
            link(dve.scalar_tensor_tensor(into[:, :, :], w.over[:, :, :], float(FAR), w.slot[:, :, :],
                                          ALU.mult, ALU.add))
            dve.nop().then_inc(slots_done, 1)
            link(dve.tensor_scalar(w.rank[:, :, :], w.rank[:, :, :], float(CAP0 - 1), None, ALU.min))
            link(dve.scalar_tensor_tensor(env.slot0[:, :, :], w.idf[:, :, :], float(CAP0), w.rank[:, :, :],
                                          ALU.mult, ALU.add))
            link(dve.tensor_scalar(w.over[:, :, :], w.over[:, :, :], -1.0, 1.0, ALU.mult, ALU.add))
            link(dve.tensor_tensor(env.wt0[:, :, :], w.top[:, :, 0:K0].rearrange("p t k -> p k t"), w.over[:, :, :],
                                   ALU.mult))


WCH = 1024
PIECES = (KD * 2 * FF0 + FF0 // P * D) // WCH
STAGES = 3


class Weights:

    def __init__(self, sb, sem):
        FB = FF0 // P
        self.stage = sb("stage", [P, STAGES, WCH])
        self.w12 = [sb(f"w12{n}", [P, 2, KD, 2 * FF0], F32R) for n in "hl"]
        self.w3 = [sb(f"w3{n}", [P, 2, FB, D], F32R) for n in "hl"]
        self.staged = [sem(f"staged{i}") for i in range(STAGES)]
        self.high_done, self.low_done = sem("w_high_done"), sem("w_low_done")

    def part(self, low, s, c):
        n12 = KD * 2 * FF0 // WCH
        if c < n12:
            k, f = divmod(c * WCH, 2 * FF0)
            return self.w12[low][:, s, k, f:f + WCH]
        j = (c - n12) * WCH // D
        return self.w3[low][:, s, j:j + WCH // D, :].rearrange("p j d -> p (j d)")


def piece_at(e, c):
    return e * PIECES + c


def load_weights(sp, ins, ew, e, s):
    n12 = KD * 2 * FF0 // WCH
    for c in range(PIECES):
        if not isinstance(e, int) or piece_at(e, c) >= STAGES:
            sp.wait_ge(ew.low_done, piece_at(e, c) - STAGES + 1)
        if c < n12:
            k, f = divmod(c * WCH, 2 * FF0)
            src = ins["W12T"][e].rearrange("(k p) f -> k p f", p=P)[k, :, f:f + WCH]
            dst = ew.stage[:, c % STAGES, :]
        else:
            j = (c - n12) * WCH // D
            src = ins["W3T"][e].rearrange("(j p) d -> p j d", p=P)[:, j:j + WCH // D, :]
            dst = ew.stage[:, c % STAGES, :].rearrange("p (j d) -> p j d", d=D)
        sp.dma_start(dst, src).then_inc(ew.staged[c % STAGES], 16)


def load_weights_high(act, ew, e, s, pieces=range(PIECES)):
    for c in pieces:
        act.wait_ge(ew.staged[c % STAGES], 16 * (e * (PIECES // STAGES) + c // STAGES + 1))
        act.copy(ew.part(0, s, c), ew.stage[:, c % STAGES, :]).then_inc(ew.high_done, 1)


def load_weights_low(pool, ew, e, s):
    for c in range(PIECES):
        pool.wait_ge(ew.high_done, piece_at(e, c) + 1)
        pool.tensor_tensor(ew.part(1, s, c), ew.stage[:, c % STAGES, :], ew.part(0, s, c).bitcast(F32),
                           ALU.subtract).then_inc(ew.low_done, 1)


PASSES = ((0, 0), (0, 1), (1, 0))


def experts0(nc, env, ins):
    NTE = CAP0 // P
    FB = FF0 // P
    HALF = CAP0 // 2
    HFS = 4
    CH = 2 * FB
    ew = env.EW
    with ExitStack() as ctx:
        sb, ps, sem = scope(nc, ctx)
        rows = env.ON[:, :, :].rearrange("p g t -> p (g t)")
        XS = rows[:, 0:2 * NTE * D].rearrange("p (s n d) -> p s n d", s=2, n=NTE)
        YS = rows[:, 2 * NTE * D:3 * NTE * D].rearrange("p (n d) -> p n d", n=NTE)
        XST = [sb(f"XSTm0{n}", [P, KD, CAP0], F32R) for n in "hl"]
        HT = [sb(f"HTm0{n}", [P, FB, CAP0], F32R) for n in "hl"]
        SG, HF = sb("SGm0", [P, 2, HALF]), sb("HFm0", [P, HFS, HALF])
        G, U = ps("Gm0", [P, 2, SEQ]), ps("Um0", [P, 2, SEQ])
        TP, Y = ps("TPm0", [P, 2, SEQ]), ps("Ym0", [P, 2, SEQ])
        x_loaded = [sem(f"x_loaded{i}m0") for i in range(2)]
        tp_ready, xh_done, xst_done, gu_ready, sg_done, hf_done, hh_done, h_done, y_ready, y_done, y_stored = (
            sem(n + "m0") for n in ("tp_ready", "xh_done", "xst_done", "gu_ready", "sg_done", "hf_done", "hh_done",
                                    "h_done", "y_ready", "y_done", "y_stored"))
        block = ctx.enter_context(nc.Block())

        def pairs(eng, expert):
            for s in range(2):
                expert(0, s)
            with eng.Fori(1, E0 // 2 - 1) as r:
                for s in range(2):
                    expert(r, s)
            for s in range(2):
                expert(E0 // 2 - 1, s)

        def final(r, s):
            return isinstance(r, int) and 2 * r + s == E0 - 1

        @block.sync
        def _(sp):
            def load(r, s):
                sp.dma_start(XS[:, s, :, :], env.xs0[:, :].rearrange("(e n p) d -> e p n d", p=P, n=NTE)[2 * r + s]
                             ).then_inc(x_loaded[s], 16)

            for s in range(2):
                load(0, s)

            def expert(r, s):
                e = 2 * r + s
                if not final(r, s):
                    load_weights(sp, ins, ew, e + 1, 1 - s)
                if not (isinstance(r, int) and r == E0 // 2 - 1):
                    sp.wait_ge(tp_ready, NTE * (e + 1))
                    load(r + 1, s)
                sp.wait_ge(y_done, NTE * (e + 1))
                sp.dma_start(env.ys0[:, :].rearrange("(e n p) d -> e p n d", p=P, n=NTE)[e], YS[:, :, :]
                             ).then_inc(y_stored, 16)

            pairs(sp, expert)
            sp.wait_ge(y_stored, 16 * E0)

        @block.gpsimd
        def _(pool):
            def expert(r, s):
                if not final(r, s):
                    load_weights_low(pool, ew, 2 * r + s + 1, 1 - s)

            pairs(pool, expert)

        @block.tensor
        def _(pe):
            def turn(r, s, i):
                e = 2 * r + s
                if i == 0:
                    pe.wait_ge(x_loaded[s], 16 * (r + 1))
                wait(pe, xst_done, e * NTE + i - 1)
                for k in range(KD):
                    m = pe.transpose(TP[:, (s * NTE + i) % 2, k * P:(k + 1) * P],
                                     XS[:, s, i, k * P:(k + 1) * P], env.ident[:, :])
                m.then_inc(tp_ready, 1)

            for i in range(NTE):
                turn(0, 0, i)

            def expert(r, s):
                e = 2 * r + s
                pe.wait_ge(xst_done, NTE * (e + 1))
                pe.wait_ge(ew.low_done, PIECES * (e + 1))
                for c in range(CH):
                    half, j = divmod(c, FB)
                    wait(pe, hf_done, e * CH + c - 1)
                    for bank, f in ((G, j * P), (U, FF0 + j * P)):
                        for k in range(KD):
                            for a, b in PASSES:
                                m = pe.matmul(bank[:, c % 2, 0:HALF], ew.w12[a][:, s, k, f:f + P],
                                              XST[b][:, k, half * HALF:(half + 1) * HALF],
                                              start=(k == 0 and (a, b) == PASSES[0]),
                                              stop=(k == KD - 1 and (a, b) == PASSES[-1]))
                    m.then_inc(gu_ready, 1)
                for i in range(NTE):
                    if not final(r, s):
                        turn(r + s, 1 - s, i)
                    pe.wait_ge(h_done, CH * e + (FB if (i + 1) * P <= HALF else CH))
                    wait(pe, y_done, e * NTE + i - 1)
                    for j in range(FB):
                        for a, b in PASSES:
                            m = pe.matmul(Y[:, (s * NTE + i) % 2, 0:D], HT[a][:, j, i * P:(i + 1) * P],
                                          ew.w3[b][:, s, j, :], start=(j == 0 and (a, b) == PASSES[0]),
                                          stop=(j == FB - 1 and (a, b) == PASSES[-1]))
                    m.then_inc(y_ready, 1)

            pairs(pe, expert)

        @block.scalar
        def _(act):
            def turn(r, s):
                for i in range(NTE):
                    act.wait_ge(tp_ready, (2 * r + s) * NTE + i + 1)
                    act.copy(XST[0][:, :, i * P:(i + 1) * P],
                             TP[:, (s * NTE + i) % 2, 0:D].rearrange("p (k c) -> p k c", k=KD)).then_inc(xh_done, 1)

            turn(0, 0)

            def expert(r, s):
                e = 2 * r + s

                def high(c):
                    half, j = divmod(c, FB)
                    act.wait_ge(hf_done, e * CH + c + 1)
                    act.copy(HT[0][:, j, half * HALF:(half + 1) * HALF], HF[:, c % HFS, :]).then_inc(hh_done, 1)

                for c in range(CH):
                    act.wait_ge(gu_ready, e * CH + c + 1)
                    wait(act, hf_done, e * CH + c - 1)
                    act.activation(SG[:, c % 2, :], G[:, c % 2, 0:HALF], ACT.Silu).then_inc(sg_done, 1)
                    if c:
                        high(c - 1)
                    if c >= 2 and c % 2 == 0 and c // 2 <= PIECES and not final(r, s):
                        load_weights_high(act, ew, e + 1, 1 - s, [c // 2 - 1])
                high(CH - 1)
                if not final(r, s):
                    turn(r + s, 1 - s)

            pairs(act, expert)

        @block.vector
        def _(dve):
            def turn(r, s, i):
                dve.wait_ge(xh_done, (2 * r + s) * NTE + i + 1)
                at = slice(i * P, (i + 1) * P)
                dve.tensor_tensor(XST[1][:, :, at], TP[:, (s * NTE + i) % 2, 0:D].rearrange("p (k c) -> p k c", k=KD),
                                  XST[0][:, :, at].bitcast(F32), ALU.subtract).then_inc(xst_done, 1)

            for i in range(NTE):
                turn(0, 0, i)

            def expert(r, s):
                e = 2 * r + s

                def low(c):
                    half, j = divmod(c, FB)
                    at = slice(half * HALF, (half + 1) * HALF)
                    dve.wait_ge(hh_done, e * CH + c + 1)
                    dve.tensor_tensor(HT[1][:, j, at], HF[:, c % HFS, :], HT[0][:, j, at].bitcast(F32),
                                      ALU.subtract).then_inc(h_done, 1)

                for c in range(CH):
                    dve.wait_ge(sg_done, e * CH + c + 1)
                    wait(dve, h_done, e * CH + c - HFS + 1)
                    dve.tensor_tensor(HF[:, c % HFS, :], U[:, c % 2, 0:HALF], SG[:, c % 2, :],
                                      ALU.mult).then_inc(hf_done, 1)
                    if c:
                        low(c - 1)
                low(CH - 1)
                for i in range(NTE):
                    if not final(r, s):
                        turn(r + s, 1 - s, i)
                    dve.wait_ge(y_ready, e * NTE + i + 1)
                    if i == 0 and not (isinstance(r, int) and e == 0):
                        dve.wait_ge(y_stored, 16 * e)
                    dve.tensor_copy(YS[:, i, :], Y[:, (s * NTE + i) % 2, 0:D]).then_inc(y_done, 1)

            pairs(dve, expert)


GDEEP = 8


class Slots:

    def __init__(self, K, rows, slot, weight):
        self.K, self.rows, self.slot, self.weight = K, rows, slot, weight


def gather(pool, ex, YG, gathered, added, n):
    t, k = divmod(n, ex.K)
    if n >= GDEEP:
        pool.wait_ge(added, n - GDEEP + 1)
    pool.indirect_dma_start(
        out=YG[:, n % GDEEP, :], out_offset=None, in_=ex.rows[:, :],
        in_offset=bass.IndirectOffsetOnAxis(ap=ex.slot[:, k, t:t + 1], axis=0),
    ).then_inc(gathered[n % GDEEP], 16)


def add_gathered(dve, env, ex, YG, gathered, added, n):
    t, k = divmod(n, ex.K)
    dve.wait_ge(gathered[n % GDEEP], 16 * (n // GDEEP + 1))
    if k:
        dve.wait_ge(added, n)
    dve.scalar_tensor_tensor(env.X[:, t, :], YG[:, n % GDEEP, :], ex.weight[:, k, t:t + 1], env.X[:, t, :],
                             ALU.mult, ALU.add).then_inc(added, 1)


def combine(nc, env, ex, out):
    with ExitStack() as ctx:
        sb, ps, sem = scope(nc, ctx)
        YG = sb("YGc", [P, GDEEP, D])
        gathered = [sem(f"gathered{i}c") for i in range(GDEEP)]
        added, sent = sem("addedc"), sem("sentc")
        block = ctx.enter_context(nc.Block())

        @block.gpsimd
        def _(pool):
            for n in range(NT * ex.K):
                gather(pool, ex, YG, gathered, added, n)

        @block.vector
        def _(dve):
            for n in range(NT * ex.K):
                add_gathered(dve, env, ex, YG, gathered, added, n)

        @block.sync
        def _(sp):
            for t in range(0, NT, 2):
                sp.wait_ge(added, ex.K * (t + 2))
                sp.dma_start(out.rearrange("(t p) d -> p t d", p=P)[:, t:t + 2, :], env.X[:, t:t + 2, :]
                             ).then_inc(sent, 16)
            sp.wait_ge(sent, 16 * (NT // 2))


def route1(nc, env, ins, lay):
    JS = FFS // P
    with ExitStack() as ctx:
        sb, ps, sem = scope(nc, ctx)
        WO = sb("WO1", [P, lay.gpb, D])
        XF, XFT = sb("XF1", [P, NT, D]), sb("XFT1", [P, KD, TOK])
        gate, s1, s2 = sb("gate", [P, KD, E1]), sb("s1", [P, KD, 2 * FFS]), sb("s2", [P, JS, D])
        s1b, smul = sb("s1b", [P, 2 * JS]), sb("smul", [P, JS])
        s2b, f2b = sb("s2b", [1, D]), sb("f2b", [E1, D])
        ln1 = Norm(sb, sem, "r1")
        w = routing_buffers(sb, "1", E1, K1)
        comb, combT = sb("comb", [P, NT, E1]), sb("combT", [E1, TOK])
        fill, ntile, base, ends = sb("fill", [P, E1]), sb("ntile", [P, E1]), sb("base", [P, E1]), sb("ends", [P, E1])
        sq, many, upto = sb("sq", [P, E1, E1]), sb("many", [P, E1, NT]), sb("upto", [1, TILES1, E1])
        tile_e = sb("tile_e", [1, TILES1])
        GE, AT = sb("GE1", [P, 2, SEQ]), sb("AT1", [P, JS, SEQ])
        pw, pg = ps("pw1", [P, 2, SEQ]), ps("pg1", [P, 4, SEQ])
        lgp, rk = ps("lgp1", [P, NT, E1]), ps("rk1", [P, NT + 1, E1])
        wo_zero, wo_loaded, wo_ready, x_done, chain, xf_done, r_loaded, chain_p = (sem(n + "1r") for n in (
            "wo_zero", "wo_loaded", "wo_ready", "x_done", "chain", "xf_done", "r_loaded", "chain_p"))
        tp_ready, xft_done, lg_ready, lg_sub, ex_done, run_done, rk_ready, slots_done, scattered = (
            sem(n + "1r") for n in ("tp_ready", "xft_done", "lg_ready", "lg_sub", "ex_done", "run_done", "rk_ready",
                                    "slots_done", "scattered"))
        gs_ready, ge_done, at_done, comb_done, ct_ready, ct_done, ys_ready, shared_done, folded = (
            sem(n + "1r") for n in ("gs_ready", "ge_done", "at_done", "comb_done", "ct_ready", "ct_done", "ys_ready",
                                    "shared_done", "folded"))
        block = ctx.enter_context(nc.Block())
        n_small = 8

        @block.sync
        def _(sp):
            with nc.allow_non_contiguous_dma(reason="small matrices and vectors"):
                sp.dma_start(gate[:, :, :], ins["gateT"].rearrange("(k p) e -> p k e", p=P)).then_inc(r_loaded, 16)
                sp.dma_start(s1b[:, :], ins["s_fc1_b"].rearrange("(j p) -> p j", p=P)).then_inc(r_loaded, 16)
                sp.dma_start(smul[:, :], ins["s_mult"].rearrange("(j p) -> p j", p=P)).then_inc(r_loaded, 16)
                sp.dma_start(env.mult[:, :, :], ins["mult"].rearrange("e (k p) -> p e k", p=P)).then_inc(r_loaded, 16)
            sp.dma_start(s2b[:, :], ins["s_fc2_b"].unsqueeze(0)).then_inc(r_loaded, 16)
            sp.dma_start(f2b[:, :], ins["fc2_b"]).then_inc(r_loaded, 16)
            load_out_weights(sp, ins, lay, WO, wo_zero, wo_loaded)
            sp.dma_start(s1[:, :, :], ins["s_fc1T"].rearrange("(k p) f -> p k f", p=P)).then_inc(r_loaded, 16)
            sp.dma_start(s2[:, :, :], ins["s_fc2T"].rearrange("(j p) d -> p j d", p=P)).then_inc(r_loaded, 16)
            for k in range(KD):
                sp.dma_start(env.W1[:, k, :, :], ins["fc1T"].rearrange("e (k p) f -> k p e f", p=P)[k]).then_inc(env.w1_loaded, 16)
            sp.wait_ge(wo_ready, NT)
            for k in range(FF1 // P):
                sp.dma_start(env.W2[:, k, :, :], ins["fc2T"].rearrange("e (k p) d -> k p e d", p=P)[k]).then_inc(env.w2_loaded, 16)

        @block.gpsimd
        def _(pool):
            pool.memset(WO[:, :, :], 0.0).then_inc(wo_zero, 1)
            pool.wait_ge(r_loaded, 16 * n_small)
            for j in range(JS):
                pool.tensor_scalar(s2[:, j, :], s2[:, j, :], smul[:, j:j + 1], None, ALU.mult).then_inc(folded, 1)
            pool.wait_ge(slots_done, 1)
            for t in range(NT):
                for k in range(K1):
                    pool.indirect_dma_start(
                        out=env.xs1[:, :], out_offset=bass.IndirectOffsetOnAxis(ap=env.slot1[:, k, t:t + 1], axis=0),
                        in_=XF[:, t, :], in_offset=None).then_inc(scattered, 16)
            pool.wait_ge(scattered, 16 * NT * K1)

        @block.tensor
        def _(pe):
            out_projection(pe, env, lay, WO, pw, wo_loaded, wo_ready, x_done)

            def router(b):
                pe.wait_ge(xft_done, (b + 1) * KD)
                for t in range(b * TPB, (b + 1) * TPB):
                    for k in range(KD):
                        m = pe.matmul(lgp[:, t, :], XFT[:, k, t * P:(t + 1) * P], gate[:, k, :],
                                      start=(k == 0), stop=(k == KD - 1))
                return m

            pe.wait_ge(r_loaded, 16 * n_small)
            for b in range(BATCH):
                pe.wait_ge(ln1.done, (b + 1) * TPB)
                for n in range(b * KD, (b + 1) * KD):
                    if n >= 2:
                        pe.wait_ge(xft_done, n - 1)
                    for j in range(TPB):
                        m = pe.transpose(pg[:, n % 2, j * P:(j + 1) * P],
                                         XF[:, b * TPB + j, (n - b * KD) * P:(n - b * KD + 1) * P], env.ident[:, :])
                    m.then_inc(tp_ready, 1)
                if b:
                    router(b - 1)
            router(BATCH - 1).then_inc(lg_ready, 1)

            def shared_in(c):
                for j in range(JS):
                    i = c * JS + j
                    if i >= 2:
                        pe.wait_ge(at_done, i - 1)
                    for half in range(2):
                        for k in range(KD):
                            m = pe.matmul(pg[:, 2 * (i % 2) + half, :], s1[:, k, half * FFS + j * P:half * FFS + (j + 1) * P],
                                          XFT[:, k, c * SEQ:(c + 1) * SEQ], start=(k == 0), stop=(k == KD - 1))
                    m.then_inc(gs_ready, 1)

            def shared_out(c):
                pe.wait_ge(at_done, JS * (c + 1))
                pe.wait_ge(folded, JS)
                for q in range(TPB):
                    t = c * TPB + q
                    if t >= 2:
                        pe.wait_ge(shared_done, t - 1)
                    for j in range(JS):
                        pe.matmul(pw[:, t % 2, 0:D], AT[:, j, q * P:(q + 1) * P], s2[:, j, :],
                                  start=(j == 0), stop=False)
                    pe.matmul(pw[:, t % 2, 0:D], env.ones[0:1, :], s2b[:, :], start=False, stop=False)
                    pe.matmul(pw[:, t % 2, 0:D], combT[:, t * P:(t + 1) * P], f2b[:, :],
                              start=False, stop=True).then_inc(ys_ready, 1)

            shared_in(0)
            pe.wait_ge(run_done, 1)
            pe.matmul(rk[:, 0:NT, :], env.before[:, :], w.all[:, :, :], start=True, stop=False)
            pe.matmul(rk[:, 0:NT, :], env.ones[:, :], w.run[:, 0:NT, :], start=False, stop=True)
            pe.matmul(rk[:, NT, :], env.ones[:, :], w.run[:, NT, :], start=True, stop=True).then_inc(rk_ready, 1)
            for t4 in range(TPB):
                if t4 >= 2:
                    pe.wait_ge(ct_done, t4 - 1)
                if t4 == 0:
                    pe.wait_ge(comb_done, 1)
                for j in range(TPB):
                    m = pe.transpose(pw[0:E1, t4 % 2, j * P:(j + 1) * P], comb[:, t4 * TPB + j, :], env.ident[:, :])
                m.then_inc(ct_ready, 1)
            pe.wait_ge(ct_done, TPB)
            for c in range(BATCH):
                shared_out(c)
                if c + 1 < BATCH:
                    shared_in(c + 1)

        @block.scalar
        def _(act):
            for b in range(BATCH):
                norm_root(act, env, ln1, b)
            for n in range(TPB * KD):
                t4, k = divmod(n, KD)
                act.wait_ge(tp_ready, n + 1)
                act.copy(XFT[:, k, t4 * SEQ:(t4 + 1) * SEQ], pg[:, n % 2, :]).then_inc(xft_done, 1)
            act.wait_ge(lg_sub, 1)
            act.activation(w.ex[:, :, :], w.lg[:, :, :], ACT.Exp).then_inc(ex_done, 1)
            act.wait_ge(r_loaded, 16 * n_small)

            def gelu(c):
                for j in range(JS):
                    i = c * JS + j
                    act.wait_ge(gs_ready, i + 1)
                    if i >= 2:
                        act.wait_ge(at_done, i - 1)
                    act.activation(GE[:, i % 2, :], pg[:, 2 * (i % 2) + 1, :], ACT.Gelu,
                                   bias=s1b[:, JS + j:JS + j + 1]).then_inc(ge_done, 1)

            gelu(0)
            act.wait_ge(env.w2_loaded, 16 * FF1 // P)
            for k in range(FF1 // P):
                for e in range(E1):
                    act.activation(env.W2[:, k, e, :], env.W2[:, k, e, :], ACT.Copy, scale=env.mult[:, e, k:k + 1])
            for t4 in range(TPB):
                act.wait_ge(ct_ready, t4 + 1)
                act.copy(combT[:, t4 * SEQ:(t4 + 1) * SEQ], pw[0:E1, t4 % 2, :]).then_inc(ct_done, 1)
            for c in range(1, BATCH):
                gelu(c)

        @block.vector
        def _(dve):
            link = Link(dve, chain)
            for b in range(BATCH + 1):
                if b < BATCH:
                    for t in range(b * TPB, (b + 1) * TPB):
                        dve.wait_ge(wo_ready, t + 1)
                        dve.tensor_tensor(env.X[:, t, :], pw[:, t % 2, 0:D], env.X[:, t, :], ALU.add).then_inc(x_done, 1)
                    dve.wait_ge(x_done, (b + 1) * TPB)
                    norm_stats(dve, link, ln1, env.X, b)
                if b:
                    norm_apply(dve, link, ln1, env.X, XF, b - 1)
            dve.wait_ge(lg_ready, 1)
            pick(dve, link, env, w, E1, K1, lgp[:, :, :], False)
            dve.nop().then_inc(lg_sub, 1)
            dve.wait_ge(ex_done, 1)
            softmax_top(dve, link, env, w, E1, K1, 0.0)
            dve.nop().then_inc(run_done, 1)

            def shared(c):
                for j in range(JS):
                    i = c * JS + j
                    dve.wait_ge(ge_done, i + 1)
                    if c >= 1:
                        dve.wait_ge(ys_ready, TPB * c)
                    dve.scalar_tensor_tensor(AT[:, j, :], pg[:, 2 * (i % 2), :], s1b[:, j:j + 1],
                                             GE[:, i % 2, :], ALU.add, ALU.mult).then_inc(at_done, 1)

            shared(0)
            dve.wait_ge(rk_ready, 1)
            link(dve.tensor_copy(fill[:, :], rk[:, NT, :]))
            link(dve.tensor_scalar(w.red[:, :], env.iota[:, 0:NT], float(P), None, ALU.mult))
            link(dve.tensor_tensor(many[:, :, :], fill[:, :].unsqueeze(2).to_broadcast([P, E1, NT]),
                                   w.red[:, :].unsqueeze(1).to_broadcast([P, E1, NT]), ALU.is_gt))
            link(dve.tensor_reduce(ntile[:, :], many[:, :, :], AX.X, ALU.add))
            link(dve.tensor_tensor(sq[:, :, :], ntile[:, :].unsqueeze(1).to_broadcast([P, E1, E1]),
                                   env.earlier[:, :, :], ALU.mult))
            link(dve.tensor_reduce(base[:, :], sq[:, :, :], AX.X, ALU.add))
            link(dve.tensor_tensor(ends[:, :], base[:, :], ntile[:, :], ALU.add))
            link(dve.tensor_tensor(upto[:, :, :], env.iota[0:1, :].unsqueeze(2).to_broadcast([1, TILES1, E1]),
                                   ends[0:1, :].unsqueeze(1).to_broadcast([1, TILES1, E1]), ALU.is_ge))
            link(dve.tensor_reduce(tile_e[:, :], upto[:, :, :], AX.X, ALU.add))
            link(dve.tensor_scalar(env.expert[:, :], tile_e[:, :], float(E1 - 1), None, ALU.min))
            link(dve.scalar_tensor_tensor(
                w.lg[:, :, :], base[:, :].unsqueeze(1).to_broadcast([P, NT, E1]), float(P), rk[:, 0:NT, :],
                ALU.mult, ALU.add))
            for k in range(K1):
                link(dve.tensor_tensor(w.tmp[:, :, :], w.lg[:, :, :], w.hot[:, k, :, :], ALU.mult))
                link(dve.tensor_reduce(w.slot[:, k, :], w.tmp[:, :, :], AX.X, ALU.add))
            link(dve.tensor_copy(env.slot1[:, :, :], w.slot[:, :, :]))
            dve.nop().then_inc(slots_done, 1)
            link(dve.tensor_reduce(w.red[:, :], w.top[:, :, 0:K1], AX.X, ALU.add))
            link(dve.tensor_scalar(w.red[:, :], w.red[:, :], 1e-20, None, ALU.add))
            link(dve.reciprocal(w.red2[:, :], w.red[:, :]))
            for k in range(K1):
                link(dve.tensor_tensor(env.wt1[:, k, :], w.top[:, :, k], w.red2[:, :], ALU.mult))
                wide = env.wt1[:, k, :].unsqueeze(2).to_broadcast([P, NT, E1])
                if k == 0:
                    link(dve.tensor_tensor(comb[:, :, :], w.hot[:, k, :, :], wide, ALU.mult))
                else:
                    link(dve.tensor_tensor(w.tmp[:, :, :], w.hot[:, k, :, :], wide, ALU.mult))
                    link(dve.tensor_tensor(comb[:, :, :], comb[:, :, :], w.tmp[:, :, :], ALU.add))
            dve.nop().then_inc(comb_done, 1)
            for c in range(BATCH):
                if c:
                    shared(c)
                for q in range(TPB):
                    t = c * TPB + q
                    dve.wait_ge(ys_ready, t + 1)
                    dve.tensor_tensor(env.X[:, t, :], pw[:, t % 2, 0:D], env.X[:, t, :], ALU.add).then_inc(shared_done, 1)


def experts1(nc, env, ins):
    KF = FF1 // P
    with ExitStack() as ctx:
        sb, ps, sem = scope(nc, ctx)
        W1, W2 = env.W1, env.W2
        B1 = sb("B1e", [P, E1, 2 * FF1])
        DEEP = 4
        XS, XST = sb("XS1", [P, DEEP, D]), sb("XST1", [P, 2, KD, P])
        HB, GE, A = sb("HB1", [P, 2, 2 * FF1]), sb("GE1e", [P, 2, FF1]), sb("A1", [P, 2, FF1])
        AT, YS = sb("AT1e", [P, 2, KF, P]), sb("YS1", [P, DEEP, D])
        TP, H = ps("TP1", [P, 2, SEQ]), ps("H1", [P, 2, SEQ])
        TA, Y = ps("TA1", [P, 2, SEQ]), ps("Y1", [P, 2, SEQ])
        xs_loaded = [sem(f"xs_loaded{i}e1") for i in range(DEEP)]
        y_stored = [sem(f"y_stored{i}e1") for i in range(DEEP)]
        (w_loaded, xt_ready, xst_done, h_ready, hb_done, ge_done, a_done, at_ready, at_done, y_ready,
         y_done) = (sem(n + "e1") for n in (
             "w_loaded", "xt_ready", "xst_done", "h_ready", "hb_done", "ge_done", "a_done", "at_ready",
             "at_done", "y_ready", "y_done"))
        block = ctx.enter_context(nc.Block())
        HEAD = 4
        LOOPS = (TILES1 - HEAD) // DEEP

        def steps(eng, step):
            for c in range(HEAD):
                step(0, c)
            with eng.Fori(1, 1 + LOOPS) as r:
                for c in range(DEEP):
                    step(r, c)
            for j in range(HEAD + DEEP * LOOPS, TILES1):
                step(j // DEEP, j % DEEP)

        xs_tiles = env.xs1[:, :].rearrange("(j p) d -> j p d", p=P)
        ys_tiles = env.ys1[:, :].rearrange("(j p) d -> j p d", p=P)

        @block.sync
        def _(sp):
            sp.dma_start(B1[:, :, :], ins["fc1_b"].partition_broadcast(P)).then_inc(w_loaded, 16)
            def step(r, c):
                j = r * DEEP + c
                if not (isinstance(r, int) and j < DEEP):
                    sp.wait_ge(xt_ready, j - DEEP + 1)
                sp.dma_start(XS[:, c, :], xs_tiles[j]).then_inc(xs_loaded[c], 16)

            steps(sp, step)

        @block.gpsimd
        def _(pool):
            def step(r, c):
                j = r * DEEP + c
                pool.wait_ge(y_done, j + 1)
                pool.dma_start(ys_tiles[j], YS[:, c, :]).then_inc(y_stored[c], 16)

            steps(pool, step)
            for c in range(DEEP):
                pool.wait_ge(y_stored[c], 16 * ((TILES1 - c + DEEP - 1) // DEEP))

        @block.tensor
        def _(pe):
            def turn(r, c):
                j = r * DEEP + c
                pe.wait_ge(xs_loaded[c % DEEP], 16 * (r + c // DEEP + 1))
                wait(pe, xst_done, j - 1)
                for k in range(KD):
                    m = pe.transpose(TP[:, c % 2, k * P:(k + 1) * P], XS[:, c % DEEP, k * P:(k + 1) * P], env.ident[:, :])
                m.then_inc(xt_ready, 1)

            def first(r, c):
                j = r * DEEP + c
                e = pe.value_load(env.expert[0:1, bass.ds(j, 1)], min_val=0, max_val=E1 - 1)
                pe.wait_ge(xst_done, j + 1)
                wait(pe, hb_done, j - 1)
                for k in range(KD):
                    m = pe.matmul(H[:, c % 2, :], XST[:, c % 2, k, :], W1[:, k, bass.ds(e, 1), :],
                                  start=(k == 0), stop=(k == KD - 1))
                m.then_inc(h_ready, 1)

            def turn_back(r, c):
                j = r * DEEP + c
                pe.wait_ge(a_done, j + 1)
                wait(pe, at_done, j - 1)
                for k in range(KF):
                    m = pe.transpose(TA[:, c % 2, k * P:(k + 1) * P], A[:, c % 2, k * P:(k + 1) * P], env.ident[:, :])
                m.then_inc(at_ready, 1)

            def second(r, c):
                j = r * DEEP + c
                e = pe.value_load(env.expert[0:1, bass.ds(j, 1)], min_val=0, max_val=E1 - 1)
                pe.wait_ge(at_done, j + 1)
                wait(pe, y_done, j - 1)
                for k in range(KF):
                    m = pe.matmul(Y[:, c % 2, 0:D], AT[:, c % 2, k, :], W2[:, k, bass.ds(e, 1), :],
                                  start=(k == 0), stop=(k == KF - 1))
                m.then_inc(y_ready, 1)

            turn(0, 0)
            pe.wait_ge(env.w1_loaded, 16 * KD)

            def step(r, c):
                j = r * DEEP + c
                static = isinstance(r, int)
                if not (static and j + 1 >= TILES1):
                    turn(r, c + 1)
                first(r, c)
                if not (static and j < 1):
                    turn_back(r, c - 1)
                if not (static and j < 2):
                    second(r, c - 2)

            steps(pe, step)
            r, c = divmod(TILES1 - 1, DEEP)
            turn_back(r, c)
            second(r, c - 1)
            second(r, c)

        @block.scalar
        def _(act):
            def turn(r, c):
                j = r * DEEP + c
                act.wait_ge(xt_ready, j + 1)
                wait(act, h_ready, j - 1)
                act.copy(XST[:, c % 2, :, :], TP[:, c % 2, 0:D].rearrange("p (k t) -> p k t", k=KD)).then_inc(xst_done, 1)

            def turn_back(r, c):
                j = r * DEEP + c
                act.wait_ge(at_ready, j + 1)
                wait(act, y_ready, j - 1)
                act.copy(AT[:, c % 2, :, :], TA[:, c % 2, 0:FF1].rearrange("p (k t) -> p k t", k=KF)).then_inc(at_done, 1)

            turn(0, 0)

            def step(r, c):
                j = r * DEEP + c
                static = isinstance(r, int)
                if not (static and j + 1 >= TILES1):
                    turn(r, c + 1)
                act.wait_ge(hb_done, j + 1)
                wait(act, a_done, j - 1)
                act.activation(GE[:, c % 2, :], HB[:, c % 2, FF1:2 * FF1], ACT.Gelu).then_inc(ge_done, 1)
                if not (static and j < 1):
                    turn_back(r, c - 1)

            steps(act, step)
            turn_back(*divmod(TILES1 - 1, DEEP))

        @block.vector
        def _(dve):
            dve.wait_ge(w_loaded, 16)

            def bias(r, c):
                j = r * DEEP + c
                e = dve.value_load(env.expert[0:1, bass.ds(j, 1)], min_val=0, max_val=E1 - 1)
                dve.wait_ge(h_ready, j + 1)
                wait(dve, a_done, j - 1)
                dve.tensor_tensor(HB[:, c % 2, :], H[:, c % 2, :], B1[:, bass.ds(e, 1), :].squeeze(1), ALU.add).then_inc(hb_done, 1)

            def gated(r, c):
                j = r * DEEP + c
                dve.wait_ge(ge_done, j + 1)
                wait(dve, at_ready, j - 1)
                dve.tensor_tensor(A[:, c % 2, :], HB[:, c % 2, 0:FF1], GE[:, c % 2, :], ALU.mult).then_inc(a_done, 1)

            def keep(r, c):
                j = r * DEEP + c
                dve.wait_ge(y_ready, j + 1)
                if not (isinstance(r, int) and j < DEEP):
                    dve.wait_ge(y_stored[c % DEEP], 16 * (r + c // DEEP))
                dve.tensor_copy(YS[:, c % DEEP, :], Y[:, c % 2, 0:D]).then_inc(y_done, 1)

            def step(r, c):
                j = r * DEEP + c
                bias(r, c)
                gated(r, c)
                if not (isinstance(r, int) and j < 2):
                    keep(r, c - 2)

            steps(dve, step)
            for j in range(TILES1 - 2, TILES1):
                keep(*divmod(j, DEEP))


def recycle(nc):
    used = sorted(s if isinstance(s, int) else s.num for s in nc.released_uncleared_semaphores)
    with nc.Block() as block:
        @block.gpsimd
        def _(pool):
            first = 0
            for i in range(1, len(used) + 1):
                if i == len(used) or used[i] != used[i - 1] + 1:
                    pool.sem_clear(range(used[first], used[i - 1] + 1))
                    first = i


class Layer:
    def __init__(self, name, heads, hd, scale):
        self.name, self.heads, self.hd, self.scale = name, heads, hd, scale
        self.gpb = heads // GH
        self.groups = BATCH * self.gpb
        self.halves = heads * HP // P


def program(nc, ins, out):
    lay0 = Layer("0", 8, 4, (D / 8) ** -0.5)
    lay1 = Layer("1", 16, 16, 16 ** -0.5)
    env = Work()
    with ExitStack() as ctx:
        sb, ps, sem = scope(nc, ctx)
        env.X = sb("X", [P, NT, D])
        env.ident, env.ones, env.before = (sb(n, [P, P]) for n in ("ident", "ones", "before"))
        env.sums = sb("sums", [P, GH])
        env.earlier, env.iota = sb("earlier", [P, E1, E1]), sb("iota", [P, TILES1])
        env.slot0, env.wt0 = sb("slot0", [P, K0, NT], U32), sb("wt0", [P, K0, NT])
        env.slot1, env.wt1 = sb("slot1", [P, K1, NT], U32), sb("wt1", [P, K1, NT])
        env.eps = sb("eps", [P, 1])
        env.x_loaded, env.filled = sem("x_loaded"), sem("filled")
        env.expert = sb("expert", [1, TILES1], I32)
        env.mult = sb("mult", [P, E1, FF1 // P])

        def dram(name, shape, dt=F32):
            return nc.dram_tensor(name, shape, dt, kind="Internal").ap()

        env.xs0, env.ys0 = dram("xs0", [E0 * CAP0, D]), dram("ys0", [E0 * CAP0, D])
        env.xs1, env.ys1 = dram("xs1", [TILES1 * P, D]), dram("ys1", [TILES1 * P, D])
        ex0 = Slots(K0, env.ys0, env.slot0, env.wt0)
        ex1 = Slots(K1, env.ys1, env.slot1, env.wt1)

        def attention(sb, lay, experts=None):
            env.scr = {w: dram(f"scr{w}{lay.name}", [3, lay.groups, GH * HP, SEQ], BF16) for w in "qk"}
            env.ON = sb(f"ON{lay.name}", [P, lay.groups, SEQ])
            with ExitStack() as values:
                vsb, _, _ = scope(nc, values)
                env.VA = vsb(f"VA{lay.name}", [P, lay.groups, TPB, GH * VW])
                if lay is lay0:
                    env.zeros = vsb("zeros", [P, ZROWS * D // P])
                    setup(nc, env, ins)
                project(nc, env, ins, lay, experts)
                attend(nc, env, lay)

        with ExitStack() as first:
            sb, _, sem = scope(nc, first)
            attention(sb, lay0)
            env.EW = Weights(sb, sem)
            route0(nc, env, ins, lay0)
            experts0(nc, env, ins)
        recycle(nc)
        with ExitStack() as second:
            sb, _, sem = scope(nc, second)
            attention(sb, lay1, ex0)
            env.W1 = sb("W1", [P, KD, E1, 2 * FF1])
            env.w1_loaded, env.w2_loaded = sem("w1_loaded"), sem("w2_loaded")
            env.W2 = env.ON[:, :, :].rearrange("p g t -> p (g t)")[:, 0:FF1 // P * E1 * D].rearrange(
                "p (k e d) -> p k e d", k=FF1 // P, e=E1)
            route1(nc, env, ins, lay1)
            experts1(nc, env, ins)
            combine(nc, env, ex1, out)


def kernel(**a):
    import numpy as np
    import concourse.bacc as bacc
    from concourse.bass_utils import run_bass_kernel_spmd

    a = {k: np.asarray(v) for k, v in a.items()}
    kv_w = a["L1_xattn_Wkv"].reshape(D, D, 2)
    kv_b = a["L1_xattn_bkv"].reshape(D, 2)
    arrays = {
        "x": a["x"].reshape(TOK, D), "ctxT": a["ctx_1024"].reshape(TOK, D).T,
        "Wq0": a["L0_xattn_Wq"], "bq0": a["L0_xattn_bq"], "Wk0": a["L0_xattn_Wk"], "bk0": a["L0_xattn_bk"],
        "Wv0": a["L0_xattn_Wv"], "bv0": a["L0_xattn_bv"], "Wo0": a["L0_xattn_Wo"], "bo0": a["L0_xattn_bo"],
        "gamma": a["L0_ffn_ln_gamma"], "beta": a["L0_ffn_ln_beta"], "WrT": a["L0_ffn_Wr"].T,
        "W12T": a["L0_ffn_W12"].transpose(0, 2, 1), "W3T": a["L0_ffn_W3"].transpose(0, 2, 1),
        "Wq1": a["L1_xattn_Wq"], "bq1": a["L1_xattn_bq"], "Wk1": kv_w[:, :, 0], "bk1": kv_b[:, 0],
        "Wv1": kv_w[:, :, 1], "bv1": kv_b[:, 1], "Wo1": a["L1_xattn_Wout"], "bo1": a["L1_xattn_bout"],
        "gateT": a["L1_ffn_gate_w"].T, "fc1T": a["L1_ffn_fc1_w"].transpose(0, 2, 1), "fc1_b": a["L1_ffn_fc1_b"],
        "mult": a["L1_ffn_geglu_mult"], "fc2T": a["L1_ffn_fc2_w"].transpose(0, 2, 1), "fc2_b": a["L1_ffn_fc2_b"],
        "s_fc1T": a["L1_ffn_s_fc1_w"].T, "s_fc1_b": a["L1_ffn_s_fc1_b"], "s_mult": a["L1_ffn_s_geglu_mult"],
        "s_fc2T": a["L1_ffn_s_fc2_w"].T, "s_fc2_b": a["L1_ffn_s_fc2_b"],
    }
    nc = bacc.Bacc("TRN2", target_bir_lowering=False, num_devices=1)
    ins, feeds = {}, {}
    for name, v in arrays.items():
        v = np.ascontiguousarray(v)
        feeds[f"in_{name}"] = v
        ins[name] = nc.dram_tensor(f"in_{name}", v.shape, mybir.dt.from_np(v.dtype), kind="ExternalInput").ap()
    out = nc.dram_tensor("out", (TOK, D), F32, kind="ExternalOutput").ap()
    program(nc, ins, out)
    r = run_bass_kernel_spmd(nc, [feeds], core_ids=[0])
    return np.asarray(r.results[0]["out"]).reshape(BATCH, SEQ, D)
```

```python
from contextlib import ExitStack

import concourse.bass as bass
from concourse import mybir

F32 = mybir.dt.float32
F32R = mybir.dt.float32r
BF16 = mybir.dt.bfloat16
I32 = mybir.dt.int32
U32 = mybir.dt.uint32
ALU = mybir.AluOpType
ACT = mybir.ActivationFunctionType
AX = mybir.AxisListType

P = 128
BATCH, SEQ, D = 4, 512, 256
TOK = BATCH * SEQ
NT = TOK // P
TPB = SEQ // P
KD = D // P
EPS = 1e-5
HP = 16
GH = 4
VW = 32
Q_TERMS = (0, 0, 0, 1, 1, 2)
K_TERMS = (0, 1, 2, 0, 1, 0)
ROWS = HP * len(Q_TERMS)
SHIFT = 2
PB = 4
SLOTS = 4

E0, K0, FF0, CAP0 = 8, 2, 1024, 640
E1, K1, FF1, FFS = 15, 3, 256, 512
TILES1 = (TOK * K1 + E1 * (P - 1)) // P
FAR = 1 << 20


def wait(eng, sem, value):
    if not isinstance(value, int) or value > 0:
        eng.wait_ge(sem, value)


class Link:

    def __init__(self, eng, sem):
        self.eng, self.sem, self.count = eng, sem, 0

    def __call__(self, ins):
        self.count += 1
        ins.then_inc(self.sem, 1)
        self.eng.wait_ge(self.sem, self.count)


def scope(nc, ctx):
    def sb(name, shape, dt=F32):
        return ctx.enter_context(nc.sbuf_tensor(name, shape, dt))

    def ps(name, shape):
        return ctx.enter_context(nc.psum_tensor(name, shape, F32))

    def sem(name):
        return ctx.enter_context(nc.semaphore(name))

    return sb, ps, sem


def carve(flat):
    used = 0

    def sb(name, shape, dt=F32):
        nonlocal used
        n = 1
        for d in shape[1:]:
            n *= d
        part = flat[0:shape[0], used:used + n]
        used += n
        if dt != F32:
            part = part.bitcast(dt)
        dims = "abc"[:len(shape) - 1]
        return part.rearrange(f"p ({' '.join(dims)}) -> p {' '.join(dims)}", **dict(zip(dims, shape[1:])))

    return sb


class Norm:

    def __init__(self, sb, sem, name):
        self.stats, self.mv, self.dev = sb(f"st{name}", [P, NT, 6]), sb(f"mv{name}", [P, NT, 2]), sb(f"dev{name}", [P, NT])
        self.var_ready, self.dev_done, self.done = sem(f"var_ready{name}"), sem(f"dev_done{name}"), sem(f"done{name}")


def norm_stats(dve, link, ln, src, b):
    for t in range(b * TPB, (b + 1) * TPB):
        ins = dve.bn_stats(ln.stats[:, t, :], src[:, t, :])
    link(ins)
    for t in range(b * TPB, (b + 1) * TPB):
        ins = dve.bn_aggr(ln.mv[:, t, :], ln.stats[:, t, :])
    ins.then_inc(ln.var_ready, 1)


def norm_root(act, env, ln, b):
    act.wait_ge(ln.var_ready, b + 1)
    ts = slice(b * TPB, (b + 1) * TPB)
    act.activation(ln.dev[:, ts], ln.mv[:, ts, 1], ACT.Sqrt, bias=env.eps[:, :]).then_inc(ln.dev_done, 1)


def norm_apply(dve, link, ln, src, dst, b):
    dve.wait_ge(ln.dev_done, b + 1)
    ts = slice(b * TPB, (b + 1) * TPB)
    link(dve.reciprocal(ln.dev[:, ts], ln.dev[:, ts]))
    for t in range(b * TPB, (b + 1) * TPB):
        dve.tensor_scalar(dst[:, t, :], src[:, t, :], ln.mv[:, t, 0:1], ln.dev[:, t:t + 1],
                          ALU.subtract, ALU.mult).then_inc(ln.done, 1)


def setup(nc, env):
    with ExitStack() as ctx:
        sb, ps, sem = scope(nc, ctx)
        const0 = sem("su_const0")
        block = ctx.enter_context(nc.Block())

        @block.gpsimd
        def _(pool):
            pool.memset(env.zeros[:, :], 0.0)
            for m in (env.ident, env.sums):
                pool.memset(m[:, :], 0.0)
            pool.memset(env.ones[:, :], 1.0)
            pool.memset(env.eps[:, :], EPS)
            pool.memset(env.before[:, :], 1.0)
            pool.memset(env.earlier[:, :, :], 1.0).then_inc(const0, 1)
            pool.wait_ge(const0, 1)
            pool.affine_select(out=env.ident[:, :], in_=env.ident[:, :], compare_op=ALU.not_equal, fill=1.0,
                               base=0, pattern=[[-1, P]], channel_multiplier=1)
            pool.affine_select(out=env.sums[:, :], in_=env.sums[:, :], compare_op=ALU.not_equal, fill=1.0,
                               base=-HP, pattern=[[-VW, GH]], channel_multiplier=1)
            pool.affine_select(out=env.before[:, :], in_=env.before[:, :], compare_op=ALU.is_gt, fill=0.0,
                               base=0, pattern=[[1, P]], channel_multiplier=-1)
            pool.affine_select(out=env.earlier[:, :, :], in_=env.earlier[:, :, :], compare_op=ALU.is_gt,
                               fill=0.0, base=0, pattern=[[1, E1], [-1, E1]], channel_multiplier=0)
            pool.iota(env.iota[:, :], [[1, TILES1]], base=0, channel_multiplier=0,
                      allow_small_or_imprecise_dtypes=True)


def fill_slots(pool, env, n):
    pieces = [(dram[r:min(r + ZROWS, rows), :], min(ZROWS, rows - r))
              for dram, rows in ((env.xs0, E0 * CAP0), (env.xs1, TILES1 * P)) for r in range(0, rows, ZROWS)]
    for dst, k in pieces[2 * n:2 * n + 2]:
        pool.dma_start(dst.rearrange("(p a) d -> p (a d)", p=P), env.zeros[:, 0:k * D // P]).then_inc(env.filled, 16)


ZROWS = 1024
FILLS = 16 * (-(-E0 * CAP0 // ZROWS) - (-TILES1 * P // ZROWS))


class Split:

    def __init__(self, sem, lay, name, units, W, bias, pq, parts, rest, stored):
        self.lay, self.units, self.W, self.bias = lay, units, W, bias
        self.pq, self.parts, self.rest, self.stored = pq, parts, rest, stored
        self.qk_ready, self.p1_done, self.r1_done, self.p2_done, self.p3_done = (
            sem(n + name) for n in ("qk_ready", "p1_done", "r1_done", "p2_done", "p3_done"))

    def product(self, pe, i, src):
        w, half, b = self.units[i]
        if i >= 2:
            pe.wait_ge(self.r1_done, i - 1)
        for k in range(KD):
            m = pe.matmul(self.pq[:, i % 2, :], self.W[w][:, k, half * P:(half + 1) * P],
                          src[:, k, b * SEQ:(b + 1) * SEQ], start=(k == 0), stop=(k == KD - 1))
        m.then_inc(self.qk_ready, 1)

    def first(self, act, i):
        w, half, b = self.units[i]
        act.wait_ge(self.qk_ready, i + 1)
        if i >= PB:
            act.wait_ge(self.stored[i % PB], 16 * (i // PB))
        act.activation(self.parts[:, i % PB, 0, :], self.pq[:, i % 2, :], ACT.Identity,
                       bias=self.bias[w][:, half:half + 1]).then_inc(self.p1_done, 1)

    def remain(self, dve, i):
        w, half, b = self.units[i]
        dve.wait_ge(self.p1_done, i + 1)
        if i >= 2:
            dve.wait_ge(self.p3_done, i - 1)
        dve.scalar_tensor_tensor(self.rest[:, i % 2, :], self.pq[:, i % 2, :], self.bias[w][:, half:half + 1],
                                 self.parts[:, i % PB, 0, :], ALU.add, ALU.subtract).then_inc(self.r1_done, 1)

    def second(self, act, i):
        act.wait_ge(self.r1_done, i + 1)
        act.copy(self.parts[:, i % PB, 1, :], self.rest[:, i % 2, :]).then_inc(self.p2_done, 1)

    def third(self, dve, i):
        dve.wait_ge(self.p2_done, i + 1)
        dve.tensor_tensor(self.parts[:, i % PB, 2, :], self.rest[:, i % 2, :], self.parts[:, i % PB, 1, :],
                          ALU.subtract).then_inc(self.p3_done, 1)

    def store(self, sp, i):
        w, half, b = self.units[i]
        sp.wait_ge(self.p3_done, i + 1)
        g = b * self.lay.gpb + half * (P // (GH * HP))
        dst = self.lay.scr[w][:, g:g + 2, :, :].rearrange("s g r t -> (g r) s t")
        sp.dma_start(dst, self.parts[:, i % PB, :, :]).then_inc(self.stored[i % PB], 16)


def units_of(lay, w):
    return [(w, half, b) for b in range(BATCH) for half in range(lay.halves)]


def project(nc, env, ins, lay, experts=None):
    L, hd, halves, gpb = lay.name, lay.hd, lay.halves, lay.gpb
    heads, width = lay.heads, lay.heads * HP
    with ExitStack() as ctx:
        sb, ps, sem = scope(nc, ctx)
        ctxT = sb(f"ctxT{L}", [P, KD, TOK])
        XN = sb(f"XN{L}", [P, NT, D])
        XNT = sb(f"XNT{L}", [P, KD, TOK])
        split_of = "q" if experts else "kq"
        W = {w: sb(f"w{w}{L}", [P, KD, width]) for w in "v" + split_of}
        bias = {w: sb(f"b{w}{L}", [P, halves]) for w in split_of}
        bv = sb(f"bv{L}", [1, width])
        rest = sb(f"rest{L}", [P, 2, SEQ])
        ln = Norm(sb, sem, f"p{L}")
        YG = sb(f"YG{L}p", [P, GDEEP, D])
        tp = ps(f"tp{L}", [P, 2, SEQ])
        pv = ps(f"pv{L}", [P, 2, SEQ])
        pq = ps(f"pq{L}", [P, 2, SEQ])
        w_zero, w_loaded = sem(f"w_zero{L}"), {w: sem(f"w{w}_loaded{L}") for w in W}
        ctx_loaded = [sem(f"ctx_loaded{b}{L}") for b in range(BATCH)]
        chain, va_ones, added = sem(f"chain{L}"), sem(f"va_ones{L}"), sem(f"added{L}p")
        tp_ready, xnt_done = sem(f"tp_ready{L}"), sem(f"xnt_done{L}")
        v_ready, v_done = sem(f"v_ready{L}"), sem(f"v_done{L}")
        st = env.stacks
        units = [u for w in split_of for u in units_of(lay, w)]
        split = Split(sem, lay, L, units, W, bias, pq, st.parts, rest, st.stored)
        n_k = halves * BATCH if "k" in split_of else 0
        block = ctx.enter_context(nc.Block())

        @block.sync
        def _(sp):
            def load_ctx(b):
                at = slice(b * SEQ, (b + 1) * SEQ)
                sp.dma_start(ctxT[:, :, at], ins["ctxT"].rearrange("(k p) t -> p k t", p=P)[:, :, at]
                             ).then_inc(ctx_loaded[b], 16)

            load_ctx(0)
            sp.wait_ge(w_zero, 1)
            for w in "v" + split_of:
                src = ins[f"W{w}{L}"].rearrange("(k p) (h d) -> k p h d", p=P, d=hd)
                for k in range(KD):
                    dst = W[w][:, k, :].rearrange("p (h d) -> p h d", d=HP)[:, :, 0:hd]
                    sp.dma_start(dst, src[k]).then_inc(w_loaded[w], 16)
                src = ins[f"b{w}{L}"]
                if w == "v":
                    sp.dma_start(bv[0:1, :].rearrange("o (h d) -> o h d", d=HP)[:, :, 0:hd],
                                 src.rearrange("(o h d) -> o h d", o=1, d=hd)).then_inc(w_loaded[w], 16)
                    for b in range(1, BATCH):
                        load_ctx(b)
                    if not experts:
                        sp.dma_start(env.X[:, :, :], ins["x"].rearrange("(t p) d -> p t d", p=P)).then_inc(env.x_loaded, 16)
                elif hd == HP:
                    with nc.allow_non_contiguous_dma(reason="a small bias"):
                        sp.dma_start(bias[w][:, :], src.rearrange("(f p) -> p f", p=P)).then_inc(w_loaded[w], 16)
                else:
                    for h in range(heads):
                        with nc.allow_non_contiguous_dma(reason="a small bias"):
                            sp.dma_start(bias[w][HP * h:HP * h + hd, 0:1],
                                         src[hd * h:hd * h + hd].unsqueeze(1)).then_inc(w_loaded[w], 16)
            for i in range(len(units)):
                split.store(sp, i)
                if i == n_k + 2:
                    for j in range(PB):
                        wait(sp, st.stored[j], 16 * (n_k // PB + (1 if j < 2 else 0)))
                for n in range(st.ahead):
                    if i == n_k + 2 + 2 * n:
                        load_stacks(sp, env, lay, 0, n)

        weights = {w: 16 * (KD + (heads if w in "qk" and hd != HP else 1)) for w in W}

        @block.gpsimd
        def _(pool):
            if hd != HP:
                for w in W:
                    pool.memset(W[w][:, :, :], 0.0)
                for w in bias:
                    pool.memset(bias[w][:, :], 0.0)
            pool.memset(bv[:, :], 0.0).then_inc(w_zero, 1)
            pool.memset(env.WO[:, :, :], 0.0).then_inc(env.wo_zero, 1)
            if experts:
                for n in range(NT * experts.K):
                    gather(pool, env, experts, YG, added, n)
            pool.wait_ge(env.wo_zero, 1)
            pool.memset(st.KS[ROWS:ROWS + 32, :, :, :], 1.0).then_inc(st.shift_ones, 1)
            pool.wait_ge(st.shift_ones, 1)

        @block.vector
        def _(dve):
            link = Link(dve, chain)
            dve.memset(env.VA[:, 0:lay.groups, :, :], 1.0).then_inc(va_ones, 1)

            for b in range(BATCH):
                if experts:
                    for n in range(b * TPB * experts.K, (b + 1) * TPB * experts.K):
                        add_gathered(dve, env, experts, YG, added, n)
                elif b == 0:
                    dve.wait_ge(env.x_loaded, 16)
                for i in range(n_k * b // BATCH, n_k * (b + 1) // BATCH):
                    split.remain(dve, i)
                    if i:
                        split.third(dve, i - 1)
                    if i == n_k - 1:
                        split.third(dve, i)
                if experts:
                    dve.wait_ge(added, (b + 1) * TPB * experts.K)
                norm_stats(dve, link, ln, env.X, b)
                if b:
                    norm_apply(dve, link, ln, env.X, XN, b - 1)
            norm_apply(dve, link, ln, env.X, XN, BATCH - 1)
            for i in range(n_k, len(units)):
                split.remain(dve, i)
                if i > n_k:
                    split.third(dve, i - 1)
            split.third(dve, len(units) - 1)

        @block.scalar
        def _(act):
            act.wait_ge(va_ones, 1)
            for t in range(NT):
                act.wait_ge(v_ready, t + 1)
                b, kt = divmod(t, TPB)
                dst = env.VA[:, b * gpb:(b + 1) * gpb, kt, :].rearrange("p g (h c) -> p g h c", c=VW)
                src = pv[:, t % 2, 0:width].rearrange("p (g h c) -> p g h c", h=GH, c=HP)
                for g in range(gpb):
                    ins_ = act.copy(dst[:, g, :, 0:HP], src[:, g, :, :])
                ins_.then_inc(v_done, 1)

            def turned(b):
                for k in range(KD):
                    act.wait_ge(tp_ready, b * KD + k + 1)
                    act.copy(XNT[:, k, b * SEQ:(b + 1) * SEQ], tp[:, k, :]).then_inc(xnt_done, 1)

            for b in range(BATCH):
                for i in range(n_k * b // BATCH, n_k * (b + 1) // BATCH):
                    split.first(act, i)
                    if i:
                        split.second(act, i - 1)
                    if i == n_k - 1:
                        split.second(act, i)
                norm_root(act, env, ln, b)
            turned(0)
            for b in range(BATCH):
                if b + 1 < BATCH:
                    turned(b + 1)
                for half in range(halves):
                    i = n_k + b * halves + half
                    split.first(act, i)
                    if i > n_k:
                        split.second(act, i - 1)
            split.second(act, len(units) - 1)

        @block.tensor
        def _(pe):
            pe.wait_ge(w_loaded["v"], weights["v"])
            for t in range(NT):
                if t % TPB == 0:
                    pe.wait_ge(ctx_loaded[t // TPB], 16)
                if t >= 2:
                    pe.wait_ge(v_done, t - 1)
                for k in range(KD):
                    pe.matmul(pv[:, t % 2, 0:width], ctxT[:, k, t * P:(t + 1) * P], W["v"][:, k, :],
                              start=(k == 0), stop=False)
                pe.matmul(pv[:, t % 2, 0:width], env.ones[0:1, :], bv[:, :],
                          start=False, stop=True).then_inc(v_ready, 1)

            def turn(b):
                pe.wait_ge(ln.done, (b + 1) * TPB)
                for k in range(KD):
                    if b:
                        pe.wait_ge(xnt_done, (b - 1) * KD + k + 1)
                    for j in range(TPB):
                        m = pe.transpose(tp[:, k, j * P:(j + 1) * P], XN[:, b * TPB + j, k * P:(k + 1) * P],
                                         env.ident[:, :])
                    m.then_inc(tp_ready, 1)

            if n_k:
                pe.wait_ge(w_loaded["k"], weights["k"])
            for i in range(n_k):
                split.product(pe, i, ctxT)
            turn(0)
            pe.wait_ge(w_loaded["q"], weights["q"])
            for b in range(BATCH):
                if b + 1 < BATCH:
                    turn(b + 1)
                pe.wait_ge(xnt_done, KD * (b + 1))
                for half in range(halves):
                    split.product(pe, n_k + b * halves + half, XNT)


class Stacks:

    def __init__(self, sb, sem, lay, units):
        L, self.units = lay.name, units
        self.ahead = lay.halves
        self.QS, self.KS = (sb(f"{n}{L}", [P, SLOTS, GH, SEQ], BF16) for n in ("QS", "KS"))
        self.parts = sb(f"parts{L}", [P, PB, 3, SEQ], BF16)
        self.stored = [sem(f"stored{i}{L}") for i in range(PB)]
        self.qk_loaded = [sem(f"qk_loaded{i}{L}") for i in range(SLOTS)]
        self.shift_ones = sem(f"shift_ones{L}")


def load_stacks(sp, env, lay, r, c):
    n, slot, st = r * SLOTS + c, c % SLOTS, env.stacks
    for stack, terms, w in ((st.QS, Q_TERMS, "q"), (st.KS, K_TERMS, "k")):
        for i, part in enumerate(terms):
            sp.dma_start(stack[HP * i:HP * (i + 1), slot, :, :],
                         lay.scr[w][part, n, :, :].rearrange("(h d) t -> d h t", d=HP)).then_inc(st.qk_loaded[slot], 16)


def attend(nc, env, ins, lay):
    L, NG = lay.name, lay.groups
    with ExitStack() as ctx:
        sb, ps, sem = scope(nc, ctx)
        st = env.stacks
        QS, KS, qk_loaded = st.QS, st.KS, st.qk_loaded
        PT = sb(f"PT{L}", [P, 2, GH, TPB, SEQ])
        VG = sb(f"VG{L}", [P, 2, TPB, P])
        M = sb(f"M{L}", [P, 2, GH * TPB])
        NM = sb(f"NM{L}", [GH * TPB, 2, SHIFT, P], BF16)
        OSB = sb(f"OSB{L}", [P, 2, SEQ])
        RC, RX = sb(f"RC{L}", [P, 2, TPB, GH]), sb(f"RX{L}", [P, TPB, P])
        S1 = ps(f"S1{L}", [P, 2, SEQ])
        S2 = ps(f"S2{L}", [P, 2, 2, SEQ])
        PV = ps(f"PV{L}", [P, SEQ])
        MISC = ps(f"MISC{L}", [P, SEQ])
        nm_loaded = [sem(f"nm_loaded{i}{L}") for i in range(SLOTS)]
        (s1_ready, max_done, mt_ready, nm1_done, nm_done, s2_ready, exp_done, vg_ready, pv_ready,
         osb_done, cols_ready, rc_done, rx_done, spread_ready, on_done) = (sem(n + L) for n in (
             "s1_ready", "max_done", "mt_ready", "nm1_done", "nm_done", "s2_ready", "exp_done",
             "vg_ready", "pv_ready", "osb_done", "cols_ready", "rc_done", "rx_done", "spread_ready", "on_done"))
        loads = 16 * (len(Q_TERMS) + len(K_TERMS))
        block = ctx.enter_context(nc.Block())

        def steps(eng, step):
            for c in range(SLOTS + 1):
                step(0, c)
            if NG > 2 * SLOTS:
                with eng.Fori(1, NG // SLOTS - 1) as r:
                    for c in range(1, 1 + SLOTS):
                        step(r, c)
            for c in range(1, SLOTS):
                step(NG // SLOTS - 1, c)

        def last(r, c, ahead):
            return isinstance(r, int) and SLOTS * r + c + ahead >= NG

        @block.sync
        def _(sp):
            def shift(r, c):
                n, slot = r * SLOTS + c, c % SLOTS
                sp.wait_ge(nm_done, n + 1)
                for i in range(SHIFT):
                    sp.dma_start(QS[ROWS + i:ROWS + i + 1, slot, :, :].rearrange("o h (q t) -> o (h q) t", t=P),
                                 NM[:, c % 2, i, :]).then_inc(nm_loaded[slot], 16)

            for j in range(PB):
                sp.wait_ge(st.stored[j], 16 * st.units // PB)
            for n in range(st.ahead, SLOTS - 1):
                load_stacks(sp, env, lay, 0, n)
            shift(0, 0)

            def step(r, c):
                if not last(r, c, 3):
                    wait(sp, s2_ready, 8 * (r * SLOTS + c))
                    load_stacks(sp, env, lay, r, c + 3)
                if not last(r, c, 1):
                    shift(r, c + 1)

            steps(sp, step)
            load_out_weights(sp, env, ins, lay)

        @block.gpsimd
        def _(pool):
            def step(r, c):
                n = r * SLOTS + c
                if lay.groups <= 2 * SLOTS:
                    fill_slots(pool, env, n)
                wait(pool, pv_ready, n - 1)
                pool.tensor_copy(VG[:, c % 2, :, :], env.VA[:, n, :, :]).then_inc(vg_ready, 1)

            steps(pool, step)

        @block.tensor
        def _(pe):
            def maxima(r, c, h, q):
                n, slot = r * SLOTS + c, c % SLOTS
                if h == 0 and q == 0:
                    pe.wait_ge(qk_loaded[slot], loads * (r + c // SLOTS + 1))
                i = n * GH * TPB + h * TPB + q
                wait(pe, max_done, i - 1)
                pe.matmul(S1[:, q % 2, :], QS[0:ROWS, slot, h, q * P:(q + 1) * P], KS[0:ROWS, slot, h, :],
                          start=True, stop=True).then_inc(s1_ready, 1)

            def turn(r, c):
                n = r * SLOTS + c
                pe.wait_ge(max_done, GH * TPB * (n + 1))
                wait(pe, on_done, n - 3)
                pe.transpose(MISC[0:GH * TPB, 0:P], M[:, c % 2, :], env.ident[:, :]).then_inc(mt_ready, 1)

            def scores(r, c, h, u):
                n, slot = r * SLOTS + c, c % SLOTS
                if h == 0 and u == 0:
                    pe.wait_ge(nm_loaded[slot], 16 * SHIFT * (r + c // SLOTS + 1))
                i = n * 2 * GH + h * 2 + u
                wait(pe, exp_done, i - 1)
                for j in range(2):
                    kt = 2 * u + j
                    m = pe.matmul(S2[:, u, j, :], KS[0:ROWS + SHIFT, slot, h, kt * P:(kt + 1) * P],
                                  QS[0:ROWS + SHIFT, slot, h, :], start=True, stop=True)
                m.then_inc(s2_ready, 1)

            def values(r, c, kt):
                n = r * SLOTS + c
                if kt == 0:
                    pe.wait_ge(exp_done, 2 * GH * (n + 1))
                    pe.wait_ge(vg_ready, n + 1)
                    wait(pe, osb_done, n)
                for h in range(GH):
                    m = pe.matmul(PV[VW * h:VW * (h + 1), :], VG[:, c % 2, kt, VW * h:VW * (h + 1)],
                                  PT[:, c % 2, h, kt, :], start=(kt == 0), stop=(kt == TPB - 1))
                if kt == TPB - 1:
                    m.then_inc(pv_ready, 1)

            def columns(r, c, turned):
                n = r * SLOTS + c
                pe.wait_ge(osb_done, n + 1)
                pe.wait_ge(nm_done, turned)
                wait(pe, on_done, n)
                for q in range(TPB):
                    m = pe.matmul(MISC[:, q * GH:(q + 1) * GH], OSB[:, c % 2, q * P:(q + 1) * P], env.sums[:, :],
                                  start=True, stop=True)
                m.then_inc(cols_ready, 1)

            def spread(r, c):
                n = r * SLOTS + c
                pe.wait_ge(rx_done, n + 1)
                for q in range(TPB):
                    m = pe.transpose(MISC[:, q * P:(q + 1) * P], RX[:, q, :], env.ident[:, :])
                m.then_inc(spread_ready, 1)

            pe.wait_ge(st.shift_ones, 1)
            for c in range(2):
                for h in range(GH):
                    for q in range(TPB):
                        maxima(0, c, h, q)
            turn(0, 0)

            def step(r, c):
                n = r * SLOTS + c
                least = n if isinstance(r, int) else 2
                for h in range(GH):
                    for u in range(2):
                        if not last(r, c, 2):
                            maxima(r, c + 2, h, 2 * u)
                        scores(r, c, h, u)
                        if not last(r, c, 2):
                            maxima(r, c + 2, h, 2 * u + 1)
                        if u == 0 and h >= 1 and least >= 1:
                            values(r, c - 1, h - 1)
                    if h == 1 and not last(r, c, 1):
                        turn(r, c + 1)
                    if h == 2 and least >= 2:
                        columns(r, c - 2, NG if last(r, c, 2) else n + 2)
                if least >= 1:
                    values(r, c - 1, TPB - 1)
                if least >= 2:
                    spread(r, c - 2)

            steps(pe, step)
            r, c = divmod(NG - 1, SLOTS)
            for kt in range(TPB):
                values(r, c, kt)
            for m in range(NG - 2, NG):
                columns(*divmod(m, SLOTS), NG)
                spread(*divmod(m, SLOTS))

        @block.scalar
        def _(act):
            def negate(r, c):
                n = r * SLOTS + c
                act.wait_ge(mt_ready, n + 1)
                if not (isinstance(r, int) and n < 2):
                    act.wait_ge(nm_loaded[(c - 2) % SLOTS], 16 * SHIFT * (r + (c - 2) // SLOTS + 1))
                act.activation(NM[:, c % 2, 0, :], MISC[0:GH * TPB, 0:P], ACT.Copy, scale=-1.0).then_inc(nm1_done, 1)

            def keep(r, c):
                n = r * SLOTS + c
                act.wait_ge(pv_ready, n + 1)
                wait(act, on_done, n - 1)
                act.copy(OSB[:, c % 2, :], PV[:, :]).then_inc(osb_done, 1)

            def widen(r, c):
                n = r * SLOTS + c
                act.wait_ge(rc_done, n + 1)
                wait(act, spread_ready, n)
                act.copy(RX[:, :, :].rearrange("p q (h i) -> p q h i", i=VW),
                         RC[:, c % 2, :, :].unsqueeze(3).to_broadcast([P, TPB, GH, VW])).then_inc(rx_done, 1)

            negate(0, 0)

            def step(r, c):
                n = r * SLOTS + c
                least = n if isinstance(r, int) else 2
                wait(act, pv_ready, n - 1)
                for h in range(GH):
                    for u in range(2):
                        act.wait_ge(s2_ready, n * 2 * GH + h * 2 + u + 1)
                        act.activation(PT[:, c % 2, h, 2 * u:2 * u + 2, :], S2[:, u, :, :], ACT.Exp,
                                       scale=lay.scale).then_inc(exp_done, 1)
                        if h == 3 and u == 0 and least >= 2:
                            widen(r, c - 2)
                    if h == 0 and least >= 2:
                        keep(r, c - 2)
                    if h == 1 and not last(r, c, 1):
                        negate(r, c + 1)

            steps(act, step)
            for m in range(NG - 2, NG):
                keep(*divmod(m, SLOTS))
                widen(*divmod(m, SLOTS))

        @block.vector
        def _(dve):
            def maxima(r, c, h):
                n = r * SLOTS + c
                if h == 0:
                    wait(dve, mt_ready, n - 1)
                for q in range(TPB):
                    i = n * GH * TPB + h * TPB + q
                    dve.wait_ge(s1_ready, i + 1)
                    dve.tensor_reduce(M[:, c % 2, h * TPB + q:h * TPB + q + 1], S1[:, q % 2, :], AX.X,
                                      ALU.max).then_inc(max_done, 1)

            def negate(r, c):
                dve.wait_ge(nm1_done, r * SLOTS + c + 1)
                dve.scalar_tensor_tensor(NM[:, c % 2, 1, :], MISC[0:GH * TPB, 0:P], -1.0, NM[:, c % 2, 0, :],
                                         ALU.mult, ALU.subtract).then_inc(nm_done, 1)

            def invert(r, c):
                n = r * SLOTS + c
                dve.wait_ge(cols_ready, n + 1)
                wait(dve, rx_done, n - 1)
                dve.reciprocal(RC[:, c % 2, :, :], MISC[:, 0:TPB * GH].rearrange("p (q h) -> p q h", h=GH)).then_inc(rc_done, 1)

            def normalize(r, c):
                n = r * SLOTS + c
                dve.wait_ge(spread_ready, n + 1)
                dve.tensor_tensor(env.ON[:, n, :], OSB[:, c % 2, :], MISC[:, :], ALU.mult).then_inc(on_done, 1)

            for c in range(2):
                for h in range(GH):
                    maxima(0, c, h)
            negate(0, 0)

            def step(r, c):
                least = r * SLOTS + c if isinstance(r, int) else 3
                for h in range(GH):
                    if not last(r, c, 2):
                        maxima(r, c + 2, h)
                    if h == 0 and least >= 3:
                        normalize(r, c - 3)
                    if h == 1 and not last(r, c, 1):
                        negate(r, c + 1)
                    if h == 2 and least >= 2:
                        invert(r, c - 2)

            steps(dve, step)
            normalize(*divmod(NG - 3, SLOTS))
            for m in range(NG - 2, NG):
                invert(*divmod(m, SLOTS))
                normalize(*divmod(m, SLOTS))


def pick(dve, link, env, w, E, K, logits, cut):
    wide = [P, NT, E]
    if cut:
        link(dve.tensor_scalar(w.lg[:, :, :], logits, -1e4, 1e4, ALU.max, ALU.min))
    else:
        link(dve.tensor_copy(w.lg[:, :, :], logits))
    link(dve.tensor_reduce(w.red[:, :], w.lg[:, :, :], AX.X, ALU.max))
    link(dve.tensor_tensor(w.lg[:, :, :], w.lg[:, :, :], w.red[:, :].unsqueeze(2).to_broadcast(wide), ALU.subtract))


def softmax_top(dve, link, env, w, E, K, floor):
    wide = [P, NT, E]
    link(dve.tensor_reduce(w.red[:, :], w.ex[:, :, :], AX.X, ALU.add))
    if floor:
        link(dve.tensor_scalar(w.red[:, :], w.red[:, :], floor, None, ALU.add))
    link(dve.reciprocal(w.red2[:, :], w.red[:, :]))
    link(dve.tensor_tensor(w.pr[:, :, :], w.ex[:, :, :], w.red2[:, :].unsqueeze(2).to_broadcast(wide), ALU.mult))
    for t in range(NT):
        ins = dve.max(w.top[:, t, :], w.pr[:, t, :])
    link(ins)
    for t in range(NT):
        ins = dve.max_index(w.idx[:, t, :], w.top[:, t, :], w.pr[:, t, :])
    link(ins)
    link(dve.tensor_copy(w.idf[:, :, :], w.idx[:, :, 0:K].rearrange("p t k -> p k t")))
    for k in range(K):
        ins = dve.tensor_tensor(w.hot[:, k, :, :], env.iota[:, 0:E].unsqueeze(1).to_broadcast(wide),
                                w.idf[:, k, :].unsqueeze(2).to_broadcast(wide), ALU.is_equal)
    link(ins)
    link(dve.tensor_tensor(w.all[:, :, :], w.hot[:, 0, :, :], w.hot[:, 1, :, :], ALU.add))
    for k in range(2, K):
        link(dve.tensor_tensor(w.all[:, :, :], w.all[:, :, :], w.hot[:, k, :, :], ALU.add))
    dve.memset(w.run[:, 0, :], 0.0)
    src, dst, d = w.all, w.tmp, 1
    while d < NT:
        if 2 * d >= NT:
            dst = w.run[:, 1:NT + 1, :]
        dve.tensor_copy(dst[:, 0:d, :], src[:, 0:d, :])
        link(dve.tensor_tensor(dst[:, d:NT, :], src[:, d:NT, :], src[:, 0:NT - d, :], ALU.add))
        src, dst, d = dst, w.pr if dst is w.tmp else w.tmp, 2 * d


class Work:
    pass


def routing_buffers(sb, L, E, K):
    w = Work()
    w.lg, w.ex, w.pr, w.all, w.tmp = (sb(f"{n}{L}", [P, NT, E]) for n in ("lg", "ex", "pr", "all", "tmp"))
    w.red, w.red2 = sb(f"red{L}", [P, NT]), sb(f"red2{L}", [P, NT])
    w.top, w.idx = sb(f"top{L}", [P, NT, 8]), sb(f"idx{L}", [P, NT, 8], U32)
    w.idf, w.hot = sb(f"idf{L}", [P, K, NT]), sb(f"hot{L}", [P, K, NT, E])
    w.run = sb(f"run{L}", [P, NT + 1, E])
    w.rank, w.over = sb(f"rank{L}", [P, K, NT]), sb(f"over{L}", [P, K, NT])
    w.slot = sb(f"pos{L}", [P, K, NT])
    return w


def out_projection(pe, env, lay, po, wo_ready, x_done):
    pe.wait_ge(env.wo_loaded, 16 * (lay.gpb * GH + 1))
    for t in range(NT):
        b, q = divmod(t, TPB)
        if t >= 2:
            pe.wait_ge(x_done, t - 1)
        for g in range(lay.gpb):
            m = pe.matmul(po[:, t % 2, 0:D], env.ON[:, b * lay.gpb + g, q * P:(q + 1) * P], env.WO[:, g, :],
                          start=(g == 0), stop=(g == lay.gpb - 1))
        m.then_inc(wo_ready, 1)


def load_out_weights(sp, env, ins, lay):
    sp.wait_ge(env.wo_zero, 1)
    for g in range(lay.gpb):
        for h in range(GH):
            r = (g * GH + h) * lay.hd
            sp.dma_start(env.WO[VW * h:VW * h + lay.hd, g, :], ins[f"Wo{lay.name}"][r:r + lay.hd, :]
                         ).then_inc(env.wo_loaded, 16)
    sp.dma_start(env.WO[HP:HP + 1, 0, :], ins[f"bo{lay.name}"].unsqueeze(0)).then_inc(env.wo_loaded, 16)


def route0(nc, env, ins, lay, after):
    with ExitStack() as ctx:
        sb, ps, sem = scope(nc, ctx)
        Hn, XF, XFT = sb("H0", [P, NT, D]), sb("XF0", [P, NT, D]), sb("XFT0", [P, KD, TOK])
        gamma, beta, Wr = sb("gamma", [P, D]), sb("beta", [P, D]), sb("Wr", [P, KD, E0])
        gammaT, betaT = sb("gammaT", [P, KD]), sb("betaT", [P, KD])
        ln1, ln2 = Norm(sb, sem, "r0"), Norm(sb, sem, "f0")
        w = routing_buffers(sb, "0", E0, K0)
        scaled = sem("scaled0r")
        into = sb("into0", [P, K0, NT], U32)
        Wk, bk = sb("Wk1", [P, KD, after.heads * HP]), sb("bk1", [P, after.halves])
        ctxT, flat = XFT, XF[:, :, :].rearrange("p t d -> p (t d)")
        words = PB * 3 * SEQ // 2
        parts = flat[:, 0:words].bitcast(BF16).rearrange("p (i s t) -> p i s t", i=PB, s=3)
        rest = flat[:, words:words + 2 * SEQ].rearrange("p (i t) -> p i t", i=2)
        po, tp = ps("po0", [P, 2, SEQ]), ps("tp0r", [P, 2, SEQ])
        lgp, rk = ps("lgp0", [P, NT, E0]), ps("rk0", [P, NT, E0])
        wo_ready, x_done, chain, xf_done, r_loaded, t_loaded = (sem(n + "0r") for n in (
            "wo_ready", "x_done", "chain", "xf_done", "r_loaded", "t_loaded"))
        tp_ready, xft_done, lg_ready, lg_sub, ex_done, run_done, rk_ready, slots_done = (
            sem(n + "0r") for n in ("tp_ready", "xft_done", "lg_ready", "lg_sub", "ex_done", "run_done", "rk_ready",
                                    "slots_done"))
        wk_loaded, ctx_loaded = sem("wk_loaded0r"), [sem(f"ctx_loaded{b}0r") for b in range(BATCH)]
        split = Split(sem, after, "0r", units_of(after, "k"), {"k": Wk}, {"k": bk}, po, parts, rest,
                      [sem(f"stored{i}0r") for i in range(PB)])
        n_k = len(split.units)
        block = ctx.enter_context(nc.Block())

        @block.sync
        def _(sp):
            sp.dma_start(gamma[:, :], ins["gamma"].partition_broadcast(P)).then_inc(r_loaded, 16)
            sp.dma_start(beta[:, :], ins["beta"].partition_broadcast(P)).then_inc(r_loaded, 16)
            with nc.allow_non_contiguous_dma(reason="a small matrix"):
                sp.dma_start(Wr[:, :, :], ins["WrT"].rearrange("(k p) e -> p k e", p=P)).then_inc(t_loaded, 16)
                sp.dma_start(gammaT[:, :], ins["gamma"].rearrange("(k p) -> p k", p=P)).then_inc(t_loaded, 16)
                sp.dma_start(betaT[:, :], ins["beta"].rearrange("(k p) -> p k", p=P)).then_inc(t_loaded, 16)
                sp.dma_start(bk[:, :], ins[f"bk{after.name}"].rearrange("(f p) -> p f", p=P)).then_inc(wk_loaded, 16)
            sp.dma_start(Wk[:, :, :], ins[f"Wk{after.name}"].rearrange("(k p) c -> p k c", p=P)).then_inc(wk_loaded, 16)
            load_weights(sp, ins, env.EW, 0, 0, range(STAGES))
            for b in range(BATCH):
                if b == BATCH - 1:
                    load_weights(sp, ins, env.EW, 0, 0, range(STAGES, PIECES))
                sp.wait_ge(lg_ready, b + 1)
                at = slice(b * SEQ, (b + 1) * SEQ)
                sp.dma_start(ctxT[:, :, at], ins["ctxT"].rearrange("(k p) t -> p k t", p=P)[:, :, at]
                             ).then_inc(ctx_loaded[b], 16)
            for i in range(n_k):
                split.store(sp, i)
            for j in range(PB):
                sp.wait_ge(split.stored[j], 16 * n_k // PB)

        @block.gpsimd
        def _(pool):
            pool.wait_ge(r_loaded, 32)
            for t in range(NT):
                pool.wait_ge(ln2.done, t + 1)
                pool.tensor_tensor(Hn[:, t, :], XF[:, t, :], gamma[:, :], ALU.mult).then_inc(scaled, 1)
                pool.wait_ge(scaled, t + 1)
                pool.tensor_tensor(Hn[:, t, :], Hn[:, t, :], beta[:, :], ALU.add).then_inc(xf_done, 1)
            load_weights_low(pool, env.EW, 0, 0)
            pool.wait_ge(env.filled, FILLS)
            pool.wait_ge(xf_done, NT)
            pool.wait_ge(slots_done, 1)
            for t in range(NT):
                for k in range(K0):
                    pool.indirect_dma_start(
                        out=env.xs0[:, :], out_offset=bass.IndirectOffsetOnAxis(ap=into[:, k, t:t + 1], axis=0),
                        in_=Hn[:, t, :], in_offset=None, bounds_check=E0 * CAP0 - 1, oob_is_err=False,
                    ).then_inc(env.scattered, 16)
            pool.wait_ge(env.scattered, 16 * NT * K0)

        @block.tensor
        def _(pe):
            out_projection(pe, env, lay, po, wo_ready, x_done)

            def router(b):
                pe.wait_ge(xft_done, (b + 1) * KD)
                for t in range(b * TPB, (b + 1) * TPB):
                    for k in range(KD):
                        m = pe.matmul(lgp[:, t, :], XFT[:, k, t * P:(t + 1) * P], Wr[:, k, :],
                                      start=(k == 0), stop=(k == KD - 1))
                m.then_inc(lg_ready, 1)

            pe.wait_ge(t_loaded, 48)
            for b in range(BATCH):
                pe.wait_ge(ln2.done, (b + 1) * TPB)
                for n in range(b * KD, (b + 1) * KD):
                    if n >= 2:
                        pe.wait_ge(xft_done, n - 1)
                    for j in range(TPB):
                        m = pe.transpose(tp[:, n % 2, j * P:(j + 1) * P],
                                         XF[:, b * TPB + j, (n - b * KD) * P:(n - b * KD + 1) * P], env.ident[:, :])
                    m.then_inc(tp_ready, 1)
                if b:
                    router(b - 1)
            router(BATCH - 1)
            pe.wait_ge(run_done, 1)
            pe.matmul(rk[:, :, :], env.before[:, :], w.all[:, :, :], start=True, stop=False)
            pe.matmul(rk[:, :, :], env.ones[:, :], w.run[:, 0:NT, :], start=False, stop=True).then_inc(rk_ready, 1)
            pe.wait_ge(wk_loaded, 32)
            pe.wait_ge(x_done, NT)
            for i in range(n_k):
                if i % after.halves == 0:
                    pe.wait_ge(ctx_loaded[i // after.halves], 16)
                split.product(pe, i, ctxT)

        @block.scalar
        def _(act):
            for b in range(BATCH + 1):
                if b < BATCH:
                    norm_root(act, env, ln1, b)
                if b:
                    norm_root(act, env, ln2, b - 1)
            act.wait_ge(t_loaded, 48)
            for n in range(BATCH * KD):
                t4, k = divmod(n, KD)
                act.wait_ge(tp_ready, n + 1)
                act.activation(XFT[:, k, t4 * SEQ:(t4 + 1) * SEQ], tp[:, n % 2, :], ACT.Identity,
                               bias=betaT[:, k:k + 1], scale=gammaT[:, k:k + 1]).then_inc(xft_done, 1)
            load_weights_high(act, env.EW, 0, 0, range(STAGES))
            act.wait_ge(lg_sub, 1)
            act.activation(w.ex[:, :, :], w.lg[:, :, :], ACT.Exp).then_inc(ex_done, 1)
            load_weights_high(act, env.EW, 0, 0, range(STAGES, PIECES))
            act.wait_ge(xf_done, NT)
            for i in range(n_k):
                split.first(act, i)
                if i:
                    split.second(act, i - 1)
            split.second(act, n_k - 1)

        @block.vector
        def _(dve):
            link = Link(dve, chain)
            for b in range(BATCH + 2):
                if b < BATCH:
                    for t in range(b * TPB, (b + 1) * TPB):
                        dve.wait_ge(wo_ready, t + 1)
                        dve.tensor_tensor(env.X[:, t, :], po[:, t % 2, 0:D], env.X[:, t, :], ALU.add).then_inc(x_done, 1)
                    dve.wait_ge(x_done, (b + 1) * TPB)
                    norm_stats(dve, link, ln1, env.X, b)
                if 1 <= b <= BATCH:
                    norm_apply(dve, link, ln1, env.X, Hn, b - 1)
                    dve.wait_ge(ln1.done, b * TPB)
                    norm_stats(dve, link, ln2, Hn, b - 1)
                if b >= 2:
                    norm_apply(dve, link, ln2, Hn, XF, b - 2)
            dve.wait_ge(lg_ready, BATCH)
            pick(dve, link, env, w, E0, K0, lgp[:, :, :], True)
            dve.nop().then_inc(lg_sub, 1)
            dve.wait_ge(ex_done, 1)
            softmax_top(dve, link, env, w, E0, K0, 1e-12)
            dve.nop().then_inc(run_done, 1)
            dve.wait_ge(rk_ready, 1)
            for k in range(K0):
                link(dve.tensor_tensor(w.tmp[:, :, :], rk[:, :, :], w.hot[:, k, :, :], ALU.mult))
                link(dve.tensor_reduce(w.rank[:, k, :], w.tmp[:, :, :], AX.X, ALU.add))
            link(dve.tensor_scalar(w.over[:, :, :], w.rank[:, :, :], float(CAP0), None, ALU.is_ge))
            link(dve.scalar_tensor_tensor(w.slot[:, :, :], w.idf[:, :, :], float(CAP0), w.rank[:, :, :],
                                          ALU.mult, ALU.add))
            link(dve.scalar_tensor_tensor(into[:, :, :], w.over[:, :, :], float(FAR), w.slot[:, :, :],
                                          ALU.mult, ALU.add))
            dve.nop().then_inc(slots_done, 1)
            link(dve.tensor_scalar(w.rank[:, :, :], w.rank[:, :, :], float(CAP0 - 1), None, ALU.min))
            link(dve.scalar_tensor_tensor(env.slot0[:, :, :], w.idf[:, :, :], float(CAP0), w.rank[:, :, :],
                                          ALU.mult, ALU.add))
            link(dve.tensor_scalar(w.over[:, :, :], w.over[:, :, :], -1.0, 1.0, ALU.mult, ALU.add))
            link(dve.tensor_tensor(env.wt0[:, :, :], w.top[:, :, 0:K0].rearrange("p t k -> p k t"), w.over[:, :, :],
                                   ALU.mult))
            for i in range(n_k):
                split.remain(dve, i)
                if i:
                    split.third(dve, i - 1)
            split.third(dve, n_k - 1)


WCH = 1024
PIECES = (KD * 2 * FF0 + FF0 // P * D) // WCH
STAGES = 3


class Weights:

    def __init__(self, sb, sem):
        FB = FF0 // P
        self.stage = sb("stage", [P, STAGES, WCH])
        self.w12 = [sb(f"w12{n}", [P, 2, KD, 2 * FF0], F32R) for n in "hl"]
        self.w3 = [sb(f"w3{n}", [P, 2, FB, D], F32R) for n in "hl"]
        self.staged = [sem(f"staged{i}") for i in range(STAGES)]
        self.high_done, self.low_done = sem("w_high_done"), sem("w_low_done")

    def part(self, low, s, c):
        n12 = KD * 2 * FF0 // WCH
        if c < n12:
            k, f = divmod(c * WCH, 2 * FF0)
            return self.w12[low][:, s, k, f:f + WCH]
        j = (c - n12) * WCH // D
        return self.w3[low][:, s, j:j + WCH // D, :].rearrange("p j d -> p (j d)")


def piece_at(e, c):
    return e * PIECES + c


def load_weights(sp, ins, ew, e, s, pieces=None):
    n12 = KD * 2 * FF0 // WCH
    for c in pieces or range(PIECES):
        if not isinstance(e, int) or piece_at(e, c) >= STAGES:
            sp.wait_ge(ew.low_done, piece_at(e, c) - STAGES + 1)
        if c < n12:
            k, f = divmod(c * WCH, 2 * FF0)
            src = ins["W12T"][e].rearrange("(k p) f -> k p f", p=P)[k, :, f:f + WCH]
            dst = ew.stage[:, c % STAGES, :]
        else:
            j = (c - n12) * WCH // D
            src = ins["W3T"][e].rearrange("(j p) d -> p j d", p=P)[:, j:j + WCH // D, :]
            dst = ew.stage[:, c % STAGES, :].rearrange("p (j d) -> p j d", d=D)
        sp.dma_start(dst, src).then_inc(ew.staged[c % STAGES], 16)


def load_weights_high(act, ew, e, s, pieces):
    for c in pieces:
        act.wait_ge(ew.staged[c % STAGES], 16 * (e * (PIECES // STAGES) + c // STAGES + 1))
        act.copy(ew.part(0, s, c), ew.stage[:, c % STAGES, :]).then_inc(ew.high_done, 1)


def load_weights_low(pool, ew, e, s):
    for c in range(PIECES):
        pool.wait_ge(ew.high_done, piece_at(e, c) + 1)
        pool.tensor_tensor(ew.part(1, s, c), ew.stage[:, c % STAGES, :], ew.part(0, s, c).bitcast(F32),
                           ALU.subtract).then_inc(ew.low_done, 1)


PASSES = ((0, 0), (0, 1), (1, 0))


def experts0(nc, env, ins):
    NTE = CAP0 // P
    FB = FF0 // P
    HALF = CAP0 // 2
    HFS = 4
    CH = 2 * FB
    ew = env.EW
    with ExitStack() as ctx:
        sb, ps, sem = scope(nc, ctx)
        rows = env.ON[:, :, :].rearrange("p g t -> p (g t)")
        XS = rows[:, 0:2 * NTE * D].rearrange("p (s n d) -> p s n d", s=2, n=NTE)
        YS = rows[:, 2 * NTE * D:3 * NTE * D].rearrange("p (n d) -> p n d", n=NTE)
        XST = [sb(f"XSTm0{n}", [P, KD, CAP0], F32R) for n in "hl"]
        HT = [sb(f"HTm0{n}", [P, FB, CAP0], F32R) for n in "hl"]
        SG, HF = sb("SGm0", [P, 2, HALF]), sb("HFm0", [P, HFS, HALF])
        G, U = ps("Gm0", [P, 2, SEQ]), ps("Um0", [P, 2, SEQ])
        TP, Y = ps("TPm0", [P, 2, SEQ]), ps("Ym0", [P, 2, SEQ])
        x_loaded = [sem(f"x_loaded{i}m0") for i in range(2)]
        tp_ready, xh_done, xst_done, gu_ready, sg_done, hf_done, hh_done, h_done, y_ready, y_done, y_stored = (
            sem(n + "m0") for n in ("tp_ready", "xh_done", "xst_done", "gu_ready", "sg_done", "hf_done", "hh_done",
                                    "h_done", "y_ready", "y_done", "y_stored"))
        block = ctx.enter_context(nc.Block())

        def pairs(eng, expert):
            for s in range(2):
                expert(0, s)
            with eng.Fori(1, E0 // 2 - 1) as r:
                for s in range(2):
                    expert(r, s)
            for s in range(2):
                expert(E0 // 2 - 1, s)

        def final(r, s):
            return isinstance(r, int) and 2 * r + s == E0 - 1

        @block.sync
        def _(sp):
            def load(r, s):
                sp.dma_start(XS[:, s, :, :], env.xs0[:, :].rearrange("(e n p) d -> e p n d", p=P, n=NTE)[2 * r + s]
                             ).then_inc(x_loaded[s], 16)

            for s in range(2):
                load(0, s)

            def expert(r, s):
                e = 2 * r + s
                if not final(r, s):
                    load_weights(sp, ins, ew, e + 1, 1 - s)
                if not (isinstance(r, int) and r == E0 // 2 - 1):
                    sp.wait_ge(tp_ready, NTE * (e + 1))
                    load(r + 1, s)
                sp.wait_ge(y_done, NTE * (e + 1))
                sp.dma_start(env.ys0[:, :].rearrange("(e n p) d -> e p n d", p=P, n=NTE)[e], YS[:, :, :]
                             ).then_inc(y_stored, 16)

            pairs(sp, expert)
            sp.wait_ge(y_stored, 16 * E0)

        @block.gpsimd
        def _(pool):
            def expert(r, s):
                if not final(r, s):
                    load_weights_low(pool, ew, 2 * r + s + 1, 1 - s)

            pairs(pool, expert)

        @block.tensor
        def _(pe):
            def turn(r, s, i):
                e = 2 * r + s
                if i == 0:
                    pe.wait_ge(x_loaded[s], 16 * (r + 1))
                wait(pe, xst_done, e * NTE + i - 1)
                for k in range(KD):
                    m = pe.transpose(TP[:, (s * NTE + i) % 2, k * P:(k + 1) * P],
                                     XS[:, s, i, k * P:(k + 1) * P], env.ident[:, :])
                m.then_inc(tp_ready, 1)

            for i in range(NTE):
                turn(0, 0, i)

            def expert(r, s):
                e = 2 * r + s
                pe.wait_ge(xst_done, NTE * (e + 1))
                pe.wait_ge(ew.low_done, PIECES * (e + 1))
                for c in range(CH):
                    half, j = divmod(c, FB)
                    wait(pe, hf_done, e * CH + c - 1)
                    for bank, f in ((G, j * P), (U, FF0 + j * P)):
                        for k in range(KD):
                            for a, b in PASSES:
                                m = pe.matmul(bank[:, c % 2, 0:HALF], ew.w12[a][:, s, k, f:f + P],
                                              XST[b][:, k, half * HALF:(half + 1) * HALF],
                                              start=(k == 0 and (a, b) == PASSES[0]),
                                              stop=(k == KD - 1 and (a, b) == PASSES[-1]))
                    m.then_inc(gu_ready, 1)
                for i in range(NTE):
                    if not final(r, s):
                        turn(r + s, 1 - s, i)
                    pe.wait_ge(h_done, CH * e + (FB if (i + 1) * P <= HALF else CH))
                    wait(pe, y_done, e * NTE + i - 1)
                    for j in range(FB):
                        for a, b in PASSES:
                            m = pe.matmul(Y[:, (s * NTE + i) % 2, 0:D], HT[a][:, j, i * P:(i + 1) * P],
                                          ew.w3[b][:, s, j, :], start=(j == 0 and (a, b) == PASSES[0]),
                                          stop=(j == FB - 1 and (a, b) == PASSES[-1]))
                    m.then_inc(y_ready, 1)

            pairs(pe, expert)

        @block.scalar
        def _(act):
            def turn(r, s):
                for i in range(NTE):
                    act.wait_ge(tp_ready, (2 * r + s) * NTE + i + 1)
                    act.copy(XST[0][:, :, i * P:(i + 1) * P],
                             TP[:, (s * NTE + i) % 2, 0:D].rearrange("p (k c) -> p k c", k=KD)).then_inc(xh_done, 1)

            turn(0, 0)

            def expert(r, s):
                e = 2 * r + s

                def high(c):
                    half, j = divmod(c, FB)
                    act.wait_ge(hf_done, e * CH + c + 1)
                    act.copy(HT[0][:, j, half * HALF:(half + 1) * HALF], HF[:, c % HFS, :]).then_inc(hh_done, 1)

                for c in range(CH):
                    act.wait_ge(gu_ready, e * CH + c + 1)
                    wait(act, hf_done, e * CH + c - 1)
                    act.activation(SG[:, c % 2, :], G[:, c % 2, 0:HALF], ACT.Silu).then_inc(sg_done, 1)
                    if c:
                        high(c - 1)
                    if c >= 2 and c % 2 == 0 and c // 2 <= PIECES and not final(r, s):
                        load_weights_high(act, ew, e + 1, 1 - s, [c // 2 - 1])
                high(CH - 1)
                if not final(r, s):
                    turn(r + s, 1 - s)

            pairs(act, expert)

        @block.vector
        def _(dve):
            def turn(r, s, i):
                dve.wait_ge(xh_done, (2 * r + s) * NTE + i + 1)
                at = slice(i * P, (i + 1) * P)
                dve.tensor_tensor(XST[1][:, :, at], TP[:, (s * NTE + i) % 2, 0:D].rearrange("p (k c) -> p k c", k=KD),
                                  XST[0][:, :, at].bitcast(F32), ALU.subtract).then_inc(xst_done, 1)

            for i in range(NTE):
                turn(0, 0, i)

            def expert(r, s):
                e = 2 * r + s

                def low(c):
                    half, j = divmod(c, FB)
                    at = slice(half * HALF, (half + 1) * HALF)
                    dve.wait_ge(hh_done, e * CH + c + 1)
                    dve.tensor_tensor(HT[1][:, j, at], HF[:, c % HFS, :], HT[0][:, j, at].bitcast(F32),
                                      ALU.subtract).then_inc(h_done, 1)

                for c in range(CH):
                    dve.wait_ge(sg_done, e * CH + c + 1)
                    wait(dve, h_done, e * CH + c - HFS + 1)
                    dve.tensor_tensor(HF[:, c % HFS, :], U[:, c % 2, 0:HALF], SG[:, c % 2, :],
                                      ALU.mult).then_inc(hf_done, 1)
                    if c:
                        low(c - 1)
                low(CH - 1)
                for i in range(NTE):
                    if not final(r, s):
                        turn(r + s, 1 - s, i)
                    dve.wait_ge(y_ready, e * NTE + i + 1)
                    if i == 0 and not (isinstance(r, int) and e == 0):
                        dve.wait_ge(y_stored, 16 * e)
                    dve.tensor_copy(YS[:, i, :], Y[:, (s * NTE + i) % 2, 0:D]).then_inc(y_done, 1)

            pairs(dve, expert)


GDEEP = 8


class Slots:

    def __init__(self, K, rows, slot, weight, earlier):
        self.K, self.rows, self.slot, self.weight, self.earlier = K, rows, slot, weight, earlier


def gather(pool, env, ex, YG, added, n):
    t, k = divmod(n, ex.K)
    if n >= GDEEP:
        pool.wait_ge(added, n - GDEEP + 1)
    pool.indirect_dma_start(
        out=YG[:, n % GDEEP, :], out_offset=None, in_=ex.rows[:, :],
        in_offset=bass.IndirectOffsetOnAxis(ap=ex.slot[:, k, t:t + 1], axis=0),
    ).then_inc(env.gathered[n % GDEEP], 16)


def add_gathered(dve, env, ex, YG, added, n):
    t, k = divmod(n, ex.K)
    dve.wait_ge(env.gathered[n % GDEEP], 16 * ((ex.earlier + n) // GDEEP + 1))
    if k:
        dve.wait_ge(added, n)
    dve.scalar_tensor_tensor(env.X[:, t, :], YG[:, n % GDEEP, :], ex.weight[:, k, t:t + 1], env.X[:, t, :],
                             ALU.mult, ALU.add).then_inc(added, 1)


def combine(nc, env, ex, out):
    with ExitStack() as ctx:
        sb, ps, sem = scope(nc, ctx)
        YG = sb("YGc", [P, GDEEP, D])
        added, sent = sem("addedc"), sem("sentc")
        block = ctx.enter_context(nc.Block())

        @block.gpsimd
        def _(pool):
            for n in range(NT * ex.K):
                gather(pool, env, ex, YG, added, n)

        @block.vector
        def _(dve):
            for n in range(NT * ex.K):
                add_gathered(dve, env, ex, YG, added, n)

        @block.sync
        def _(sp):
            for t in range(0, NT, 2):
                sp.wait_ge(added, ex.K * (t + 2))
                sp.dma_start(out.rearrange("(t p) d -> p t d", p=P)[:, t:t + 2, :], env.X[:, t:t + 2, :]
                             ).then_inc(sent, 16)
            sp.wait_ge(sent, 16 * (NT // 2))


def route1(nc, env, ins, lay):
    JS = FFS // P
    with ExitStack() as ctx:
        sb, ps, sem = scope(nc, ctx)
        early = carve(env.B1[:, :, :].rearrange("p e f -> p (e f)"))
        XF, XFT = early("XF1", [P, NT, D]), sb("XFT1", [P, KD, TOK])
        gate, s1, s2 = sb("gate", [P, KD, E1]), sb("s1", [P, KD, 2 * FFS]), sb("s2", [P, JS, D])
        s1b, smul = sb("s1b", [P, 2 * JS]), sb("smul", [P, JS])
        s2b, f2b = sb("s2b", [1, D]), sb("f2b", [E1, D])
        ln1 = Norm(sb, sem, "r1")
        w = routing_buffers(early, "1", E1, K1)
        comb, combT = sb("comb", [P, NT, E1]), sb("combT", [E1, TOK])
        fill, ntile, base, ends = sb("fill", [P, E1]), sb("ntile", [P, E1]), sb("base", [P, E1]), sb("ends", [P, E1])
        sq, many, upto = early("sq", [P, E1, E1]), early("many", [P, E1, NT]), sb("upto", [1, TILES1, E1])
        tile_e = sb("tile_e", [1, TILES1])
        GE, AT = sb("GE1", [P, 2, SEQ]), sb("AT1", [P, JS, SEQ])
        pw, pg = ps("pw1", [P, 2, SEQ]), ps("pg1", [P, 4, SEQ])
        lgp, rk = ps("lgp1", [P, NT, E1]), ps("rk1", [P, NT + 1, E1])
        wo_ready, x_done, chain, xf_done, r_loaded, chain_p = (sem(n + "1r") for n in (
            "wo_ready", "x_done", "chain", "xf_done", "r_loaded", "chain_p"))
        tp_ready, xft_done, lg_ready, lg_sub, ex_done, run_done, rk_ready, slots_done = (
            sem(n + "1r") for n in ("tp_ready", "xft_done", "lg_ready", "lg_sub", "ex_done", "run_done", "rk_ready",
                                    "slots_done"))
        gs_ready, ge_done, at_done, comb_done, ct_ready, ct_done, ys_ready, shared_done, folded = (
            sem(n + "1r") for n in ("gs_ready", "ge_done", "at_done", "comb_done", "ct_ready", "ct_done", "ys_ready",
                                    "shared_done", "folded"))
        block = ctx.enter_context(nc.Block())
        n_small = 8

        @block.sync
        def _(sp):
            with nc.allow_non_contiguous_dma(reason="small matrices and vectors"):
                sp.dma_start(gate[:, :, :], ins["gateT"].rearrange("(k p) e -> p k e", p=P)).then_inc(r_loaded, 16)
                sp.dma_start(s1b[:, :], ins["s_fc1_b"].rearrange("(j p) -> p j", p=P)).then_inc(r_loaded, 16)
                sp.dma_start(smul[:, :], ins["s_mult"].rearrange("(j p) -> p j", p=P)).then_inc(r_loaded, 16)
                sp.dma_start(env.mult[:, :, :], ins["mult"].rearrange("e (k p) -> p e k", p=P)).then_inc(r_loaded, 16)
            sp.dma_start(s2b[:, :], ins["s_fc2_b"].unsqueeze(0)).then_inc(r_loaded, 16)
            sp.dma_start(f2b[:, :], ins["fc2_b"]).then_inc(r_loaded, 16)
            sp.dma_start(s1[:, :, :], ins["s_fc1T"].rearrange("(k p) f -> p k f", p=P)).then_inc(r_loaded, 16)
            sp.dma_start(s2[:, :, :], ins["s_fc2T"].rearrange("(j p) d -> p j d", p=P)).then_inc(r_loaded, 16)
            for k in range(KD):
                sp.dma_start(env.W1[:, k, :, :], ins["fc1T"].rearrange("e (k p) f -> k p e f", p=P)[k]).then_inc(env.w1_loaded, 16)
            sp.wait_ge(wo_ready, NT)
            for k in range(FF1 // P):
                sp.dma_start(env.W2[:, k, :, :], ins["fc2T"].rearrange("e (k p) d -> k p e d", p=P)[k]).then_inc(env.w2_loaded, 16)
            sp.wait_ge(env.scattered, 16 * NT * (K0 + K1))
            sp.wait_ge(comb_done, 1)
            sp.dma_start(env.B1[:, :, :], ins["fc1_b"].partition_broadcast(P)).then_inc(env.b1_loaded, 16)

        @block.gpsimd
        def _(pool):
            pool.wait_ge(r_loaded, 16 * n_small)
            for j in range(JS):
                pool.tensor_scalar(s2[:, j, :], s2[:, j, :], smul[:, j:j + 1], None, ALU.mult).then_inc(folded, 1)
            pool.wait_ge(slots_done, 1)
            for t in range(NT):
                for k in range(K1):
                    pool.indirect_dma_start(
                        out=env.xs1[:, :], out_offset=bass.IndirectOffsetOnAxis(ap=env.slot1[:, k, t:t + 1], axis=0),
                        in_=XF[:, t, :], in_offset=None).then_inc(env.scattered, 16)
            pool.wait_ge(env.scattered, 16 * NT * (K0 + K1))

        @block.tensor
        def _(pe):
            out_projection(pe, env, lay, pw, wo_ready, x_done)

            def router(b):
                pe.wait_ge(xft_done, (b + 1) * KD)
                for t in range(b * TPB, (b + 1) * TPB):
                    for k in range(KD):
                        m = pe.matmul(lgp[:, t, :], XFT[:, k, t * P:(t + 1) * P], gate[:, k, :],
                                      start=(k == 0), stop=(k == KD - 1))
                return m

            pe.wait_ge(r_loaded, 16 * n_small)
            for b in range(BATCH):
                pe.wait_ge(ln1.done, (b + 1) * TPB)
                for n in range(b * KD, (b + 1) * KD):
                    if n >= 2:
                        pe.wait_ge(xft_done, n - 1)
                    for j in range(TPB):
                        m = pe.transpose(pg[:, n % 2, j * P:(j + 1) * P],
                                         XF[:, b * TPB + j, (n - b * KD) * P:(n - b * KD + 1) * P], env.ident[:, :])
                    m.then_inc(tp_ready, 1)
                if b:
                    router(b - 1)
            router(BATCH - 1).then_inc(lg_ready, 1)

            def shared_in(c):
                for j in range(JS):
                    i = c * JS + j
                    if i >= 2:
                        pe.wait_ge(at_done, i - 1)
                    for half in range(2):
                        for k in range(KD):
                            m = pe.matmul(pg[:, 2 * (i % 2) + half, :], s1[:, k, half * FFS + j * P:half * FFS + (j + 1) * P],
                                          XFT[:, k, c * SEQ:(c + 1) * SEQ], start=(k == 0), stop=(k == KD - 1))
                    m.then_inc(gs_ready, 1)

            def shared_out(c):
                pe.wait_ge(at_done, JS * (c + 1))
                pe.wait_ge(folded, JS)
                for q in range(TPB):
                    t = c * TPB + q
                    if t >= 2:
                        pe.wait_ge(shared_done, t - 1)
                    for j in range(JS):
                        pe.matmul(pw[:, t % 2, 0:D], AT[:, j, q * P:(q + 1) * P], s2[:, j, :],
                                  start=(j == 0), stop=False)
                    pe.matmul(pw[:, t % 2, 0:D], env.ones[0:1, :], s2b[:, :], start=False, stop=False)
                    pe.matmul(pw[:, t % 2, 0:D], combT[:, t * P:(t + 1) * P], f2b[:, :],
                              start=False, stop=True).then_inc(ys_ready, 1)

            shared_in(0)
            pe.wait_ge(run_done, 1)
            pe.matmul(rk[:, 0:NT, :], env.before[:, :], w.all[:, :, :], start=True, stop=False)
            pe.matmul(rk[:, 0:NT, :], env.ones[:, :], w.run[:, 0:NT, :], start=False, stop=True)
            pe.matmul(rk[:, NT, :], env.ones[:, :], w.run[:, NT, :], start=True, stop=True).then_inc(rk_ready, 1)
            for t4 in range(TPB):
                if t4 >= 2:
                    pe.wait_ge(ct_done, t4 - 1)
                if t4 == 0:
                    pe.wait_ge(comb_done, 1)
                for j in range(TPB):
                    m = pe.transpose(pw[0:E1, t4 % 2, j * P:(j + 1) * P], comb[:, t4 * TPB + j, :], env.ident[:, :])
                m.then_inc(ct_ready, 1)
            pe.wait_ge(ct_done, TPB)
            for c in range(BATCH):
                shared_out(c)
                if c + 1 < BATCH:
                    shared_in(c + 1)

        @block.scalar
        def _(act):
            for b in range(BATCH):
                norm_root(act, env, ln1, b)
            for n in range(TPB * KD):
                t4, k = divmod(n, KD)
                act.wait_ge(tp_ready, n + 1)
                act.copy(XFT[:, k, t4 * SEQ:(t4 + 1) * SEQ], pg[:, n % 2, :]).then_inc(xft_done, 1)
            act.wait_ge(lg_sub, 1)
            act.activation(w.ex[:, :, :], w.lg[:, :, :], ACT.Exp).then_inc(ex_done, 1)
            act.wait_ge(r_loaded, 16 * n_small)

            def gelu(c):
                for j in range(JS):
                    i = c * JS + j
                    act.wait_ge(gs_ready, i + 1)
                    if i >= 2:
                        act.wait_ge(at_done, i - 1)
                    act.activation(GE[:, i % 2, :], pg[:, 2 * (i % 2) + 1, :], ACT.Gelu,
                                   bias=s1b[:, JS + j:JS + j + 1]).then_inc(ge_done, 1)

            gelu(0)
            act.wait_ge(env.w2_loaded, 16 * FF1 // P)
            for k in range(FF1 // P):
                for e in range(E1):
                    act.activation(env.W2[:, k, e, :], env.W2[:, k, e, :], ACT.Copy, scale=env.mult[:, e, k:k + 1])
            for t4 in range(TPB):
                act.wait_ge(ct_ready, t4 + 1)
                act.copy(combT[:, t4 * SEQ:(t4 + 1) * SEQ], pw[0:E1, t4 % 2, :]).then_inc(ct_done, 1)
            for c in range(1, BATCH):
                gelu(c)

        @block.vector
        def _(dve):
            link = Link(dve, chain)
            for b in range(BATCH + 1):
                if b < BATCH:
                    for t in range(b * TPB, (b + 1) * TPB):
                        dve.wait_ge(wo_ready, t + 1)
                        dve.tensor_tensor(env.X[:, t, :], pw[:, t % 2, 0:D], env.X[:, t, :], ALU.add).then_inc(x_done, 1)
                    dve.wait_ge(x_done, (b + 1) * TPB)
                    norm_stats(dve, link, ln1, env.X, b)
                if b:
                    norm_apply(dve, link, ln1, env.X, XF, b - 1)
            dve.wait_ge(lg_ready, 1)
            pick(dve, link, env, w, E1, K1, lgp[:, :, :], False)
            dve.nop().then_inc(lg_sub, 1)
            dve.wait_ge(ex_done, 1)
            softmax_top(dve, link, env, w, E1, K1, 0.0)
            dve.nop().then_inc(run_done, 1)

            def shared(c):
                for j in range(JS):
                    i = c * JS + j
                    dve.wait_ge(ge_done, i + 1)
                    if c >= 1:
                        dve.wait_ge(ys_ready, TPB * c)
                    dve.scalar_tensor_tensor(AT[:, j, :], pg[:, 2 * (i % 2), :], s1b[:, j:j + 1],
                                             GE[:, i % 2, :], ALU.add, ALU.mult).then_inc(at_done, 1)

            shared(0)
            dve.wait_ge(rk_ready, 1)
            link(dve.tensor_copy(fill[:, :], rk[:, NT, :]))
            link(dve.tensor_scalar(w.red[:, :], env.iota[:, 0:NT], float(P), None, ALU.mult))
            link(dve.tensor_tensor(many[:, :, :], fill[:, :].unsqueeze(2).to_broadcast([P, E1, NT]),
                                   w.red[:, :].unsqueeze(1).to_broadcast([P, E1, NT]), ALU.is_gt))
            link(dve.tensor_reduce(ntile[:, :], many[:, :, :], AX.X, ALU.add))
            link(dve.tensor_tensor(sq[:, :, :], ntile[:, :].unsqueeze(1).to_broadcast([P, E1, E1]),
                                   env.earlier[:, :, :], ALU.mult))
            link(dve.tensor_reduce(base[:, :], sq[:, :, :], AX.X, ALU.add))
            link(dve.tensor_tensor(ends[:, :], base[:, :], ntile[:, :], ALU.add))
            link(dve.tensor_tensor(upto[:, :, :], env.iota[0:1, :].unsqueeze(2).to_broadcast([1, TILES1, E1]),
                                   ends[0:1, :].unsqueeze(1).to_broadcast([1, TILES1, E1]), ALU.is_ge))
            link(dve.tensor_reduce(tile_e[:, :], upto[:, :, :], AX.X, ALU.add))
            link(dve.tensor_scalar(env.expert[:, :], tile_e[:, :], float(E1 - 1), None, ALU.min))
            link(dve.scalar_tensor_tensor(
                w.lg[:, :, :], base[:, :].unsqueeze(1).to_broadcast([P, NT, E1]), float(P), rk[:, 0:NT, :],
                ALU.mult, ALU.add))
            for k in range(K1):
                link(dve.tensor_tensor(w.tmp[:, :, :], w.lg[:, :, :], w.hot[:, k, :, :], ALU.mult))
                link(dve.tensor_reduce(w.slot[:, k, :], w.tmp[:, :, :], AX.X, ALU.add))
            link(dve.tensor_copy(env.slot1[:, :, :], w.slot[:, :, :]))
            dve.nop().then_inc(slots_done, 1)
            link(dve.tensor_reduce(w.red[:, :], w.top[:, :, 0:K1], AX.X, ALU.add))
            link(dve.tensor_scalar(w.red[:, :], w.red[:, :], 1e-20, None, ALU.add))
            link(dve.reciprocal(w.red2[:, :], w.red[:, :]))
            for k in range(K1):
                link(dve.tensor_tensor(env.wt1[:, k, :], w.top[:, :, k], w.red2[:, :], ALU.mult))
                wide = env.wt1[:, k, :].unsqueeze(2).to_broadcast([P, NT, E1])
                if k == 0:
                    link(dve.tensor_tensor(comb[:, :, :], w.hot[:, k, :, :], wide, ALU.mult))
                else:
                    link(dve.tensor_tensor(w.tmp[:, :, :], w.hot[:, k, :, :], wide, ALU.mult))
                    link(dve.tensor_tensor(comb[:, :, :], comb[:, :, :], w.tmp[:, :, :], ALU.add))
            dve.nop().then_inc(comb_done, 1)
            for c in range(BATCH):
                if c:
                    shared(c)
                for q in range(TPB):
                    t = c * TPB + q
                    dve.wait_ge(ys_ready, t + 1)
                    dve.tensor_tensor(env.X[:, t, :], pw[:, t % 2, 0:D], env.X[:, t, :], ALU.add).then_inc(shared_done, 1)


def experts1(nc, env, ins):
    KF = FF1 // P
    with ExitStack() as ctx:
        sb, ps, sem = scope(nc, ctx)
        W1, W2, B1 = env.W1, env.W2, env.B1
        DEEP = 4
        XS, XST = sb("XS1", [P, DEEP, D]), sb("XST1", [P, 2, KD, P])
        HB, GE, A = sb("HB1", [P, 2, 2 * FF1]), sb("GE1e", [P, 2, FF1]), sb("A1", [P, 2, FF1])
        AT, YS = sb("AT1e", [P, 2, KF, P]), sb("YS1", [P, DEEP, D])
        TP, H = ps("TP1", [P, 2, SEQ]), ps("H1", [P, 2, SEQ])
        TA, Y = ps("TA1", [P, 2, SEQ]), ps("Y1", [P, 2, SEQ])
        xs_loaded = [sem(f"xs_loaded{i}e1") for i in range(DEEP)]
        y_stored = [sem(f"y_stored{i}e1") for i in range(DEEP)]
        (xt_ready, xst_done, h_ready, hb_done, ge_done, a_done, at_ready, at_done, y_ready,
         y_done) = (sem(n + "e1") for n in (
             "xt_ready", "xst_done", "h_ready", "hb_done", "ge_done", "a_done", "at_ready",
             "at_done", "y_ready", "y_done"))
        block = ctx.enter_context(nc.Block())
        HEAD = 4
        LOOPS = (TILES1 - HEAD) // DEEP

        def steps(eng, step):
            for c in range(HEAD):
                step(0, c)
            with eng.Fori(1, 1 + LOOPS) as r:
                for c in range(DEEP):
                    step(r, c)
            for j in range(HEAD + DEEP * LOOPS, TILES1):
                step(j // DEEP, j % DEEP)

        xs_tiles = env.xs1[:, :].rearrange("(j p) d -> j p d", p=P)
        ys_tiles = env.ys1[:, :].rearrange("(j p) d -> j p d", p=P)

        @block.sync
        def _(sp):
            def step(r, c):
                j = r * DEEP + c
                if not (isinstance(r, int) and j < DEEP):
                    sp.wait_ge(xt_ready, j - DEEP + 1)
                sp.dma_start(XS[:, c, :], xs_tiles[j]).then_inc(xs_loaded[c], 16)

            steps(sp, step)

        @block.gpsimd
        def _(pool):
            def step(r, c):
                j = r * DEEP + c
                pool.wait_ge(y_done, j + 1)
                pool.dma_start(ys_tiles[j], YS[:, c, :]).then_inc(y_stored[c], 16)

            steps(pool, step)
            for c in range(DEEP):
                pool.wait_ge(y_stored[c], 16 * ((TILES1 - c + DEEP - 1) // DEEP))

        @block.tensor
        def _(pe):
            def turn(r, c):
                j = r * DEEP + c
                pe.wait_ge(xs_loaded[c % DEEP], 16 * (r + c // DEEP + 1))
                wait(pe, xst_done, j - 1)
                for k in range(KD):
                    m = pe.transpose(TP[:, c % 2, k * P:(k + 1) * P], XS[:, c % DEEP, k * P:(k + 1) * P], env.ident[:, :])
                m.then_inc(xt_ready, 1)

            def first(r, c):
                j = r * DEEP + c
                e = pe.value_load(env.expert[0:1, bass.ds(j, 1)], min_val=0, max_val=E1 - 1)
                pe.wait_ge(xst_done, j + 1)
                wait(pe, hb_done, j - 1)
                for k in range(KD):
                    m = pe.matmul(H[:, c % 2, :], XST[:, c % 2, k, :], W1[:, k, bass.ds(e, 1), :],
                                  start=(k == 0), stop=(k == KD - 1))
                m.then_inc(h_ready, 1)

            def turn_back(r, c):
                j = r * DEEP + c
                pe.wait_ge(a_done, j + 1)
                wait(pe, at_done, j - 1)
                for k in range(KF):
                    m = pe.transpose(TA[:, c % 2, k * P:(k + 1) * P], A[:, c % 2, k * P:(k + 1) * P], env.ident[:, :])
                m.then_inc(at_ready, 1)

            def second(r, c):
                j = r * DEEP + c
                e = pe.value_load(env.expert[0:1, bass.ds(j, 1)], min_val=0, max_val=E1 - 1)
                pe.wait_ge(at_done, j + 1)
                wait(pe, y_done, j - 1)
                for k in range(KF):
                    m = pe.matmul(Y[:, c % 2, 0:D], AT[:, c % 2, k, :], W2[:, k, bass.ds(e, 1), :],
                                  start=(k == 0), stop=(k == KF - 1))
                m.then_inc(y_ready, 1)

            turn(0, 0)
            pe.wait_ge(env.w1_loaded, 16 * KD)

            def step(r, c):
                j = r * DEEP + c
                static = isinstance(r, int)
                if not (static and j + 1 >= TILES1):
                    turn(r, c + 1)
                first(r, c)
                if not (static and j < 1):
                    turn_back(r, c - 1)
                if not (static and j < 2):
                    second(r, c - 2)

            steps(pe, step)
            r, c = divmod(TILES1 - 1, DEEP)
            turn_back(r, c)
            second(r, c - 1)
            second(r, c)

        @block.scalar
        def _(act):
            def turn(r, c):
                j = r * DEEP + c
                act.wait_ge(xt_ready, j + 1)
                wait(act, h_ready, j - 1)
                act.copy(XST[:, c % 2, :, :], TP[:, c % 2, 0:D].rearrange("p (k t) -> p k t", k=KD)).then_inc(xst_done, 1)

            def turn_back(r, c):
                j = r * DEEP + c
                act.wait_ge(at_ready, j + 1)
                wait(act, y_ready, j - 1)
                act.copy(AT[:, c % 2, :, :], TA[:, c % 2, 0:FF1].rearrange("p (k t) -> p k t", k=KF)).then_inc(at_done, 1)

            turn(0, 0)

            def step(r, c):
                j = r * DEEP + c
                static = isinstance(r, int)
                if not (static and j + 1 >= TILES1):
                    turn(r, c + 1)
                act.wait_ge(hb_done, j + 1)
                wait(act, a_done, j - 1)
                act.activation(GE[:, c % 2, :], HB[:, c % 2, FF1:2 * FF1], ACT.Gelu).then_inc(ge_done, 1)
                if not (static and j < 1):
                    turn_back(r, c - 1)

            steps(act, step)
            turn_back(*divmod(TILES1 - 1, DEEP))

        @block.vector
        def _(dve):
            dve.wait_ge(env.b1_loaded, 16)

            def bias(r, c):
                j = r * DEEP + c
                e = dve.value_load(env.expert[0:1, bass.ds(j, 1)], min_val=0, max_val=E1 - 1)
                dve.wait_ge(h_ready, j + 1)
                wait(dve, a_done, j - 1)
                dve.tensor_tensor(HB[:, c % 2, :], H[:, c % 2, :], B1[:, bass.ds(e, 1), :].squeeze(1), ALU.add).then_inc(hb_done, 1)

            def gated(r, c):
                j = r * DEEP + c
                dve.wait_ge(ge_done, j + 1)
                wait(dve, at_ready, j - 1)
                dve.tensor_tensor(A[:, c % 2, :], HB[:, c % 2, 0:FF1], GE[:, c % 2, :], ALU.mult).then_inc(a_done, 1)

            def keep(r, c):
                j = r * DEEP + c
                dve.wait_ge(y_ready, j + 1)
                if not (isinstance(r, int) and j < DEEP):
                    dve.wait_ge(y_stored[c % DEEP], 16 * (r + c // DEEP))
                dve.tensor_copy(YS[:, c % DEEP, :], Y[:, c % 2, 0:D]).then_inc(y_done, 1)

            def step(r, c):
                j = r * DEEP + c
                bias(r, c)
                gated(r, c)
                if not (isinstance(r, int) and j < 2):
                    keep(r, c - 2)

            steps(dve, step)
            for j in range(TILES1 - 2, TILES1):
                keep(*divmod(j, DEEP))


def recycle(nc):
    used = sorted(s if isinstance(s, int) else s.num for s in nc.released_uncleared_semaphores)
    with nc.Block() as block:
        @block.gpsimd
        def _(pool):
            first = 0
            for i in range(1, len(used) + 1):
                if i == len(used) or used[i] != used[i - 1] + 1:
                    pool.sem_clear(range(used[first], used[i - 1] + 1))
                    first = i


class Layer:
    def __init__(self, name, heads, hd, scale):
        self.name, self.heads, self.hd, self.scale = name, heads, hd, scale
        self.gpb = heads // GH
        self.groups = BATCH * self.gpb
        self.halves = heads * HP // P


def program(nc, ins, out):
    lay0 = Layer("0", 8, 4, (D / 8) ** -0.5)
    lay1 = Layer("1", 16, 16, 16 ** -0.5)
    env = Work()
    with ExitStack() as ctx:
        sb, ps, sem = scope(nc, ctx)
        env.X = sb("X", [P, NT, D])
        env.ident, env.ones, env.before = (sb(n, [P, P]) for n in ("ident", "ones", "before"))
        env.sums = sb("sums", [P, GH])
        env.earlier, env.iota = sb("earlier", [P, E1, E1]), sb("iota", [P, TILES1])
        env.slot0, env.wt0 = sb("slot0", [P, K0, NT], U32), sb("wt0", [P, K0, NT])
        env.slot1, env.wt1 = sb("slot1", [P, K1, NT], U32), sb("wt1", [P, K1, NT])
        env.eps = sb("eps", [P, 1])
        env.WO = sb("WO", [P, max(lay0.gpb, lay1.gpb), D])
        env.x_loaded = sem("x_loaded")
        env.filled, env.scattered = sem("filled"), sem("scattered")
        env.gathered = [sem(f"gathered{i}") for i in range(GDEEP)]
        env.expert = sb("expert", [1, TILES1], I32)
        env.mult = sb("mult", [P, E1, FF1 // P])

        def dram(name, shape, dt=F32):
            return nc.dram_tensor(name, shape, dt, kind="Internal").ap()

        env.xs0, env.ys0 = dram("xs0", [E0 * CAP0, D]), dram("ys0", [E0 * CAP0, D])
        env.xs1, env.ys1 = dram("xs1", [TILES1 * P, D]), dram("ys1", [TILES1 * P, D])
        for lay in (lay0, lay1):
            lay.scr = {w: dram(f"scr{w}{lay.name}", [3, lay.groups, GH * HP, SEQ], BF16) for w in "qk"}
        ex0 = Slots(K0, env.ys0, env.slot0, env.wt0, 0)
        ex1 = Slots(K1, env.ys1, env.slot1, env.wt1, NT * K0)

        def attention(sb, sem, lay, experts=None):
            env.ON = sb(f"ON{lay.name}", [P, lay.groups, SEQ])
            env.wo_zero, env.wo_loaded = sem(f"wo_zero{lay.name}"), sem(f"wo_loaded{lay.name}")
            with ExitStack() as values:
                vsb, _, vsem = scope(nc, values)
                env.stacks = Stacks(vsb, vsem, lay, BATCH * lay.halves * (1 if experts else 2))
                env.VA = vsb(f"VA{lay.name}", [P, lay.groups, TPB, GH * VW])
                if lay is lay0:
                    env.zeros = vsb("zeros", [P, ZROWS * D // P])
                    setup(nc, env)
                project(nc, env, ins, lay, experts)
                attend(nc, env, ins, lay)

        with ExitStack() as first:
            sb, _, sem = scope(nc, first)
            attention(sb, sem, lay0)
            env.EW = Weights(sb, sem)
            route0(nc, env, ins, lay0, lay1)
            experts0(nc, env, ins)
        recycle(nc)
        with ExitStack() as second:
            sb, _, sem = scope(nc, second)
            attention(sb, sem, lay1, ex0)
            env.W1 = sb("W1", [P, KD, E1, 2 * FF1])
            env.B1 = sb("B1", [P, E1, 2 * FF1])
            env.w1_loaded, env.w2_loaded, env.b1_loaded = sem("w1_loaded"), sem("w2_loaded"), sem("b1_loaded")
            env.W2 = env.ON[:, :, :].rearrange("p g t -> p (g t)")[:, 0:FF1 // P * E1 * D].rearrange(
                "p (k e d) -> p k e d", k=FF1 // P, e=E1)
            route1(nc, env, ins, lay1)
            experts1(nc, env, ins)
            combine(nc, env, ex1, out)


def kernel(**a):
    import numpy as np
    import concourse.bacc as bacc
    from concourse.bass_utils import run_bass_kernel_spmd

    a = {k: np.asarray(v) for k, v in a.items()}
    kv_w = a["L1_xattn_Wkv"].reshape(D, D, 2)
    kv_b = a["L1_xattn_bkv"].reshape(D, 2)
    arrays = {
        "x": a["x"].reshape(TOK, D), "ctxT": a["ctx_1024"].reshape(TOK, D).T,
        "Wq0": a["L0_xattn_Wq"], "bq0": a["L0_xattn_bq"], "Wk0": a["L0_xattn_Wk"], "bk0": a["L0_xattn_bk"],
        "Wv0": a["L0_xattn_Wv"], "bv0": a["L0_xattn_bv"], "Wo0": a["L0_xattn_Wo"], "bo0": a["L0_xattn_bo"],
        "gamma": a["L0_ffn_ln_gamma"], "beta": a["L0_ffn_ln_beta"], "WrT": a["L0_ffn_Wr"].T,
        "W12T": a["L0_ffn_W12"].transpose(0, 2, 1), "W3T": a["L0_ffn_W3"].transpose(0, 2, 1),
        "Wq1": a["L1_xattn_Wq"], "bq1": a["L1_xattn_bq"], "Wk1": kv_w[:, :, 0], "bk1": kv_b[:, 0],
        "Wv1": kv_w[:, :, 1], "bv1": kv_b[:, 1], "Wo1": a["L1_xattn_Wout"], "bo1": a["L1_xattn_bout"],
        "gateT": a["L1_ffn_gate_w"].T, "fc1T": a["L1_ffn_fc1_w"].transpose(0, 2, 1), "fc1_b": a["L1_ffn_fc1_b"],
        "mult": a["L1_ffn_geglu_mult"], "fc2T": a["L1_ffn_fc2_w"].transpose(0, 2, 1), "fc2_b": a["L1_ffn_fc2_b"],
        "s_fc1T": a["L1_ffn_s_fc1_w"].T, "s_fc1_b": a["L1_ffn_s_fc1_b"], "s_mult": a["L1_ffn_s_geglu_mult"],
        "s_fc2T": a["L1_ffn_s_fc2_w"].T, "s_fc2_b": a["L1_ffn_s_fc2_b"],
    }
    nc = bacc.Bacc("TRN2", target_bir_lowering=False, num_devices=1)
    ins, feeds = {}, {}
    for name, v in arrays.items():
        v = np.ascontiguousarray(v)
        feeds[f"in_{name}"] = v
        ins[name] = nc.dram_tensor(f"in_{name}", v.shape, mybir.dt.from_np(v.dtype), kind="ExternalInput").ap()
    out = nc.dram_tensor("out", (TOK, D), F32, kind="ExternalOutput").ap()
    program(nc, ins, out)
    r = run_bass_kernel_spmd(nc, [feeds], core_ids=[0])
    return np.asarray(r.results[0]["out"]).reshape(BATCH, SEQ, D)
```
